# Optimizing a Trainium2 kernel written in Bass

```python
import numpy as np
import jax
import jax.numpy as jnp

def _softmax(x, axis=-1):
    return jax.nn.softmax(x, axis=axis)

def _gelu(x):
    return jax.nn.gelu(x, approximate=True)

def _silu(x):
    return jax.nn.silu(x)

def _sigmoid(x):
    return jax.nn.sigmoid(x)

def _layernorm(x, axis=-1, eps=1e-05):
    m = jnp.mean(x, axis=axis, keepdims=True)
    v = jnp.var(x, axis=axis, keepdims=True)
    return (x - m) / jnp.sqrt(v + eps)

def _scatter_add(tgt, idx, src, axis=0):
    return tgt.at[idx].add(src)

def _segment_sum(src, seg, n):
    return jax.ops.segment_sum(src, seg, n)
kernel_name = 'mk_lm_tower_d2_tok_ids512_r4_dcb447'

def setup_inputs(seed: int=0):
    np.random.seed(seed)
    _w = jnp.asarray

    def _rec_inputs():
        import jax
        import jax.numpy as jnp
        _rk = jax.random.key(seed)
        x = jax.random.randint(jax.random.fold_in(_rk, 1), (8, 512), 0, 24991, jnp.int32)
        return x
    x = _rec_inputs()

    def _L0_tok_setup():
        import jax, jax.numpy as jnp
        import numpy as np
        VOCAB = 25000
        HIDDEN = 128
        NUM_CLUSTERS = 64
        B, S = (8, 512)
        key = jax.random.key(seed)
        k1, k2, k3, k4, k5 = jax.random.split(key, 5)
        return {'location_ids': jax.random.randint(k1, (B, S), 0, VOCAB), 'fine_embed_w': jax.random.normal(k2, (VOCAB, HIDDEN // 2), dtype=jnp.float32), 'coarse_embed_w': jax.random.normal(k3, (NUM_CLUSTERS, HIDDEN // 2), dtype=jnp.float32), 'loc_to_cluster_w': jax.random.normal(k4, (NUM_CLUSTERS, VOCAB), dtype=jnp.float32), 'loc_to_cluster_b': jax.random.normal(k5, (NUM_CLUSTERS,), dtype=jnp.float32)}
    _L0_tok_all = _L0_tok_setup()
    _L0_tok_in = {k: v for k, v in _L0_tok_all.items() if k in ('fine_embed_w', 'coarse_embed_w', 'loc_to_cluster_w', 'loc_to_cluster_b')}
    del _L0_tok_all

    def _L0_attn_setup():
        import jax, jax.numpy as jnp
        import numpy as np
        D_MODEL = 128
        D_STATE = 16
        BATCH = 4
        SEQLEN = 1024
        key = jax.random.key(seed)
        k_u, k_ar, k_ai, k_b, k_c, k_d = jax.random.split(key, 6)
        u = jax.random.normal(k_u, (BATCH, SEQLEN, D_MODEL), dtype=jnp.float32)
        A_real = -0.5 * jax.random.uniform(k_ar, (D_MODEL, D_STATE), dtype=jnp.float32)
        A_imag = jax.random.normal(k_ai, (D_MODEL, D_STATE), dtype=jnp.float32)
        B = 0.1 * jax.random.normal(k_b, (D_MODEL, D_STATE), dtype=jnp.float32)
        C = 0.1 * jax.random.normal(k_c, (D_MODEL, D_STATE), dtype=jnp.float32)
        delta = 0.01 * jax.random.uniform(k_d, (D_MODEL,), dtype=jnp.float32) + 0.001
        return {'u': u, 'A_real': A_real, 'A_imag': A_imag, 'B': B, 'C': C, 'delta': delta}
    _L0_attn_all = _L0_attn_setup()
    _L0_attn_in = {k: v for k, v in _L0_attn_all.items() if k in ('A_real', 'A_imag', 'B', 'C', 'delta')}
    del _L0_attn_all

    def _L0_ffn_setup():
        import jax, jax.numpy as jnp
        import numpy as np
        S, B, I, O, H, E, K = (128, 32, 128, 128, 128, 8, 2)

        def _expert(x_seq, Wi, Wh, b, Wo, bo):
            Bsz = x_seq.shape[1]
            Hd = Wh.shape[0]

            def step(carry, xt):
                h, c = carry
                gates = xt @ Wi + h @ Wh + b
                i_, f_, g_, o_ = jnp.split(gates, 4, axis=-1)
                c = jax.nn.sigmoid(f_) * c + jax.nn.sigmoid(i_) * jnp.tanh(g_)
                h = jax.nn.sigmoid(o_) * jnp.tanh(c)
                return ((h, c), h @ Wo + bo)
            init = (jnp.zeros((Bsz, Hd), x_seq.dtype), jnp.zeros((Bsz, Hd), x_seq.dtype))
            _, ys = jax.lax.scan(step, init, x_seq)
            return ys
        key = jax.random.key(seed)
        ks = jax.random.split(key, 6)
        s = 0.02
        return {'x': jax.random.normal(ks[0], (S, B, I), dtype=jnp.float32), 'router_w': jax.random.normal(ks[1], (I, E), dtype=jnp.float32) * s, 'router_b': jnp.zeros((E,), dtype=jnp.float32), 'Wi': jax.random.normal(ks[2], (E, I, 4 * H), dtype=jnp.float32) * s, 'Wh': jax.random.normal(ks[3], (E, H, 4 * H), dtype=jnp.float32) * s, 'b': jnp.zeros((E, 4 * H), dtype=jnp.float32), 'Wo': jax.random.normal(ks[4], (E, H, O), dtype=jnp.float32) * s, 'bo': jnp.zeros((E, O), dtype=jnp.float32)}
    _L0_ffn_all = _L0_ffn_setup()
    _L0_ffn_in = {k: v for k, v in _L0_ffn_all.items() if k in ('router_w', 'router_b', 'Wi', 'Wh', 'b', 'Wo', 'bo')}
    del _L0_ffn_all

    def _L1_attn_setup():
        import jax, jax.numpy as jnp
        import numpy as np
        HIGHEST = jax.lax.Precision.HIGHEST
        KEY_CHUNK_SIZE = 1024 * 4
        HEADS = 8
        DIM_HEAD = 64

        def _query_chunk_size(num_q: int) -> int:
            if num_q % 64 == 0:
                return num_q // 64
            if num_q % 16 == 0:
                return num_q // 16
            if num_q % 4 == 0:
                return num_q // 4
            return num_q

        def _me_attention(q, k, v, q_chunk: int, k_chunk: int):
            S, H, D = q.shape
            num_kv = k.shape[0]
            k_chunk = min(k_chunk, num_kv)
            q = q / jnp.sqrt(jnp.asarray(D, q.dtype))
            kc = k.reshape(-1, k_chunk, H, D)
            vc = v.reshape(-1, k_chunk, H, v.shape[-1])

            def per_qchunk(qch):

                def summarize(args):
                    kch, vch = args
                    s = jnp.einsum('qhd,khd->qhk', qch, kch, precision=HIGHEST)
                    m = jax.lax.stop_gradient(jnp.max(s, axis=-1, keepdims=True))
                    e = jnp.exp(s - m)
                    ev = jnp.einsum('khf,qhk->qhf', vch, e, precision=HIGHEST)
                    return (ev, e.sum(axis=-1), m[..., 0])
                evs, ews, ms = jax.lax.map(summarize, (kc, vc))
                gm = jnp.max(ms, axis=0)
                sc = jnp.exp(ms - gm)
                num = (evs * sc[..., None]).sum(axis=0)
                den = (ews * sc).sum(axis=0)
                return num / den[..., None]
            qs = q.reshape(-1, q_chunk, H, D)
            out = jax.lax.map(per_qchunk, qs)
            return out.reshape(S, H, -1)

        def _forward(hidden_states, w_q, w_k, w_v, w_out, b_out):
            B, S, Dm = hidden_states.shape
            H, dh = (HEADS, DIM_HEAD)
            q = hidden_states @ w_q
            k = hidden_states @ w_k
            v = hidden_states @ w_v

            def to_heads(t):
                return t.reshape(B, S, H, dh).transpose(0, 2, 1, 3).reshape(B * H, S, dh)
            qs, ks, vs = (to_heads(q), to_heads(k), to_heads(v))
            qcs = _query_chunk_size(S)
            attn = _me_attention(qs.transpose(1, 0, 2), ks.transpose(1, 0, 2), vs.transpose(1, 0, 2), qcs, KEY_CHUNK_SIZE)
            attn = attn.transpose(1, 0, 2)
            attn = attn.reshape(B, H, S, dh).transpose(0, 2, 1, 3).reshape(B, S, H * dh)
            return attn @ w_out + b_out
        key = jax.random.key(seed)
        ks = jax.random.split(key, 6)
        B, S, Dm = (2, 2048, 128)
        inner = HEADS * DIM_HEAD
        return {'hidden_states': jax.random.normal(ks[0], (B, S, Dm), dtype=jnp.float32), 'w_q': jax.random.normal(ks[1], (Dm, inner), dtype=jnp.float32) * 0.02, 'w_k': jax.random.normal(ks[2], (Dm, inner), dtype=jnp.float32) * 0.02, 'w_v': jax.random.normal(ks[3], (Dm, inner), dtype=jnp.float32) * 0.02, 'w_out': jax.random.normal(ks[4], (inner, Dm), dtype=jnp.float32) * 0.02, 'b_out': jnp.zeros((Dm,), dtype=jnp.float32)}
    _L1_attn_all = _L1_attn_setup()
    _L1_attn_in = {k: v for k, v in _L1_attn_all.items() if k in ('w_q', 'w_k', 'w_v', 'w_out', 'b_out')}
    del _L1_attn_all

    def _L1_ffn_setup():
        import jax, jax.numpy as jnp
        import numpy as np
        E = 8
        TOP_K = 2
        D = 128
        H = 256
        B, S = (16, 1024)
        key = jax.random.key(seed)
        ks = jax.random.split(key, 10)
        sd = lambda fan_in: 1.0 / np.sqrt(fan_in)
        x = jax.random.normal(ks[0], (B, S, D), dtype=jnp.float32)
        gw1 = jax.random.uniform(ks[1], (D, D // 2), jnp.float32, -sd(D), sd(D))
        gb1 = jnp.zeros((D // 2,), jnp.float32)
        gw2 = jax.random.uniform(ks[2], (D // 2, E), jnp.float32, -sd(D // 2), sd(D // 2))
        gb2 = jnp.zeros((E,), jnp.float32)
        we1 = jax.random.uniform(ks[3], (E, D, H), jnp.float32, -sd(D), sd(D))
        be1 = jnp.zeros((E, H), jnp.float32)
        we2 = jax.random.uniform(ks[4], (E, H, D), jnp.float32, -sd(H), sd(H))
        be2 = jnp.zeros((E, D), jnp.float32)
        return {'x': x, 'gw1': gw1, 'gb1': gb1, 'gw2': gw2, 'gb2': gb2, 'we1': we1, 'be1': be1, 'we2': we2, 'be2': be2}
    _L1_ffn_all = _L1_ffn_setup()
    _L1_ffn_in = {k: v for k, v in _L1_ffn_all.items() if k in ('gw1', 'gb1', 'gw2', 'gb2', 'we1', 'be1', 'we2', 'be2')}
    del _L1_ffn_all
    return {'x': x, 'L0_tok_fine_embed_w': _L0_tok_in['fine_embed_w'], 'L0_tok_coarse_embed_w': _L0_tok_in['coarse_embed_w'], 'L0_tok_loc_to_cluster_w': _L0_tok_in['loc_to_cluster_w'], 'L0_tok_loc_to_cluster_b': _L0_tok_in['loc_to_cluster_b'], 'L0_attn_A_real': _L0_attn_in['A_real'], 'L0_attn_A_imag': _L0_attn_in['A_imag'], 'L0_attn_B': _L0_attn_in['B'], 'L0_attn_C': _L0_attn_in['C'], 'L0_attn_delta': _L0_attn_in['delta'], 'L0_ffn_router_w': _L0_ffn_in['router_w'], 'L0_ffn_router_b': _L0_ffn_in['router_b'], 'L0_ffn_Wi': _L0_ffn_in['Wi'], 'L0_ffn_Wh': _L0_ffn_in['Wh'], 'L0_ffn_b': _L0_ffn_in['b'], 'L0_ffn_Wo': _L0_ffn_in['Wo'], 'L0_ffn_bo': _L0_ffn_in['bo'], 'L1_attn_w_q': _L1_attn_in['w_q'], 'L1_attn_w_k': _L1_attn_in['w_k'], 'L1_attn_w_v': _L1_attn_in['w_v'], 'L1_attn_w_out': _L1_attn_in['w_out'], 'L1_attn_b_out': _L1_attn_in['b_out'], 'L1_ffn_gw1': _L1_ffn_in['gw1'], 'L1_ffn_gb1': _L1_ffn_in['gb1'], 'L1_ffn_gw2': _L1_ffn_in['gw2'], 'L1_ffn_gb2': _L1_ffn_in['gb2'], 'L1_ffn_we1': _L1_ffn_in['we1'], 'L1_ffn_be1': _L1_ffn_in['be1'], 'L1_ffn_we2': _L1_ffn_in['we2'], 'L1_ffn_be2': _L1_ffn_in['be2']}

def reference(x, L0_tok_fine_embed_w, L0_tok_coarse_embed_w, L0_tok_loc_to_cluster_w, L0_tok_loc_to_cluster_b, L0_attn_A_real, L0_attn_A_imag, L0_attn_B, L0_attn_C, L0_attn_delta, L0_ffn_router_w, L0_ffn_router_b, L0_ffn_Wi, L0_ffn_Wh, L0_ffn_b, L0_ffn_Wo, L0_ffn_bo, L1_attn_w_q, L1_attn_w_k, L1_attn_w_v, L1_attn_w_out, L1_attn_b_out, L1_ffn_gw1, L1_ffn_gb1, L1_ffn_gw2, L1_ffn_gb2, L1_ffn_we1, L1_ffn_be1, L1_ffn_we2, L1_ffn_be2):
    import jax
    import jax.numpy as jnp

    def _L0_tok_ref(location_ids, fine_embed_w, coarse_embed_w, loc_to_cluster_w, loc_to_cluster_b):
        import jax, jax.numpy as jnp
        import numpy as np
        VOCAB = 25000
        HIDDEN = 128
        NUM_CLUSTERS = 64
        B, S = (8, 512)
        fine_emb = fine_embed_w[location_ids]
        cluster_logits = loc_to_cluster_w.T[location_ids] + loc_to_cluster_b
        cluster_dist = jax.nn.softmax(cluster_logits, axis=-1)
        coarse_emb = jnp.einsum('bsc,ch->bsh', cluster_dist, coarse_embed_w)
        return jnp.concatenate([fine_emb, coarse_emb], axis=-1)

    def _L0_attn_ref(u, A_real, A_imag, B, C, delta):
        import jax, jax.numpy as jnp
        import numpy as np
        D_MODEL = 128
        D_STATE = 16
        BATCH = 4
        SEQLEN = 1024
        A = A_real + 1j * A_imag
        dtA = delta[:, None] * A
        A_bar = jnp.exp(dtA)
        B_bar = (A_bar - 1.0) / A * B
        L = u.shape[1]
        l = jnp.arange(L, dtype=jnp.float32)
        vand = jnp.exp(dtA[:, :, None] * l)
        K = jnp.einsum('dn,dnl->dl', C * B_bar, vand)
        n = 2 * L
        Uf = jnp.fft.fft(u, n=n, axis=1)
        Kf = jnp.fft.fft(K, n=n, axis=-1)
        y = jnp.fft.ifft(Uf * Kf.T[None], axis=1)[:, :L].real
        return y.astype(u.dtype)

    def _L0_ffn_ref(x, router_w, router_b, Wi, Wh, b, Wo, bo):
        import jax, jax.numpy as jnp
        import numpy as np
        S, B, I, O, H, E, K = (128, 32, 128, 128, 128, 8, 2)

        def _expert(x_seq, Wi, Wh, b, Wo, bo):
            Bsz = x_seq.shape[1]
            Hd = Wh.shape[0]

            def step(carry, xt):
                h, c = carry
                gates = xt @ Wi + h @ Wh + b
                i_, f_, g_, o_ = jnp.split(gates, 4, axis=-1)
                c = jax.nn.sigmoid(f_) * c + jax.nn.sigmoid(i_) * jnp.tanh(g_)
                h = jax.nn.sigmoid(o_) * jnp.tanh(c)
                return ((h, c), h @ Wo + bo)
            init = (jnp.zeros((Bsz, Hd), x_seq.dtype), jnp.zeros((Bsz, Hd), x_seq.dtype))
            _, ys = jax.lax.scan(step, init, x_seq)
            return ys
        S_, B_, I_ = x.shape
        N = S_ * B_
        flat_x = x.reshape(N, I_)
        logits = flat_x @ router_w + router_b
        top_vals, top_idx = jax.lax.top_k(logits, K)
        rw = jax.nn.softmax(top_vals, axis=1)
        mask = (top_idx.T[:, None, :] == jnp.arange(E)[None, :, None]).astype(x.dtype)
        expert_x = (mask[..., None] * flat_x[None, None]).reshape(K, E, S_, B_, I_)
        run_e = jax.vmap(_expert, in_axes=(0, 0, 0, 0, 0, 0))
        run_ke = jax.vmap(run_e, in_axes=(0, None, None, None, None, None))
        out = run_ke(expert_x, Wi, Wh, b, Wo, bo)
        out = out.reshape(K, E, N, -1)
        y = jnp.einsum('ken,nk,keno->no', mask, rw, out)
        return y.reshape(S_, B_, -1)

    def _L1_attn_ref(hidden_states, w_q, w_k, w_v, w_out, b_out):
        import jax, jax.numpy as jnp
        import numpy as np
        HIGHEST = jax.lax.Precision.HIGHEST
        KEY_CHUNK_SIZE = 1024 * 4
        HEADS = 8
        DIM_HEAD = 64

        def _query_chunk_size(num_q: int) -> int:
            if num_q % 64 == 0:
                return num_q // 64
            if num_q % 16 == 0:
                return num_q // 16
            if num_q % 4 == 0:
                return num_q // 4
            return num_q

        def _me_attention(q, k, v, q_chunk: int, k_chunk: int):
            S, H, D = q.shape
            num_kv = k.shape[0]
            k_chunk = min(k_chunk, num_kv)
            q = q / jnp.sqrt(jnp.asarray(D, q.dtype))
            kc = k.reshape(-1, k_chunk, H, D)
            vc = v.reshape(-1, k_chunk, H, v.shape[-1])

            def per_qchunk(qch):

                def summarize(args):
                    kch, vch = args
                    s = jnp.einsum('qhd,khd->qhk', qch, kch, precision=HIGHEST)
                    m = jax.lax.stop_gradient(jnp.max(s, axis=-1, keepdims=True))
                    e = jnp.exp(s - m)
                    ev = jnp.einsum('khf,qhk->qhf', vch, e, precision=HIGHEST)
                    return (ev, e.sum(axis=-1), m[..., 0])
                evs, ews, ms = jax.lax.map(summarize, (kc, vc))
                gm = jnp.max(ms, axis=0)
                sc = jnp.exp(ms - gm)
                num = (evs * sc[..., None]).sum(axis=0)
                den = (ews * sc).sum(axis=0)
                return num / den[..., None]
            qs = q.reshape(-1, q_chunk, H, D)
            out = jax.lax.map(per_qchunk, qs)
            return out.reshape(S, H, -1)

        def _forward(hidden_states, w_q, w_k, w_v, w_out, b_out):
            B, S, Dm = hidden_states.shape
            H, dh = (HEADS, DIM_HEAD)
            q = hidden_states @ w_q
            k = hidden_states @ w_k
            v = hidden_states @ w_v

            def to_heads(t):
                return t.reshape(B, S, H, dh).transpose(0, 2, 1, 3).reshape(B * H, S, dh)
            qs, ks, vs = (to_heads(q), to_heads(k), to_heads(v))
            qcs = _query_chunk_size(S)
            attn = _me_attention(qs.transpose(1, 0, 2), ks.transpose(1, 0, 2), vs.transpose(1, 0, 2), qcs, KEY_CHUNK_SIZE)
            attn = attn.transpose(1, 0, 2)
            attn = attn.reshape(B, H, S, dh).transpose(0, 2, 1, 3).reshape(B, S, H * dh)
            return attn @ w_out + b_out
        return _forward(hidden_states, w_q, w_k, w_v, w_out, b_out)

    def _L1_ffn_ref(x, gw1, gb1, gw2, gb2, we1, be1, we2, be2):
        import jax, jax.numpy as jnp
        import numpy as np
        E = 8
        TOP_K = 2
        D = 128
        H = 256
        B, S = (16, 1024)
        b, s, d = x.shape
        xf = x.reshape(-1, d)
        T = xf.shape[0]
        gate_logits = jax.nn.relu(xf @ gw1 + gb1) @ gw2 + gb2
        gate_weights = jax.nn.softmax(gate_logits, axis=-1)
        top_w, top_idx = jax.lax.top_k(gate_weights, TOP_K)
        top_w = jax.nn.softmax(top_w, axis=-1)
        combine = jnp.zeros((T, E), dtype=xf.dtype)
        combine = combine.at[jnp.arange(T)[:, None], top_idx].add(top_w)
        out = jnp.zeros_like(xf)
        for e in range(E):
            h = jax.nn.gelu(xf @ we1[e] + be1[e], approximate=False)
            y = h @ we2[e] + be2[e]
            out = out + combine[:, e:e + 1] * y
        return out.reshape(b, s, d)
    h = _L0_tok_ref(x, L0_tok_fine_embed_w, L0_tok_coarse_embed_w, L0_tok_loc_to_cluster_w, L0_tok_loc_to_cluster_b)
    h = h + _L0_attn_ref(_layernorm(h, axis=-1), L0_attn_A_real, L0_attn_A_imag, L0_attn_B, L0_attn_C, L0_attn_delta)
    h = h + _L0_ffn_ref(_layernorm(h, axis=-1), L0_ffn_router_w, L0_ffn_router_b, L0_ffn_Wi, L0_ffn_Wh, L0_ffn_b, L0_ffn_Wo, L0_ffn_bo)
    h = h + _L1_attn_ref(_layernorm(h, axis=-1), L1_attn_w_q, L1_attn_w_k, L1_attn_w_v, L1_attn_w_out, L1_attn_b_out)
    h = h + _L1_ffn_ref(_layernorm(h, axis=-1), L1_ffn_gw1, L1_ffn_gb1, L1_ffn_gw2, L1_ffn_gb2, L1_ffn_we1, L1_ffn_be1, L1_ffn_we2, L1_ffn_be2)
    return h

_drawn_inputs = setup_inputs


def setup_inputs(seed=0):
    import zlib

    import numpy as np

    out = dict(_drawn_inputs(seed))
    spreads = {'L0_ffn_router_b': (0.0, 0.1),
     'L0_ffn_b': (0.0, 0.43),
     'L0_ffn_bo': (0.0, 0.1),
     'L1_attn_b_out': (0.0, 0.1),
     'L1_ffn_gb1': (0.0, 0.1),
     'L1_ffn_gb2': (0.0, 0.1),
     'L1_ffn_be1': (0.0, 0.1),
     'L1_ffn_be2': (0.0, 0.1)}
    factors = {'L0_attn_A_real': 8.0,
     'L0_attn_A_imag': 6.016,
     'L0_attn_B': 3.535,
     'L0_attn_C': 3.436,
     'L0_attn_delta': 6.034,
     'L0_ffn_Wi': 3.031,
     'L0_ffn_Wh': 8.0,
     'L1_attn_w_q': 8.0,
     'L1_attn_w_k': 8.0}
    for name, (base, spread) in spreads.items():
        noise = np.random.default_rng([zlib.crc32(name.encode()), seed]).standard_normal(out[name].shape)
        drawn = base * np.exp(spread * noise) if base else spread * noise
        out[name] = jnp.asarray(drawn.astype(out[name].dtype))
    for name, factor in factors.items():
        out[name] = (out[name] * factor).astype(out[name].dtype)
    return out
```

```python
from contextlib import ExitStack

import concourse.bass as bass
from concourse import mybir

P = 128
TILES, D = 32, 128
SEQS, SEQ = 8, 512
CHUNKS = SEQ // P
STATES = 16
HALF_D = D // 2
F32, F16, I32 = mybir.dt.float32, mybir.dt.float16, mybir.dt.int32
ACT, ALU, AX = mybir.ActivationFunctionType, mybir.AluOpType, mybir.AxisListType
EPS = 1e-5


class Chain:

    def __init__(self, engine, sem, base=0):
        self.engine, self.sem, self.base, self.n = engine, sem, base, 0

    def __call__(self, instruction):
        instruction.then_inc(self.sem, 1)
        self.n += 1

    def done(self, back=0):
        self.engine.wait_ge(self.sem, self.base + (self.n - back))

    def link(self, instruction):
        self(instruction)
        self.done()


class Memory:

    def __init__(self, nc, stage, ctx):
        self.nc, self.stage, self.ctx, self.sems = nc, stage, ctx, []
        ctx.callback(self.clear)

    def sbuf(self, name, shape, dtype=F32):
        return self.ctx.enter_context(self.nc.sbuf_tensor(f"{self.stage}_{name}", shape, dtype))

    def psum(self, name, shape, dtype=F32):
        return self.ctx.enter_context(self.nc.psum_tensor(f"{self.stage}_{name}", shape, dtype))

    def sem(self, name):
        self.sems.append(self.nc.alloc_semaphore(f"{self.stage}_{name}"))
        return self.sems[-1]

    def clear(self):
        if self.sems:
            self.nc.clear_and_free_semaphores(self.sems)
            self.nc.all_engine_barrier()


def token_statistics(nc, dve, chain, H, stats, mean, var, scratch):
    for t in range(TILES):
        chain(nc.vector.bn_stats(stats[:, t, :], H[:, t, :]))
    chain.done()
    chain(nc.vector.tensor_tensor(mean, stats[:, :, 1], stats[:, :, 4], ALU.add))
    chain(nc.vector.tensor_tensor(scratch, stats[:, :, 1], stats[:, :, 4], ALU.subtract))
    chain(nc.vector.tensor_tensor(var, stats[:, :, 2], stats[:, :, 5], ALU.add))
    chain.done()
    chain(nc.vector.tensor_scalar(mean, mean, 0.5, None, ALU.mult))
    chain(nc.vector.scalar_tensor_tensor(scratch, scratch, 0.25, scratch, ALU.mult, ALU.mult))
    chain.done()
    return nc.vector.scalar_tensor_tensor(var, var, 1.0 / D, scratch, ALU.mult, ALU.add)


def embed_and_convolve(nc, H, ident, ident16, d):
    NPOS = d["positions"].shape[1]
    FINE_STEP = 32
    NA, NR = SEQ // FINE_STEP, FINE_STEP
    TWO_PI = 6.283185307179586
    TWO_PI_HI = 6.28125
    ROUND = 1.5 * 2.0 ** 23
    GROUPS, GT = 4, TILES // 4
    SLOTS = 4

    with ExitStack() as ctx:
        m = Memory(nc, "conv", ctx)
        idx = m.sbuf("ids", [P, TILES], I32)
        cb = m.sbuf("cluster_b", [P, HALF_D])
        cw = m.sbuf("coarse_w", [P, D])
        fwd = m.sbuf("dft", [P, CHUNKS, SEQ])
        inv = m.sbuf("inverse_dft", [P, SLOTS, SEQ])
        par = m.sbuf("ssm_params", [P, 4, STATES])
        delta = m.sbuf("delta", [P, 1])
        pos = m.sbuf("positions", [P, NPOS])
        U = m.sbuf("u", [P, TILES, D])
        logits = m.sbuf("logits", [P, GT, HALF_D])
        top = m.sbuf("top", [P, GT])
        total = m.sbuf("total", [P, GT])
        dist = m.sbuf("dist", [P, GT, HALF_D])
        distT = m.sbuf("distT", [P, GT // 2, P])
        dtA = m.sbuf("dtA", [P, 2, STATES])
        phase = m.sbuf("phase", [P, NPOS, STATES])
        turns = m.sbuf("turns", [P, NPOS, STATES])
        sin = m.sbuf("sin", [P, NPOS, STATES])
        cos = m.sbuf("cos", [P, NPOS, STATES])
        mag = m.sbuf("mag", [P, NPOS, STATES])
        small = m.sbuf("small", [P, 16, STATES])
        fine = m.sbuf("fine", [P, NR, 2 * STATES])
        rough = m.sbuf("rough", [P, NA, 2 * STATES])
        prod = m.sbuf("prod", [P, NA // 4, NR, 2 * STATES])
        K = m.sbuf("k", [P, SEQ])
        KT = m.sbuf("kT", [P, CHUNKS, D])
        Kr = m.sbuf("k_re", [P, 2, 2, D])
        Krn = m.sbuf("k_re_nyquist", [P, 2, D])
        Ki = m.sbuf("k_im", [P, 2, 2, D])
        stats = m.sbuf("stats", [P, TILES, 6])
        mean = m.sbuf("mean", [P, TILES])
        var = m.sbuf("var", [P, TILES])
        tmp = m.sbuf("tmp", [P, TILES])
        eps = m.sbuf("eps", [P, 1])
        terms = m.sbuf("terms", [P, 12, 512])
        sums = m.sbuf("sums", [P, 4, 512])
        Y = m.sbuf("y", [P, 2, SLOTS, 2, 512])

        ps = m.psum("ps", [P, 8, 512])

        idx_in, params_in, cw_in, dft_in, inv_in, idn_in = (m.sem(n) for n in (
            "idx_in", "params_in", "cw_in", "dft_in", "inv_in", "ident_in"))
        gathered = [m.sem(f"gathered{g}") for g in range(GROUPS)]
        shifted, exped, dist_ready, turned, distT_ready, coarse_done, coarse_in_h = (m.sem(n) for n in (
            "shifted", "exped", "dist_ready", "turned", "distT_ready", "coarse_done", "coarse_in_h"))
        tanh_ready, mag_in, mag_ready, trig_in, trig_ready, k_ready, kT_psum, kT_ready, kf_psum, kf_ready = (
            m.sem(n) for n in ("tanh_ready", "mag_in", "mag_ready", "trig_in", "trig_ready", "k_ready",
                               "kT_psum", "kT_ready", "kf_psum", "kf_ready"))
        var_ready, std_ready, u_ready, eps_ready, cw_cleared = (
            m.sem(n) for n in ("var_ready", "std_ready", "u_ready", "eps_ready", "cw_cleared"))
        spectrum, terms_ready, y_ready, pool_sums, out_psum, out_done, dve_own = (m.sem(n) for n in (
            "spectrum", "terms_ready", "y_ready", "pool_sums", "out_psum", "out_done", "dve_own"))

        block = ctx.enter_context(nc.Block())

        @block.sync
        def _(sp):
            sp.dma_start(idx[:, :], d["ids"]).then_inc(idx_in, 16)
            for n, source in enumerate((d["A_re"], d["A_im"], d["B_in"], d["C_in"])):
                sp.dma_start(par[:, n, :], source).then_inc(params_in, 16)
            sp.dma_start(delta[:, :], d["delta"]).then_inc(params_in, 16)
            sp.dma_start(pos[:, :], d["positions"]).then_inc(params_in, 16)
            sp.dma_start(cb[:, :], d["cluster_b"]).then_inc(cw_in, 16)
            sp.wait_ge(cw_cleared, 1)
            for half in range(2):
                here = slice(HALF_D * half, HALF_D * (half + 1))
                sp.dma_start(cw[here, here], d["coarse_w"]).then_inc(cw_in, 16)
            sp.dma_start(ident[:, :], d["ident"]).then_inc(idn_in, 16)
            sp.dma_start(ident16[:, :], d["ident16"]).then_inc(idn_in, 16)
            sp.dma_start(fwd[:, :, :], d["dft"].rearrange("(c p) f -> p c f", p=P)).then_inc(dft_in, 16)
            sp.dma_start(inv[:, :, :], d["inverse_dft"].rearrange("(c p) l -> p c l", p=P)).then_inc(inv_in, 16)

        @block.gpsimd
        def _(pool):
            pool.wait_ge(idx_in, 16)
            for t in range(TILES):
                pool.indirect_dma_start(
                    out=H[:, t, :], out_offset=None, in_=d["table"],
                    in_offset=bass.IndirectOffsetOnAxis(ap=idx[:, t:t + 1], axis=0),
                ).then_inc(gathered[t // GT], 16)
            for u in range(4):
                half, b = u // 2, u % 2
                pool.wait_ge(terms_ready, 12 * (u + 1))
                if u >= 1:
                    pool.wait_ge(pool_sums, 8 * u)
                for n, (x, y, op) in enumerate(((4, 5, ALU.subtract), (6, 7, ALU.subtract), (8, 9, ALU.add), (10, 11, ALU.add))):
                    nc.gpsimd.tensor_tensor(sums[:, n, :], terms[:, x, :], terms[:, y, :], op).then_inc(pool_sums, 1)
                nc.gpsimd.tensor_tensor(Y[:, half, b, 0, :], terms[:, 0, :], terms[:, 1, :], ALU.subtract).then_inc(pool_sums, 1)
                nc.gpsimd.tensor_tensor(Y[:, half, 2 + b, 0, :], terms[:, 2, :], terms[:, 3, :], ALU.add).then_inc(pool_sums, 1)
                pool.wait_ge(pool_sums, 8 * u + 4)
                nc.gpsimd.tensor_tensor(Y[:, half, b, 1, :], sums[:, 0, :], sums[:, 1, :], ALU.add).then_inc(pool_sums, 1)
                nc.gpsimd.tensor_tensor(Y[:, half, 2 + b, 1, :], sums[:, 2, :], sums[:, 3, :], ALU.add).then_inc(pool_sums, 1)

        @block.scalar
        def _(act):
            act.wait_ge(mag_in, 1)
            nc.scalar.activation(small[:, 0, :], dtA[:, 0, :], ACT.Tanh, scale=0.5).then_inc(tanh_ready, 1)
            nc.scalar.activation(mag[:, :, :], mag[:, :, :], ACT.Exp).then_inc(mag_ready, 1)
            act.wait_ge(trig_in, 2)
            nc.scalar.activation(sin[:, :, :], phase[:, :, :], ACT.Sin).then_inc(trig_ready, 1)
            nc.scalar.activation(cos[:, :, :], turns[:, :, :], ACT.Sin).then_inc(trig_ready, 1)
            for g in range(GROUPS):
                act.wait_ge(shifted, g + 1)
                if g >= 1:
                    act.wait_ge(dist_ready, g)
                nc.scalar.activation(dist[:, :, :], logits[:, :, :], ACT.Exp).then_inc(exped, 1)
                act.wait_ge(turned, g + 1)
                if g >= 1:
                    act.wait_ge(coarse_done, g)
                nc.scalar.activation(distT[:, :, :], ps[:, 0, :], ACT.Copy).then_inc(distT_ready, 1)
                act.wait_ge(coarse_done, g + 1)
                nc.scalar.activation(H[:, g * GT:(g + 1) * GT, HALF_D:D],
                                     ps[:, 1, :].rearrange("p (t c) -> p t c", c=HALF_D), ACT.Copy).then_inc(coarse_in_h, 1)
            act.wait_ge(kT_psum, 1)
            nc.scalar.activation(KT[:, :, :], ps[:, 2, :], ACT.Copy).then_inc(kT_ready, 1)
            act.wait_ge(kf_psum, 1)
            for w in range(2):
                bank = ps[:, 3 + w, :].rearrange("p (s d) -> p s d", d=D)
                nc.scalar.activation(Kr[:, w, :, :], bank[:, 0:2, :], ACT.Copy).then_inc(kf_ready, 1)
                nc.scalar.activation(Ki[:, w, :, :], bank[:, 2:4, :], ACT.Copy).then_inc(kf_ready, 1)
                nc.scalar.activation(Krn[:, w, :], bank[:, 0, :], ACT.Copy).then_inc(kf_ready, 1)
            act.wait_ge(var_ready, 1)
            act.wait_ge(eps_ready, 1)
            nc.scalar.activation(var[:, :], var[:, :], ACT.Sqrt, bias=eps[:, 0:1]).then_inc(std_ready, 1)

        @block.tensor
        def _(pe):
            pe.wait_ge(idn_in, 32)
            pe.wait_ge(cw_in, 48)
            for g in range(GROUPS):
                pe.wait_ge(dist_ready, g + 1)
                if g >= 1:
                    pe.wait_ge(distT_ready, g)
                for t in range(GT // 2):
                    last = nc.tensor.transpose(ps[:, 0, t * P:(t + 1) * P],
                                               dist[:, 2 * t:2 * t + 2, :].rearrange("p t c -> p (t c)"), ident[:, :])
                last.then_inc(turned, 1)
                pe.wait_ge(distT_ready, g + 1)
                if g >= 1:
                    pe.wait_ge(coarse_in_h, g)
                for t in range(GT // 2):
                    last = nc.tensor.matmul(ps[:, 1, t * D:(t + 1) * D], distT[:, t, :], cw[:, :], start=True, stop=True)
                last.then_inc(coarse_done, 1)
            pe.wait_ge(k_ready, 1)
            for c in range(CHUNKS):
                last = nc.tensor.transpose(ps[:, 2, c * P:(c + 1) * P], K[:, c * P:(c + 1) * P], ident[:, :])
            last.then_inc(kT_psum, 1)
            pe.wait_ge(kT_ready, 1)
            pe.wait_ge(dft_in, 16)
            for w, chunks in enumerate((2, 4)):
                for s in range(SLOTS):
                    for c in range(chunks):
                        last = nc.tensor.matmul(ps[:, 3 + w, s * D:(s + 1) * D], fwd[:, c, s * P:(s + 1) * P], KT[:, c, :],
                                                start=(c == 0), stop=(c == chunks - 1))
            last.then_inc(kf_psum, 1)
            pe.wait_ge(u_ready, 1)
            pe.wait_ge(kf_ready, 6)
            pe.wait_ge(inv_in, 16)
            Uv = U[:, :, :].rearrange("p (b c) d -> p b c d", c=CHUNKS)

            def forward(u):
                half, b = u // 2, u % 2
                if u >= 1:
                    pe.wait_ge(terms_ready, 12 * u)
                for j in range(2):
                    for ri in range(2):
                        for c in range(2):
                            last = nc.tensor.matmul(ps[:, 2 * j + ri, :], fwd[:, 2 * j + c, (2 * ri + b) * P:(2 * ri + b + 1) * P],
                                                    Uv[:, 4 * half:4 * half + 4, 2 * j + c, :], start=(c == 0), stop=(c == 1))
                last.then_inc(spectrum, 1)

            def inverse(half):
                pe.wait_ge(pool_sums, 16 * (half + 1))
                for q in range(CHUNKS):
                    if half:
                        pe.wait_ge(out_done, q + 1)
                    for s in range(SLOTS):
                        last = nc.tensor.matmul(ps[:, 4 + q, :], inv[:, s, q * P:(q + 1) * P], Y[:, half, s, q // 2, :],
                                                start=(s == 0), stop=(s == SLOTS - 1))
                    last.then_inc(out_psum, 1)

            for u in range(3):
                forward(u)
            inverse(0)
            forward(3)
            inverse(1)

        @block.vector
        def _(dve):
            V = nc.vector
            own = Chain(dve, dve_own)
            V.memset(cw[:, :], 0.0).then_inc(cw_cleared, 1)
            V.memset(eps[:, :], EPS).then_inc(eps_ready, 1)
            dve.wait_ge(params_in, 96)
            own(V.tensor_scalar(dtA[:, 0, :], par[:, 0, :], delta[:, 0:1], None, ALU.mult))
            own.link(V.tensor_scalar(dtA[:, 1, :], par[:, 1, :], delta[:, 0:1], None, ALU.mult))
            where = pos[:, :].rearrange("p (c a) -> p c a", a=1).broadcast_to([P, NPOS, STATES])
            one = dtA[:, 0, :].rearrange("p (a n) -> p a n", a=1).broadcast_to([P, NPOS, STATES])
            two = dtA[:, 1, :].rearrange("p (a n) -> p a n", a=1).broadcast_to([P, NPOS, STATES])
            V.tensor_tensor(mag[:, :, :], where, one, ALU.mult).then_inc(mag_in, 1)
            own.link(V.tensor_tensor(phase[:, :, :], where, two, ALU.mult))
            own.link(V.tensor_scalar(turns[:, :, :], phase[:, :, :], 1.0 / TWO_PI, ROUND, ALU.mult, ALU.add))
            own.link(V.tensor_scalar(turns[:, :, :], turns[:, :, :], ROUND, None, ALU.subtract))
            own.link(V.scalar_tensor_tensor(phase[:, :, :], turns[:, :, :], -TWO_PI_HI, phase[:, :, :], ALU.mult, ALU.add))
            own.link(V.scalar_tensor_tensor(phase[:, :, :], turns[:, :, :], TWO_PI_HI - TWO_PI, phase[:, :, :], ALU.mult, ALU.add))
            own.link(V.tensor_scalar(phase[:, :, :], phase[:, :, :], 3.1415925, -3.1415925, ALU.min, ALU.max))
            V.scalar_tensor_tensor(turns[:, :, :], phase[:, :, :], -1.0, phase[:, :, :], ALU.mult, ALU.min).then_inc(trig_in, 1)
            dve.wait_ge(trig_in, 1)
            V.tensor_scalar(turns[:, :, :], turns[:, :, :], TWO_PI / 4, None, ALU.add).then_inc(trig_in, 1)
            t, em1, shc, er, ei, den, qr, qi, bc, x1, x2, wr, wi = (small[:, n, :] for n in range(13))
            ar, ai = par[:, 0, :], par[:, 1, :]
            dve.wait_ge(tanh_ready, 1)
            own(V.tensor_scalar(x1, t, -1.0, 1.0, ALU.mult, ALU.add))
            own(V.tensor_tensor(bc, par[:, 2, :], par[:, 3, :], ALU.mult))
            own(V.tensor_tensor(x2, ar, ar, ALU.mult))
            own(V.tensor_tensor(den, ai, ai, ALU.mult))
            own.done()
            own(V.reciprocal(x1, x1))
            own(V.tensor_tensor(den, den, x2, ALU.add))
            own.done()
            own(V.scalar_tensor_tensor(em1, t, 2.0, x1, ALU.mult, ALU.mult))
            own(V.reciprocal(den, den))
            own.done()
            dve.wait_ge(trig_ready, 2)
            dve.wait_ge(mag_ready, 1)
            half_sin, sin1, cos1 = sin[:, NPOS - 1, :], sin[:, 1, :], cos[:, 1, :]
            own(V.scalar_tensor_tensor(shc, half_sin, -2.0, half_sin, ALU.mult, ALU.mult))
            own(V.tensor_tensor(er, em1, cos1, ALU.mult))
            own(V.scalar_tensor_tensor(ei, em1, 1.0, sin1, ALU.add, ALU.mult))
            own.done()
            own.link(V.tensor_tensor(er, er, shc, ALU.add))
            own(V.tensor_tensor(qr, er, ar, ALU.mult))
            own(V.tensor_tensor(x1, ei, ai, ALU.mult))
            own(V.tensor_tensor(qi, ei, ar, ALU.mult))
            own(V.tensor_tensor(x2, er, ai, ALU.mult))
            own(V.tensor_tensor(bc, bc, den, ALU.mult))
            own.done()
            own(V.tensor_tensor(qr, qr, x1, ALU.add))
            own(V.tensor_tensor(qi, qi, x2, ALU.subtract))
            own.done()
            own(V.tensor_tensor(wr, qr, bc, ALU.mult))
            own(V.tensor_tensor(wi, qi, bc, ALU.mult))
            own(V.tensor_tensor(fine[:, :, 0:STATES], mag[:, 0:NR, :], cos[:, 0:NR, :], ALU.mult))
            own(V.tensor_tensor(fine[:, :, STATES:], mag[:, 0:NR, :], sin[:, 0:NR, :], ALU.mult))
            own(V.tensor_tensor(turns[:, 0:NA, :], mag[:, NR:NR + NA, :], cos[:, NR:NR + NA, :], ALU.mult))
            own(V.tensor_tensor(phase[:, 0:NA, :], mag[:, NR:NR + NA, :], sin[:, NR:NR + NA, :], ALU.mult))
            own.done()
            wr_b = wr.rearrange("p (a n) -> p a n", a=1).broadcast_to([P, NA, STATES])
            wi_b = wi.rearrange("p (a n) -> p a n", a=1).broadcast_to([P, NA, STATES])
            vr, vi = turns[:, 0:NA, :], phase[:, 0:NA, :]
            own(V.tensor_tensor(rough[:, :, 0:STATES], vr, wr_b, ALU.mult))
            own(V.tensor_tensor(sin[:, 0:NA, :], vi, wi_b, ALU.mult))
            own(V.tensor_tensor(rough[:, :, STATES:], vi, wr_b, ALU.mult))
            own(V.tensor_tensor(cos[:, 0:NA, :], vr, wi_b, ALU.mult))
            own.done()
            own(V.tensor_tensor(rough[:, :, 0:STATES], rough[:, :, 0:STATES], sin[:, 0:NA, :], ALU.subtract))
            own.link(V.scalar_tensor_tensor(rough[:, :, STATES:], rough[:, :, STATES:], -1.0, cos[:, 0:NA, :], ALU.mult, ALU.subtract))
            for q in range(4):
                shape = [P, NA // 4, NR, 2 * STATES]
                a = rough[:, q * NA // 4:(q + 1) * NA // 4, :].rearrange("p a (b n) -> p a b n", b=1).broadcast_to(shape)
                f = fine[:, :, :].rearrange("p (a r) n -> p a r n", a=1).broadcast_to(shape)
                own.link(V.tensor_tensor(prod[:, :, :, :], a, f, ALU.mult))
                own.link(V.tensor_reduce(K[:, q * P:(q + 1) * P], prod[:, :, :, :].rearrange("p a r n -> p (a r) n"), AX.X, ALU.add))
            V.tensor_copy(tmp[:, 0:1], eps[:, 0:1]).then_inc(k_ready, 1)
            dve.wait_ge(cw_in, 48)
            for g in range(GROUPS):
                dve.wait_ge(gathered[g], 16 * GT)
                if g >= 1:
                    dve.wait_ge(exped, g)
                cb_b = cb[:, :].rearrange("p (a c) -> p a c", a=1).broadcast_to([P, GT, HALF_D])
                own.link(V.tensor_tensor(logits[:, :, :], H[:, g * GT:(g + 1) * GT, HALF_D:D], cb_b, ALU.add))
                own.link(V.tensor_reduce(top[:, :], logits[:, :, :], AX.X, ALU.max))
                top_b = top[:, :].rearrange("p (t a) -> p t a", a=1).broadcast_to([P, GT, HALF_D])
                V.tensor_tensor(logits[:, :, :], logits[:, :, :], top_b, ALU.subtract).then_inc(shifted, 1)
                dve.wait_ge(exped, g + 1)
                own.link(V.tensor_reduce(total[:, :], dist[:, :, :], AX.X, ALU.add))
                own.link(V.reciprocal(total[:, :], total[:, :]))
                total_b = total[:, :].rearrange("p (t a) -> p t a", a=1).broadcast_to([P, GT, HALF_D])
                V.tensor_tensor(dist[:, :, :], dist[:, :, :], total_b, ALU.mult).then_inc(dist_ready, 1)
            dve.wait_ge(coarse_in_h, GROUPS)
            token_statistics(nc, dve, own, H, stats, mean[:, :], var[:, :], tmp[:, :]).then_inc(var_ready, 1)
            dve.wait_ge(kf_ready, 6)
            for w in range(2):
                own(V.tensor_copy(Krn[0:1, w, :], Ki[0:1, w, 0, :]))
            own.done()
            for w in range(2):
                own(V.memset(Ki[0:1, w, 0, :], 0.0))
            dve.wait_ge(std_ready, 1)
            own.link(V.reciprocal(var[:, :], var[:, :]))
            for t in range(TILES):
                last = V.tensor_scalar(U[:, t, :], H[:, t, :], mean[:, t:t + 1], var[:, t:t + 1], ALU.subtract, ALU.mult)
                own(last)
            own.done()
            V.tensor_copy(tmp[:, 0:1], eps[:, 0:1]).then_inc(u_ready, 1)
            Hv = H[:, :, :].rearrange("p (b c) d -> p b c d", c=CHUNKS)

            def add_out(half):
                for q in range(CHUNKS):
                    dve.wait_ge(out_psum, CHUNKS * half + q + 1)
                    V.tensor_tensor(Hv[:, 4 * half:4 * half + 4, q, :], ps[:, 4 + q, :].rearrange("p (b d) -> p b d", d=D),
                                    Hv[:, 4 * half:4 * half + 4, q, :], ALU.add).then_inc(out_done, 1)

            for u in range(4):
                half, b = u // 2, u % 2
                dve.wait_ge(spectrum, u + 1)
                if u >= 1:
                    dve.wait_ge(pool_sums, 8 * u)
                def wide(x):
                    return x.rearrange("p (a d) -> p a d", a=1).broadcast_to([P, 4, D])
                def bank(n):
                    return ps[:, n, :].rearrange("p (a d) -> p a d", d=D)
                real = [wide(Kr[:, w, b, :]) for w in range(2)]
                real_n = [wide(Krn[:, w, :]) if b == 0 else real[w] for w in range(2)]
                imag = [wide(Ki[:, w, b, :]) for w in range(2)]
                HEAD, WHOLE = 0, 1
                pairs = ((0, real[HEAD]), (1, imag[HEAD]), (0, imag[HEAD]), (1, real_n[HEAD]),
                         (0, real[WHOLE]), (1, imag[WHOLE]), (2, real[HEAD]), (3, imag[HEAD]),
                         (0, imag[WHOLE]), (1, real_n[WHOLE]), (2, imag[HEAD]), (3, real_n[HEAD]))
                for n, (source, coefficient) in enumerate(pairs):
                    V.tensor_tensor(terms[:, n, :].rearrange("p (a d) -> p a d", d=D), bank(source), coefficient,
                                    ALU.mult).then_inc(terms_ready, 1)
                if u == 3:
                    add_out(0)
            add_out(1)


X_SCALE = 2.0 ** 6
PARTS = 2
HI, LO = 0, 1


def split_products(pe, out, stationary, moving, start, stop, **options):
    pairs = ((HI, HI), (HI, LO), (LO, HI))
    for n, (a, b) in enumerate(pairs):
        last = pe.matmul(out, stationary(a), moving(b), start=start and n == 0, stop=stop and n == len(pairs) - 1, **options)
    return last


def normalize(nc, stage, H, XT, ident16):
    with ExitStack() as ctx:
        m = Memory(nc, stage, ctx)
        stats = m.sbuf("stats", [P, TILES, 6])
        per_token = m.sbuf("per_token", [P, 3, TILES])
        mean, var, tmp = (per_token[:, n, :] for n in range(3))
        eps = m.sbuf("eps", [P, 1])
        norm = m.sbuf("norm", [P, 2, CHUNKS, D])
        parts = m.sbuf("parts", [P, 2, PARTS, CHUNKS * D], F16)
        ps = m.psum("ps", [P, 2, PARTS, CHUNKS * P], F16)
        (own_sem, eps_ready, var_ready, std_ready, norm_ready, hi_ready, lo_ready, turned, xt_ready) = (m.sem(n) for n in (
            "own", "eps_ready", "var_ready", "std_ready", "norm_ready", "hi_ready", "lo_ready", "turned", "xt_ready"))
        block = ctx.enter_context(nc.Block())

        @block.vector
        def _(dve):
            V = nc.vector
            own = Chain(dve, own_sem)
            V.memset(eps[:, :], EPS / X_SCALE ** 2).then_inc(eps_ready, 1)
            token_statistics(nc, dve, own, H, stats, mean[:, :], var[:, :], tmp[:, :]).then_inc(var_ready, 1)
            dve.wait_ge(std_ready, 1)
            own.link(V.reciprocal(var[:, :], var[:, :]))
            with dve.Fori(0, SEQS // 2) as i:
                for p in range(2):
                    b = i * 2 + p
                    for c in range(CHUNKS):
                        last = V.tensor_scalar(norm[:, p, c, :], H[:, bass.ds(b * CHUNKS + c, 1), :].rearrange("p a d -> p (a d)"),
                                               mean[:, bass.ds(b * CHUNKS + c, 1)], var[:, bass.ds(b * CHUNKS + c, 1)],
                                               ALU.subtract, ALU.mult)
                        last.then_inc(norm_ready, 1)
                    dve.wait_ge(norm_ready, (b + 1) * CHUNKS)
                    dve.wait_ge(hi_ready, b + 1)
                    V.tensor_tensor(parts[:, p, LO, :], norm[:, p, :, :].rearrange("p c d -> p (c d)"),
                                    parts[:, p, HI, :], ALU.subtract).then_inc(lo_ready, 1)

        @block.scalar
        def _(act):
            A = nc.scalar
            act.wait_ge(var_ready, 1)
            act.wait_ge(eps_ready, 1)
            A.activation(var[:, :], var[:, :], ACT.Sqrt, bias=eps[:, 0:1], scale=X_SCALE ** -2).then_inc(std_ready, 1)

            def high(b, p):
                act.wait_ge(norm_ready, (b + 1) * CHUNKS)
                A.activation(parts[:, p, HI, :], norm[:, p, :, :].rearrange("p c d -> p (c d)"), ACT.Copy).then_inc(hi_ready, 1)

            def out(b, p):
                act.wait_ge(turned, b + 1)
                act.wait_ge(var_ready, 1)
                A.activation(XT[:, bass.ds(b, 1), :, :], ps[:, p, :, :], ACT.Copy).then_inc(xt_ready, 1)

            high(0, 0)
            high(1, 1)
            with act.Fori(0, SEQS // 2 - 1) as i:
                for p in range(2):
                    out(i * 2 + p, p)
                    high(i * 2 + p + 2, p)
            out(SEQS - 2, 0)
            out(SEQS - 1, 1)

        @block.tensor
        def _(pe):
            def turn(b, p, first):
                pe.wait_ge(lo_ready, b + 1)
                if not first:
                    pe.wait_ge(xt_ready, b - 1)
                for part in range(PARTS):
                    for c in range(CHUNKS):
                        last = nc.tensor.transpose(ps[:, p, part, c * P:(c + 1) * P], parts[:, p, part, c * D:(c + 1) * D], ident16[:, :])
                last.then_inc(turned, 1)

            for p in range(2):
                turn(p, p, True)
            with pe.Fori(1, SEQS // 2) as i:
                for p in range(2):
                    turn(i * 2 + p, p, False)


EXPERTS = 8
NEVER = -3.0e38


def top_two(V, own, scores, rank, first, second, m1, m2, work):
    shape = scores.shape
    T = shape[1]
    rank_b = rank.rearrange("p (a e) -> p a e", a=1).broadcast_to(shape)
    wide = lambda x: x.rearrange("p (t a) -> p t a", a=1).broadcast_to(shape)
    picked = work[:, 0:T]
    own.link(V.tensor_reduce(m1, scores, AX.X, ALU.max))
    for onehot, best in ((first, m1), (second, m2)):
        own.link(V.tensor_tensor(onehot, scores, wide(best), ALU.is_equal))
        own.link(V.tensor_tensor(onehot, onehot, rank_b, ALU.mult))
        own.link(V.tensor_reduce(picked, onehot, AX.X, ALU.max))
        own.link(V.tensor_tensor(onehot, onehot, wide(picked), ALU.is_equal))
        if onehot is first:
            own.link(V.scalar_tensor_tensor(scores, first, NEVER, scores, ALU.mult, ALU.add))
            own.link(V.tensor_reduce(m2, scores, AX.X, ALU.max))


def load_bias_blocks(sp, blocks, bias, cleared, loaded):
    sp.wait_ge(cleared, 1)
    for t in range(CHUNKS):
        sp.dma_start(blocks[32 * t:32 * t + EXPERTS, t * D:(t + 1) * D], bias).then_inc(loaded, 16)


def route_recurrent(nc, H, XT, ident, d, combine, mask_rows):
    COLS = 32
    with ExitStack() as ctx:
        m = Memory(nc, "route", ctx)
        rw = m.sbuf("router_w", [P, EXPERTS])
        rws = m.sbuf("router_w_parts", [P, PARTS, EXPERTS], F16)
        rb = m.sbuf("router_b", [P, EXPERTS])
        rank = m.sbuf("rank", [P, EXPERTS])
        bias_blocks = m.sbuf("bias_blocks", [P, CHUNKS * D])
        logits = m.sbuf("logits", [P, TILES, EXPERTS])
        first = m.sbuf("first", [P, TILES, EXPERTS])
        second = m.sbuf("second", [P, TILES, EXPERTS])
        per_token = m.sbuf("per_token", [P, 5, TILES])
        m1, m2, e, r1, work = (per_token[:, n, :] for n in range(5))
        share = m.sbuf("share", [P, TILES, EXPERTS])
        record = m.sbuf("record", [P, TILES, COLS])
        rows = m.sbuf("rows", [P, SEQS, P])
        rows16 = m.sbuf("rows16", [P, SEQS, P], F16)
        psL = m.psum("psL", [P, 512])
        psR = m.psum("psR", [P, SEQS, P])
        psB = m.psum("psB", [P, 2, CHUNKS * D])
        (params_in, w_hi, w_parts, cleared, bias_in, logits_psum, own_sem, gap_ready, exp_ready, record_ready, rows_psum,
         rows_ready, rows16_ready, stored, bias_psum, bias_added) = (m.sem(n) for n in (
             "params_in", "w_hi", "w_parts", "cleared", "bias_in", "logits_psum", "own", "gap_ready", "exp_ready", "record_ready",
             "rows_psum", "rows_ready", "rows16_ready", "stored", "bias_psum", "bias_added"))
        block = ctx.enter_context(nc.Block())

        @block.sync
        def _(sp):
            sp.dma_start(rw[:, :], d["router_w"]).then_inc(params_in, 16)
            sp.dma_start(rb[:, :], d["router_b"]).then_inc(params_in, 16)
            sp.dma_start(rank[:, :], d["rank"]).then_inc(params_in, 16)
            load_bias_blocks(sp, bias_blocks, d["bo"], cleared, bias_in)
            sp.wait_ge(rows16_ready, 1)
            for t in range(CHUNKS):
                sp.dma_start(mask_rows.rearrange("j (b c q) -> j b c q", b=SEQS, c=CHUNKS)[:, :, t, :],
                             rows16[COLS * t + EXPERTS:COLS * t + 3 * EXPERTS, :, :]).then_inc(stored, 16)
            sp.wait_ge(stored, 16 * CHUNKS)

        @block.scalar
        def _(act):
            A = nc.scalar
            act.wait_ge(params_in, 48)
            A.activation(rws[:, HI, :], rw[:, :], ACT.Copy, scale=W_SCALE_ROUTER).then_inc(w_hi, 1)
            act.wait_ge(gap_ready, 1)
            A.activation(e[:, :], e[:, :], ACT.Exp).then_inc(exp_ready, 1)
            act.wait_ge(rows_psum, 1)
            A.activation(rows[:, :, :], psR[:, :, :], ACT.Copy).then_inc(rows_ready, 1)
            A.activation(rows16[:, :, :], psR[:, :, :], ACT.Copy).then_inc(rows16_ready, 1)

        @block.tensor
        def _(pe):
            pe.wait_ge(w_parts, 1)
            with pe.Fori(0, SEQS) as b:
                for c in range(CHUNKS):
                    last = split_products(
                        nc.tensor, psL[:, bass.ds((b * CHUNKS + c) * EXPERTS, EXPERTS)],
                        lambda part: XT[:, bass.ds(b, 1), part, c * P:(c + 1) * P].rearrange("p a n -> p (a n)"),
                        lambda part: rws[:, part, :], True, True)
                last.then_inc(logits_psum, 1)
            pe.wait_ge(record_ready, 1)
            for b in range(SEQS):
                last = nc.tensor.transpose(psR[:, b, :], record[:, b * CHUNKS:(b + 1) * CHUNKS, :].rearrange("p c j -> p (c j)"), ident[:, :])
            last.then_inc(rows_psum, 1)
            pe.wait_ge(rows_ready, 1)
            pe.wait_ge(bias_in, 16 * CHUNKS)
            for b in range(SEQS):
                if b >= 2:
                    pe.wait_ge(bias_added, b - 1)
                nc.tensor.matmul(psB[:, b % 2, :], rows[:, b, :], bias_blocks[:, :], start=True, stop=True).then_inc(bias_psum, 1)

        @block.vector
        def _(dve):
            V = nc.vector
            own = Chain(dve, own_sem)
            V.memset(bias_blocks[:, :], 0.0).then_inc(cleared, 1)
            own(V.memset(record[:, :, 3 * EXPERTS:], 0.0))
            dve.wait_ge(params_in, 48)
            dve.wait_ge(w_hi, 1)
            V.scalar_tensor_tensor(rws[:, LO, :], rw[:, :], W_SCALE_ROUTER, rws[:, HI, :], ALU.mult, ALU.subtract).then_inc(w_parts, 1)
            dve.wait_ge(logits_psum, SEQS)
            rb_b = rb[:, :].rearrange("p (a e) -> p a e", a=1).broadcast_to([P, TILES, EXPERTS])
            own.link(V.scalar_tensor_tensor(logits[:, :, :], psL[:, 0:TILES * EXPERTS].rearrange("p (t e) -> p t e", e=EXPERTS),
                                            1.0 / (X_SCALE * W_SCALE_ROUTER), rb_b, ALU.mult, ALU.add))
            top_two(V, own, logits[:, :, :], rank[:, :], first[:, :, :], second[:, :, :], m1[:, :], m2[:, :], work[:, :])
            V.tensor_tensor(e[:, :], m2[:, :], m1[:, :], ALU.subtract).then_inc(gap_ready, 1)
            dve.wait_ge(exp_ready, 1)
            own.link(V.tensor_scalar(r1[:, :], e[:, :], 1.0, None, ALU.add))
            own.link(V.reciprocal(r1[:, :], r1[:, :]))
            own(V.tensor_tensor(e[:, :], e[:, :], r1[:, :], ALU.mult))
            wide = lambda x: x.rearrange("p (t a) -> p t a", a=1).broadcast_to([P, TILES, EXPERTS])
            own(V.tensor_tensor(share[:, :, :], first[:, :, :], wide(r1[:, :]), ALU.mult))
            own(V.tensor_copy(record[:, :, EXPERTS:2 * EXPERTS], first[:, :, :]))
            own(V.tensor_copy(record[:, :, 2 * EXPERTS:3 * EXPERTS], second[:, :, :]))
            own.done()
            own.link(V.tensor_tensor(second[:, :, :], second[:, :, :], wide(e[:, :]), ALU.mult))
            own.link(V.tensor_tensor(record[:, :, 0:EXPERTS], share[:, :, :], second[:, :, :], ALU.add))
            V.tensor_scalar(combine[:, :, :], record[:, :, 0:EXPERTS], 1.0 / OUT_SCALE, None, ALU.mult).then_inc(record_ready, 1)
            for b in range(SEQS):
                dve.wait_ge(bias_psum, b + 1)
                here = H[:, b * CHUNKS:(b + 1) * CHUNKS, :].rearrange("p c d -> p (c d)")
                V.tensor_tensor(here, psB[:, b % 2, :], here, ALU.add).then_inc(bias_added, 1)


W_SCALE_ROUTER = 2.0 ** 8
H_SCALE = 2.0 ** 8
WI_SCALE = 2.0 ** 8
WH_SCALE = X_SCALE * WI_SCALE / H_SCALE
WO_SCALE = 2.0 ** 6
GATE_SCALE = X_SCALE * WI_SCALE
OUT_SCALE = H_SCALE * WO_SCALE
STEPS, WIDTH = SEQS, SEQ
GATES = 4
IN, FORGET, CELL, OUT = range(GATES)


def recurrent_experts(nc, H, XT, d, combine, mask_rows):
    GD = GATES * D
    ORDER = (IN, CELL, FORGET, OUT)
    with ExitStack() as ctx:
        m = Memory(nc, "lstm", ctx)
        biases = m.sbuf("biases", [P, EXPERTS * GATES])
        bias = m.sbuf("bias", [P, 2, GATES])
        raw = m.sbuf("weights", [P, 2, 2 * GD + D])
        wp = m.sbuf("weight_parts", [P, 2, PARTS, 2 * GD + D], F16)
        mask = m.sbuf("mask", [P, 2, 2, WIDTH], F16)
        xm = m.sbuf("masked_x", [P, 2, 2, PARTS, WIDTH], F16)
        gates = m.sbuf("gates", [P, 2, GATES, WIDTH])
        cell = m.sbuf("cell", [P, 2, WIDTH])
        tc = m.sbuf("tanh_cell", [P, 2, WIDTH])
        hid = m.sbuf("hidden", [P, 2, WIDTH])
        hp = m.sbuf("hidden_parts", [P, 2, PARTS, WIDTH], F16)
        z1 = m.sbuf("second_choice", [P, PARTS, WIDTH], F16)
        z = m.sbuf("chosen", [P, 2, STEPS, PARTS, WIDTH], F16)
        ps = m.psum("ps", [P, 8, WIDTH])
        bias_in = m.sem("bias_in")
        weights_in = [m.sem(f"weights_in{p}") for p in range(2)]
        mask_in = [[m.sem(f"mask_in{p}{k}") for k in range(2)] for p in range(2)]
        (bias_ready, hi_weights, weights_ready, xm_ready, gate_psum, gate_ready, own_sem, cell_ready, tc_ready, hidden_ready,
         hidden_hi, hidden_lo, z0_ready, z1_ready, z_ready, wo_psum, wo_added) = (m.sem(n) for n in (
             "bias_ready", "hi_weights", "weights_ready", "xm_ready", "gate_psum", "gate_ready", "own", "cell_ready", "tc_ready",
             "hidden_ready", "hidden_hi", "hidden_lo", "z0_ready", "z1_ready", "z_ready", "wo_psum", "wo_added"))
        block = ctx.enter_context(nc.Block())

        skip = lambda e, parity: None

        def schedule(engine, step, finish=skip, extra=skip, before=skip):
            def rest(e, parity):
                before(e, parity)
                step(e, parity, 1, 1)
                extra(e, parity)
                with engine.Fori(1, STEPS // 2) as j:
                    for p in range(2):
                        step(e, parity, j * 2 + p, p)

            step(0, 0, 0, 0)
            rest(0, 0)
            step(1, 1, 0, 0)
            finish(0, 0)
            with engine.Fori(0, EXPERTS // 2 - 1) as i:
                for n in (1, 2):
                    rest(i * 2 + n, n % 2)
                    step(i * 2 + n + 1, 1 - n % 2, 0, 0)
                    finish(i * 2 + n, n % 2)
            rest(EXPERTS - 1, 1)
            finish(EXPERTS - 1, 1)

        is_first = lambda e, s: isinstance(s, int) and isinstance(e, int) and e == 0 and s == 0
        at_start = lambda e, s: isinstance(s, int) and s == 0

        @block.sync
        def _(sp):
            sp.dma_start(biases[:, :], d["lstm_b"]).then_inc(bias_in, 16)

            def load_weights(e, parity):
                for n, (name, at, width) in enumerate((("Wi", 0, GD), ("Wh", GD, GD), ("Wo", 2 * GD, D))):
                    sp.dma_start(raw[:, parity, at:at + width], d[name][bass.ds(e * P, P), :]).then_inc(weights_in[parity], 16)

            def step(e, parity, s, p):
                n_s = e * STEPS + s
                for k in range(2):
                    if not (isinstance(n_s, int) and n_s < 2):
                        sp.wait_ge(z_ready, n_s - 1)
                    row = mask_rows[bass.ds(e + k * EXPERTS, 1), bass.ds(s * WIDTH, WIDTH)]
                    sp.dma_start(mask[:, p, k, :], row.partition_broadcast(P)).then_inc(mask_in[p][k], 16)

            def before(e, parity):
                if not (isinstance(e, int) and e == EXPERTS - 1):
                    if not (isinstance(e, int) and e == 0):
                        sp.wait_ge(weights_ready, e)
                    load_weights(e + 1, 1 - parity)

            load_weights(0, 0)
            schedule(sp, step, before=before)

        @block.gpsimd
        def _(pool):
            def z0(n_s, e_parity, s, p):
                pool.wait_ge(hidden_lo, n_s * 2 + 1)
                m0 = mask[:, p, 0, :].rearrange("p (a n) -> p a n", a=1).broadcast_to([P, PARTS, WIDTH])
                nc.gpsimd.tensor_tensor(z[:, e_parity, bass.ds(s, 1), :, :].rearrange("p a h n -> p (a h) n"), hp[:, 0, :, :], m0,
                                        ALU.mult).then_inc(z0_ready, 1)

            def step(e, parity, s, p):
                n_s = e * STEPS + s
                for k in range(2):
                    pool.wait_ge(mask_in[p][k], e * (STEPS // 2 * 16) + (s - p) * 8 + 16)
                if not (isinstance(n_s, int) and n_s < 2):
                    pool.wait_ge(gate_psum, (n_s - 1) * 2 * GATES)
                shape = [P, 2, PARTS, WIDTH]
                m_b = mask[:, p, :, :].rearrange("p k (a n) -> p k a n", a=1).broadcast_to(shape)
                x_b = XT[:, bass.ds(s, 1), :, :].broadcast_to(shape)
                nc.gpsimd.tensor_tensor(xm[:, p, :, :, :], x_b, m_b, ALU.mult).then_inc(xm_ready, 1)
                if at_start(e, s):
                    if not is_first(e, s):
                        z0(n_s - 1, 1 - parity, STEPS - 1, 1)
                else:
                    z0(n_s - 1, parity, s - 1, 1 - p)

            schedule(pool, step)
            z0(EXPERTS * STEPS - 1, 1, STEPS - 1, 1)

        @block.tensor
        def _(pe):
            def w(parity, part, at, gate):
                return wp[:, parity, part, at + gate * D:at + (gate + 1) * D]

            def step(e, parity, s, p):
                n_s = e * STEPS + s
                for k in range(2):
                    n_u = n_s * 2 + k
                    if at_start(e, s) and k == 0:
                        pe.wait_ge(weights_ready, e + 1)
                    pe.wait_ge(xm_ready, n_s + 1)
                    if not is_first(e, s):
                        pe.wait_ge(gate_ready, (n_u - 1) * GATES)
                    if isinstance(s, int) and s == 1 and not (isinstance(e, int) and e == 0):
                        pe.wait_ge(wo_added, e * STEPS - STEPS + 4 * (k + 1))
                    for g in ORDER:
                        last = split_products(nc.tensor, ps[:, 4 * k + g, :], lambda part: w(parity, part, 0, g),
                                              lambda part: xm[:, p, k, part, :], True, at_start(e, s))
                        if at_start(e, s):
                            last.then_inc(gate_psum, 1)
                    if not at_start(e, s):
                        pe.wait_ge(hidden_lo, n_u - 1)
                        for g in ORDER:
                            split_products(nc.tensor, ps[:, 4 * k + g, :], lambda part: w(parity, part, GD, g),
                                           lambda part: hp[:, k, part, :], False, True).then_inc(gate_psum, 1)

            def finish(e, parity):
                last_step = isinstance(e, int) and e == EXPERTS - 1
                for half in range(2):
                    with pe.Fori(4 * half, 4 * half + 4) as q:
                        pe.wait_ge(gate_ready, ((e * STEPS + STEPS + (0 if last_step else 1)) * 2 - 1 + half) * GATES)
                        pe.wait_ge(z_ready, e * STEPS + q + 1)
                        for c in range(CHUNKS):
                            last = split_products(
                                nc.tensor, ps[:, bass.ds(q, 1), c * P:(c + 1) * P].rearrange("p a n -> p (a n)"),
                                lambda part: z[:, parity, bass.ds(q, 1), part, c * P:(c + 1) * P].rearrange("p a n -> p (a n)"),
                                lambda part: wp[:, parity, part, 2 * GD:], True, True)
                        last.then_inc(wo_psum, 1)

            schedule(pe, step, finish=finish)

        def split_high(act, e, parity):
            act.wait_ge(weights_in[parity], (e // 2 + 1) * 48 if isinstance(e, int) else (e - parity) * 24 + 48)
            for at, width, scale in ((0, GD, WI_SCALE), (GD, GD, WH_SCALE), (2 * GD, D, WO_SCALE)):
                nc.scalar.activation(wp[:, parity, HI, at:at + width], raw[:, parity, at:at + width], ACT.Copy, scale=scale).then_inc(hi_weights, 1)

        @block.scalar
        def _(act):
            A = nc.scalar
            A.preload_act_table(ACT.Sigmoid)
            split_high(act, 0, 0)
            act.wait_ge(bias_in, 16)

            def take_bias(e, parity):
                A.activation(bias[:, parity, :], biases[:, bass.ds(e * GATES, GATES)], ACT.Copy).then_inc(bias_ready, 1)

            take_bias(0, 0)

            def step(e, parity, s, p):
                n_s = e * STEPS + s
                for k in range(2):
                    n_u = n_s * 2 + k
                    if at_start(e, s):
                        act.wait_ge(bias_ready, e + 1)
                    if not is_first(e, s):
                        act.wait_ge(hidden_ready, n_u - 1)
                    for n, g in enumerate(ORDER):
                        act.wait_ge(gate_psum, n_u * GATES + n + 1)
                        done = A.activation(gates[:, k, g, :], ps[:, 4 * k + g, :], ACT.Tanh if g == CELL else ACT.Sigmoid,
                                            bias=bias[:, parity, g:g + 1], scale=1.0 / GATE_SCALE)
                        done.then_inc(gate_ready, 1)
                    act.wait_ge(cell_ready, n_u + 1)
                    A.activation(tc[:, k, :], cell[:, k, :], ACT.Tanh).then_inc(tc_ready, 1)
                    act.wait_ge(hidden_ready, n_u + 1)
                    if not is_first(e, s):
                        act.wait_ge(z_ready, n_s)
                    A.activation(hp[:, k, HI, :], hid[:, k, :], ACT.Copy).then_inc(hidden_hi, 1)

            def extra(e, parity):
                if not (isinstance(e, int) and e == EXPERTS - 1):
                    split_high(act, e + 1, 1 - parity)
                    take_bias(e + 1, 1 - parity)

            schedule(act, step, extra=extra)

        @block.vector
        def _(dve):
            V = nc.vector

            def split_low(e, parity):
                dve.wait_ge(hi_weights, e * 3 + 3)
                for at, width, scale in ((0, GD, WI_SCALE), (GD, GD, WH_SCALE), (2 * GD, D, WO_SCALE)):
                    last = V.scalar_tensor_tensor(wp[:, parity, LO, at:at + width], raw[:, parity, at:at + width], scale,
                                                  wp[:, parity, HI, at:at + width], ALU.mult, ALU.subtract)
                last.then_inc(weights_ready, 1)

            split_low(0, 0)

            def step(e, parity, s, p):
                n_s = e * STEPS + s
                first_step = at_start(e, s)
                for k in range(2):
                    n_u = n_s * 2 + k
                    g = lambda gate: gates[:, k, gate, :]
                    dve.wait_ge(gate_ready, n_u * GATES + 2)
                    if first_step:
                        V.tensor_tensor(cell[:, k, :], g(IN), g(CELL), ALU.mult).then_inc(cell_ready, 1)
                    else:
                        V.tensor_tensor(g(IN), g(IN), g(CELL), ALU.mult).then_inc(own_sem, 1)
                        dve.wait_ge(gate_ready, n_u * GATES + 3)
                        V.tensor_tensor(cell[:, k, :], g(FORGET), cell[:, k, :], ALU.mult).then_inc(own_sem, 1)
                        dve.wait_ge(own_sem, e * (STEPS - 1) * 4 + s * 4 + (2 * k - 2))
                        V.tensor_tensor(cell[:, k, :], cell[:, k, :], g(IN), ALU.add).then_inc(cell_ready, 1)
                    dve.wait_ge(gate_ready, n_u * GATES + 4)
                    dve.wait_ge(tc_ready, n_u + 1)
                    V.scalar_tensor_tensor(hid[:, k, :], g(OUT), H_SCALE, tc[:, k, :], ALU.mult, ALU.mult).then_inc(hidden_ready, 1)
                    dve.wait_ge(hidden_hi, n_u + 1)
                    V.tensor_tensor(hp[:, k, LO, :], hid[:, k, :], hp[:, k, HI, :], ALU.subtract).then_inc(hidden_lo, 1)
                m1 = mask[:, p, 1, :].rearrange("p (a n) -> p a n", a=1).broadcast_to([P, PARTS, WIDTH])
                zs = z[:, parity, bass.ds(s, 1), :, :].rearrange("p a h n -> p (a h) n")
                dve.wait_ge(hidden_lo, n_s * 2 + 2)
                V.tensor_tensor(z1[:, :, :], hp[:, 1, :, :], m1, ALU.mult).then_inc(z1_ready, 1)
                dve.wait_ge(z1_ready, n_s + 1)
                dve.wait_ge(z0_ready, n_s + 1)
                V.tensor_tensor(zs, zs, z1[:, :, :], ALU.add).then_inc(z_ready, 1)

            def extra(e, parity):
                if not (isinstance(e, int) and e == EXPERTS - 1):
                    split_low(e + 1, 1 - parity)

            def finish(e, parity):
                with dve.Fori(0, STEPS) as q:
                    dve.wait_ge(wo_psum, e * STEPS + q + 1)
                    for c in range(CHUNKS):
                        tile = q * CHUNKS + c
                        here = H[:, bass.ds(tile, 1), :].rearrange("p a d -> p (a d)")
                        last = V.scalar_tensor_tensor(
                            here, ps[:, bass.ds(q, 1), c * P:(c + 1) * P].rearrange("p a n -> p (a n)"),
                            combine[:, bass.ds(tile, 1), bass.ds(e, 1)].rearrange("p a b -> p (a b)"), here, ALU.mult, ALU.add)
                    last.then_inc(wo_added, 1)

            schedule(dve, step, finish=finish, extra=extra)


HEADS, HEAD = 8, 64
INNER = HEADS * HEAD
PAIRS = HEADS // 2
QK_SCALE = 2.0 ** 8
V_SCALE = 2.0 ** 8
ATT_WO_SCALE = 2.0 ** 6
SHIFT = 256.0
STEPS_A = HEADS * CHUNKS


def background_tasks():
    tasks = [[] for _ in range(STEPS_A)]
    for c in range(CHUNKS):
        tasks[c].append(("split", c))
        tasks[8 + c].append(("v", c))
        tasks[8 + c].append(("turn", c))
    for t in range(2 * PAIRS):
        tasks[t].append(("qk", t))
    tasks[13].append(("out", 0))
    for j in range(STEPS_A):
        tasks[12 + j // 2].append(("max", j))
    tasks[29].append(("shift", 0))
    return tasks


def attention(nc, H, XT, ident16, d):
    with ExitStack() as ctx:
        m = Memory(nc, "att", ctx)
        raw = m.sbuf("weights", [P, 3 * INNER + CHUNKS * D])
        wp = m.sbuf("weight_parts", [P, PARTS, 3 * INNER + CHUNKS * D], F16)
        b_out = m.sbuf("b_out", [P, D])
        qk = m.sbuf("qk", [P, 2, PARTS, 2 * PAIRS, SEQ], F16)
        QS = m.sbuf("q_twice", [P, 2, HEADS, SEQ], F16)
        Q2 = m.sbuf("q_lo_shift", [P, 2, HEADS, SEQ], F16)
        KS = m.sbuf("k_parts", [P, 2, HEADS, SEQ], F16)
        K2 = m.sbuf("k_hi_ones", [P, 2, HEADS, SEQ], F16)
        V1 = m.sbuf("v_ones", [P, 2, CHUNKS, HEADS, HEAD + 1])
        prob = m.sbuf("prob", [P, 4, SEQ])
        mx = m.sbuf("max", [P, STEPS_A])
        nm = m.sbuf("shift", [P, STEPS_A], F16)
        nmT = m.sbuf("shiftT", [STEPS_A, 2, P], F16)
        rec = m.sbuf("reciprocal", [P, 2, CHUNKS])
        O = m.sbuf("o", [P, 2, CHUNKS, INNER])
        op = m.sbuf("o_parts", [P, PARTS, CHUNKS, INNER], F16)
        OT = m.sbuf("oT", [P, CHUNKS, PARTS, CHUNKS, P], F16)
        psS = m.psum("psS", [P, 2, SEQ])
        psV = m.psum("psV", [P, 2, SEQ])
        psM = m.psum("psM", [P, 2, SEQ])
        psT = m.psum("psT", [P, PARTS, CHUNKS, P], F16)
        psX = m.psum("psX", [P, SEQ])
        weights_in, consts_in, bias_added, v_ones = (m.sem(n) for n in ("weights_in", "consts_in", "bias_added", "v_ones"))
        placed = [m.sem(f"placed{p}") for p in range(2)]
        shift_in = [m.sem(f"shift_in{p}") for p in range(2)]
        (weights_hi, weights_ready, ones_ready, qk_full, qk_hi, qk_lo, v_full, v_ready, max_full, max_done, shift_ready,
         shift_turned, shiftT_ready, s_full, p_ready, av_done, rec_ready, o_ready, o_hi, o_lo, turn_full, turn_done,
         out_full, out_done) = (m.sem(n) for n in (
             "weights_hi", "weights_ready", "ones_ready", "qk_full", "qk_hi", "qk_lo", "v_full", "v_ready", "max_full", "max_done",
             "shift_ready", "shift_turned", "shiftT_ready", "s_full", "p_ready", "av_done", "rec_ready", "o_ready", "o_hi",
             "o_lo", "turn_full", "turn_done", "out_full", "out_done"))
        block = ctx.enter_context(nc.Block())
        TASKS = background_tasks()
        AHEAD, BEHIND = ("qk", "v", "max", "shift"), ("split", "turn", "out")

        def schedule(engine, task, start, step):
            def sequence(b, parity, ahead, behind):
                start(b, parity)
                for n in range(STEPS_A):
                    for kind, j in TASKS[n]:
                        if kind in AHEAD and ahead:
                            task(kind, j, b + 1, 1 - parity)
                        if kind in BEHIND and behind:
                            task(kind, j, b - 1, 1 - parity)
                    step(b, parity, n)

            def alone(kinds, b, parity):
                for n in range(STEPS_A):
                    for kind, j in TASKS[n]:
                        if kind in kinds:
                            task(kind, j, b, parity)

            alone(AHEAD, 0, 0)
            sequence(0, 0, True, False)
            with engine.Fori(0, SEQS // 2 - 1) as i:
                for n in (1, 2):
                    sequence(i * 2 + n, n % 2, True, True)
            sequence(SEQS - 1, 1, False, True)
            alone(BEHIND, SEQS - 1, 1)

        nothing = lambda *a: None
        known = lambda b, least: isinstance(b, int) and b < least

        @block.sync
        def _(sp):
            for n, name in enumerate(("w_q", "w_k", "w_v")):
                sp.dma_start(raw[:, n * INNER:(n + 1) * INNER], d[name]).then_inc(weights_in, 16)
            sp.dma_start(raw[:, 3 * INNER:].rearrange("p (c d) -> p c d", d=D), d["w_out"].rearrange("(c p) d -> p c d", p=P)).then_inc(weights_in, 16)
            sp.dma_start(b_out[:, :], d["b_out"]).then_inc(consts_in, 16)

            def task(kind, j, b, p):
                if kind == "qk" and j == 2 * PAIRS - 1:
                    sp.wait_ge(qk_lo, (b + 1) * 2 * PAIRS)
                    if not known(b, 2):
                        sp.wait_ge(s_full, (b - 1) * STEPS_A)
                    for odd in range(2):
                        rows = slice(HEAD * odd, HEAD * (odd + 1))
                        top, low = slice(0, HEAD), slice(HEAD, P)
                        for to, there, part, first in ((KS, top, HI, PAIRS), (QS, top, HI, 0), (QS, low, HI, 0), (KS, low, LO, PAIRS),
                                                       (K2, top, HI, PAIRS), (Q2, top, LO, 0)):
                            heads = to[there, p, :, :].rearrange("r (c o) n -> r c o n", o=2)[:, :, odd, :]
                            sp.dma_start(heads, qk[rows, p, part, first:first + PAIRS, :]).then_inc(placed[p], 16)
                if kind == "shift":
                    sp.wait_ge(shiftT_ready, b + 1)
                    sp.dma_start(Q2[HEAD:HEAD + 1, p, :, :].rearrange("a h (c q) -> a (h c) q", q=P), nmT[:, p, :]).then_inc(shift_in[p], 16)

            schedule(sp, task, nothing, nothing)

        @block.tensor
        def _(pe):
            T = nc.tensor

            def score(b, p, n):
                h, c = n // CHUNKS, n % CHUNKS
                if not known(b * STEPS_A + n, 2):
                    pe.wait_ge(p_ready, b * STEPS_A + n - 1)
                keys = slice(c * P, (c + 1) * P)
                T.matmul(psS[:, n % 2, :], KS[:, p, h, keys], QS[:, p, h, :], start=True, stop=False)
                T.matmul(psS[:, n % 2, :], K2[0:HEAD + 1, p, h, keys], Q2[0:HEAD + 1, p, h, :], start=False, stop=True).then_inc(s_full, 1)

            def task(kind, j, b, p):
                x = lambda part, c: XT[:, bass.ds(b, 1), part, c].rearrange("p a n -> p (a n)")
                if kind == "qk":
                    if j >= 2:
                        pe.wait_ge(qk_lo, b * 2 * PAIRS + j - 1)
                    elif not known(b, 1):
                        pe.wait_ge(max_done, b * STEPS_A)
                    split_products(T, psM[:, j % 2, :], lambda part: wp[:, part, j * P:(j + 1) * P], lambda part: x(part, slice(0, SEQ)),
                                   True, True).then_inc(qk_full, 1)
                if kind == "v":
                    if j >= 2:
                        pe.wait_ge(v_ready, b * CHUNKS + j - 1)
                    else:
                        pe.wait_ge(qk_lo, b * 2 * PAIRS + 2 * PAIRS - 1 + j)
                    split_products(T, psM[:, j % 2, :], lambda part: x(part, slice(j * P, (j + 1) * P)),
                                   lambda part: wp[:, part, 2 * INNER:3 * INNER], True, True).then_inc(v_full, 1)
                if kind == "max":
                    if j == 0:
                        pe.wait_ge(placed[p], (b - p) * 96 + 192)
                    if j >= 2:
                        pe.wait_ge(max_done, b * STEPS_A + j - 1)
                    else:
                        pe.wait_ge(v_ready, b * CHUNKS + CHUNKS - 1 + j)
                    h, c = j // CHUNKS, j % CHUNKS
                    T.matmul(psM[:, j % 2, :], QS[:, p, h, c * P:(c + 1) * P], KS[:, p, h, :], start=True, stop=True).then_inc(max_full, 1)
                if kind == "shift":
                    pe.wait_ge(shift_ready, b + 1)
                    if not known(b, 2):
                        pe.wait_ge(out_done, b - 1)
                    T.transpose(psX[:, 0:P // 2].bitcast(F16)[0:STEPS_A, :], nm[:, :], ident16[:, :]).then_inc(shift_turned, 1)
                if kind == "turn":
                    pe.wait_ge(o_lo, b * CHUNKS + j + 1)
                    if not (known(b, 1) and j == 0):
                        pe.wait_ge(turn_done, b * CHUNKS + j)
                    for part in range(PARTS):
                        for i in range(CHUNKS):
                            last = T.transpose(psT[:, part, i, :], op[:, part, j, i * P:(i + 1) * P], ident16[:, :])
                    last.then_inc(turn_full, 1)
                if kind == "out":
                    pe.wait_ge(turn_done, (b + 1) * CHUNKS)
                    pe.wait_ge(shiftT_ready, b + 2 if not (isinstance(b, int) and b >= SEQS - 2) else SEQS)
                    if not known(b, 1):
                        pe.wait_ge(out_done, b)
                    for c in range(CHUNKS):
                        for i in range(CHUNKS):
                            last = split_products(T, psX[:, c * D:(c + 1) * D], lambda part: OT[:, c, part, i, :],
                                                  lambda part: wp[:, part, 3 * INNER + i * D:3 * INNER + (i + 1) * D],
                                                  i == 0, i == CHUNKS - 1)
                    last.then_inc(out_full, 1)

            def start(b, p):
                pe.wait_ge(shift_in[p], (b - p) * 8 + 16)
                score(b, p, 0)
                score(b, p, 1)

            def step(b, p, n):
                h, c = n // CHUNKS, n % CHUNKS
                if n + 2 < STEPS_A:
                    score(b, p, n + 2)
                else:
                    pe.wait_ge(p_ready, b * STEPS_A + n + 1)
                if c == 0 and not known(b * HEADS + h, 2):
                    pe.wait_ge(o_ready, b * HEADS + h - 1)
                for i in range(CHUNKS):
                    last = T.matmul(psV[:, h % 2, i * (HEAD + 1):(i + 1) * (HEAD + 1)], prob[:, n % 4, i * P:(i + 1) * P],
                                    V1[:, p, c, h, :], start=(c == 0 and i == 0), stop=(c == CHUNKS - 1), skip_group_check=True)
                last.then_inc(av_done, 1)

            pe.wait_ge(weights_ready, 1)
            pe.wait_ge(ones_ready, 2)
            pe.wait_ge(v_ones, 1)
            schedule(pe, task, start, step)

        @block.scalar
        def _(act):
            A = nc.scalar
            act.wait_ge(weights_in, 64)
            A.activation(wp[:, HI, 0:3 * INNER], raw[:, 0:3 * INNER], ACT.Copy, scale=QK_SCALE).then_inc(weights_hi, 1)
            A.activation(wp[:, HI, 3 * INNER:], raw[:, 3 * INNER:], ACT.Copy, scale=ATT_WO_SCALE).then_inc(weights_hi, 1)
            A.preload_act_table(ACT.Exp)

            def task(kind, j, b, p):
                if kind == "qk":
                    act.wait_ge(qk_full, b * 2 * PAIRS + j + 1)
                    if j == 0 and not known(b, 2):
                        act.wait_ge(placed[p], (b - p) * 96)
                    A.activation(qk[:, p, HI, j, :], psM[:, j % 2, :], ACT.Copy, scale=1.0 / (X_SCALE * QK_SCALE)).then_inc(qk_hi, 1)
                if kind == "v":
                    act.wait_ge(v_full, b * CHUNKS + j + 1)
                    A.activation(V1[:, p, j, :, 0:HEAD], psM[:, j % 2, :].rearrange("p (h e) -> p h e", e=HEAD), ACT.Copy,
                                 scale=V_SCALE / (X_SCALE * QK_SCALE)).then_inc(v_ready, 1)
                if kind == "split":
                    act.wait_ge(o_ready, (b + 1) * HEADS)
                    if not known(b, 1):
                        act.wait_ge(turn_full, b * CHUNKS)
                    A.activation(op[:, HI, j, :], O[:, p, j, :], ACT.Copy).then_inc(o_hi, 1)
                if kind == "turn":
                    act.wait_ge(turn_full, b * CHUNKS + j + 1)
                    if not known(b, 1):
                        act.wait_ge(out_full, b)
                    A.activation(OT[:, j, :, :, :], psT[:, :, :, :], ACT.Copy).then_inc(turn_done, 1)

            def step(b, p, n):
                act.wait_ge(s_full, b * STEPS_A + n + 1)
                if not known(b * STEPS_A + n, 4):
                    act.wait_ge(av_done, b * STEPS_A + n - 3)
                A.activation(prob[:, n % 4, :], psS[:, n % 2, :], ACT.Exp, scale=HEAD ** -0.5).then_inc(p_ready, 1)

            schedule(act, task, nothing, step)

        @block.gpsimd
        def _(pool):
            for p in range(2):
                nc.gpsimd.memset(K2[HEAD:HEAD + 1, p, :, :], SHIFT).then_inc(ones_ready, 1)

        @block.vector
        def _(dve):
            V = nc.vector
            V.memset(V1[:, :, :, :, HEAD:], 1.0).then_inc(v_ones, 1)
            dve.wait_ge(weights_hi, 2)
            for at, width, scale in ((0, 3 * INNER, QK_SCALE), (3 * INNER, CHUNKS * D, ATT_WO_SCALE)):
                last = V.scalar_tensor_tensor(wp[:, LO, at:at + width], raw[:, at:at + width], scale, wp[:, HI, at:at + width],
                                              ALU.mult, ALU.subtract)
            last.then_inc(weights_ready, 1)
            dve.wait_ge(consts_in, 16)
            b_b = b_out[:, :].rearrange("p (a d) -> p a d", a=1).broadcast_to([P, TILES, D])
            V.tensor_tensor(H[:, :, :], H[:, :, :], b_b, ALU.add).then_inc(bias_added, 1)
            dve.wait_ge(bias_added, 1)

            def task(kind, j, b, p):
                if kind == "qk":
                    dve.wait_ge(qk_hi, b * 2 * PAIRS + j + 1)
                    V.scalar_tensor_tensor(qk[:, p, LO, j, :], psM[:, j % 2, :], 1.0 / (X_SCALE * QK_SCALE), qk[:, p, HI, j, :],
                                           ALU.mult, ALU.subtract).then_inc(qk_lo, 1)
                if kind == "max":
                    dve.wait_ge(max_full, b * STEPS_A + j + 1)
                    V.tensor_reduce(mx[:, j:j + 1], psM[:, j % 2, :], AX.X, ALU.max).then_inc(max_done, 1)
                if kind == "shift":
                    dve.wait_ge(max_done, (b + 1) * STEPS_A)
                    V.tensor_scalar(nm[:, :], mx[:, :], -1.0 / SHIFT, None, ALU.mult).then_inc(shift_ready, 1)
                    dve.wait_ge(shift_turned, b + 1)
                    if not known(b, 2):
                        dve.wait_ge(shift_in[p], (b - p) * 8)
                    V.tensor_copy(nmT[:, p, :], psX[:, 0:P // 2].bitcast(F16)[0:STEPS_A, :]).then_inc(shiftT_ready, 1)
                if kind == "split":
                    dve.wait_ge(o_hi, b * CHUNKS + j + 1)
                    V.tensor_tensor(op[:, LO, j, :], O[:, p, j, :], op[:, HI, j, :], ALU.subtract).then_inc(o_lo, 1)
                if kind == "out":
                    dve.wait_ge(out_full, b + 1)
                    here = H[:, bass.ds(b * CHUNKS, CHUNKS), :].rearrange("p c d -> p (c d)")
                    V.scalar_tensor_tensor(here, psX[:, :], 1.0 / (V_SCALE * ATT_WO_SCALE), here, ALU.mult, ALU.add).then_inc(out_done, 1)

            def step(b, p, n):
                h, c = n // CHUNKS, n % CHUNKS
                if c == CHUNKS - 1:
                    dve.wait_ge(av_done, b * STEPS_A + n + 1)
                    if h == 0 and not known(b, 2):
                        dve.wait_ge(o_lo, (b - 1) * CHUNKS)
                    sums = psV[:, h % 2, 0:CHUNKS * (HEAD + 1)].rearrange("p (c e) -> p c e", e=HEAD + 1)
                    if not known(b * HEADS + h, 2):
                        dve.wait_ge(o_ready, b * HEADS + h - 1)
                    V.reciprocal(rec[:, h % 2, :], sums[:, :, HEAD]).then_inc(rec_ready, 1)
                    dve.wait_ge(rec_ready, b * HEADS + h + 1)
                    V.tensor_tensor(O[:, p, :, h * HEAD:(h + 1) * HEAD], sums[:, :, 0:HEAD],
                                    rec[:, h % 2, :].rearrange("p (c a) -> p c a", a=1).broadcast_to([P, CHUNKS, HEAD]), ALU.mult).then_inc(o_ready, 1)

            schedule(dve, task, nothing, step)


GATE_HIDDEN = D // 2
EXPERT_HIDDEN = 2 * D
BLOCKS = EXPERT_HIDDEN // P
W1_SCALE = 2.0 ** 8
G_SCALE = 2.0 ** 6
W2_SCALE = 2.0 ** 8


def route_gated(nc, H, XT, ident, d, combine):
    COLS = 32
    with ExitStack() as ctx:
        m = Memory(nc, "gate", ctx)
        gw1 = m.sbuf("gw1", [P, GATE_HIDDEN])
        gwp = m.sbuf("gw1_parts", [P, PARTS, GATE_HIDDEN], F16)
        gb1 = m.sbuf("gb1", [GATE_HIDDEN, 1])
        gw2 = m.sbuf("gw2", [GATE_HIDDEN, EXPERTS])
        gb2 = m.sbuf("gb2", [P, EXPERTS])
        rank = m.sbuf("rank", [P, EXPERTS])
        bias_blocks = m.sbuf("bias_blocks", [P, CHUNKS * D])
        hidden = m.sbuf("hidden", [GATE_HIDDEN, 2, SEQ])
        scores = m.sbuf("scores", [P, TILES, EXPERTS])
        first = m.sbuf("first", [P, TILES, EXPERTS])
        second = m.sbuf("second", [P, TILES, EXPERTS])
        per_token = m.sbuf("per_token", [P, 5, TILES])
        m1, m2, e, r1, work = (per_token[:, n, :] for n in range(5))
        record = m.sbuf("record", [P, TILES, COLS])
        rows = m.sbuf("rows", [P, SEQS, P])
        psG = m.psum("psG", [P, 2, SEQ])
        psL = m.psum("psL", [P, 512])
        psR = m.psum("psR", [P, SEQS, P])
        psB = m.psum("psB", [P, 2, CHUNKS * D])
        (params_in, w_hi, w_parts, cleared, bias_in, hidden_psum, hidden_ready, logits_psum, own_sem, shifted, exped, gap_ready,
         exp_ready, record_ready, rows_psum, rows_ready, bias_psum, bias_added) = (m.sem(n) for n in (
             "params_in", "w_hi", "w_parts", "cleared", "bias_in", "hidden_psum", "hidden_ready", "logits_psum", "own", "shifted",
             "exped", "gap_ready", "exp_ready", "record_ready", "rows_psum", "rows_ready", "bias_psum", "bias_added"))
        block = ctx.enter_context(nc.Block())

        @block.sync
        def _(sp):
            for to, name in ((gw1, "gw1"), (gb1, "gb1"), (gw2, "gw2"), (gb2, "gb2"), (rank, "rank")):
                sp.dma_start(to[:, :], d[name]).then_inc(params_in, 16)
            load_bias_blocks(sp, bias_blocks, d["be2"], cleared, bias_in)

        @block.scalar
        def _(act):
            A = nc.scalar
            act.wait_ge(params_in, 80)
            A.activation(gwp[:, HI, :], gw1[:, :], ACT.Copy, scale=W_SCALE_ROUTER).then_inc(w_hi, 1)

            def relu(b, p, first_use):
                act.wait_ge(hidden_psum, b + 1)
                if not first_use:
                    act.wait_ge(logits_psum, b - 1)
                A.activation(hidden[:, p, :], psG[0:GATE_HIDDEN, p, :], ACT.Relu, bias=gb1[:, 0:1],
                             scale=1.0 / (X_SCALE * W_SCALE_ROUTER)).then_inc(hidden_ready, 1)

            relu(0, 0, True)
            relu(1, 1, True)
            with act.Fori(1, SEQS // 2) as i:
                for p in range(2):
                    relu(i * 2 + p, p, False)
            act.wait_ge(shifted, 1)
            A.activation(first[:, :, :], scores[:, :, :], ACT.Exp).then_inc(exped, 1)
            act.wait_ge(gap_ready, 1)
            A.activation(e[:, :], e[:, :], ACT.Exp).then_inc(exp_ready, 1)
            act.wait_ge(rows_psum, 1)
            A.activation(rows[:, :, :], psR[:, :, :], ACT.Copy).then_inc(rows_ready, 1)

        @block.tensor
        def _(pe):
            pe.wait_ge(w_parts, 1)

            def hidden_product(b, p):
                split_products(nc.tensor, psG[0:GATE_HIDDEN, p, :], lambda part: gwp[:, part, :],
                               lambda part: XT[:, bass.ds(b, 1), part, :].rearrange("p a n -> p (a n)"), True, True).then_inc(hidden_psum, 1)

            def logits_product(b, p):
                pe.wait_ge(hidden_ready, b + 1)
                for c in range(CHUNKS):
                    last = nc.tensor.matmul(psL[:, bass.ds((b * CHUNKS + c) * EXPERTS, EXPERTS)],
                                            hidden[:, p, c * P:(c + 1) * P], gw2[:, :], start=True, stop=True)
                last.then_inc(logits_psum, 1)

            hidden_product(0, 0)
            hidden_product(1, 1)
            with pe.Fori(0, SEQS // 2 - 1) as i:
                for p in range(2):
                    logits_product(i * 2 + p, p)
                    hidden_product(i * 2 + p + 2, p)
            logits_product(SEQS - 2, 0)
            logits_product(SEQS - 1, 1)
            pe.wait_ge(record_ready, 1)
            for b in range(SEQS):
                last = nc.tensor.transpose(psR[:, b, :], record[:, b * CHUNKS:(b + 1) * CHUNKS, :].rearrange("p c j -> p (c j)"), ident[:, :])
            last.then_inc(rows_psum, 1)
            pe.wait_ge(rows_ready, 1)
            pe.wait_ge(bias_in, 16 * CHUNKS)
            for b in range(SEQS):
                if b >= 2:
                    pe.wait_ge(bias_added, b - 1)
                nc.tensor.matmul(psB[:, b % 2, :], rows[:, b, :], bias_blocks[:, :], start=True, stop=True).then_inc(bias_psum, 1)

        @block.vector
        def _(dve):
            V = nc.vector
            own = Chain(dve, own_sem)
            V.memset(bias_blocks[:, :], 0.0).then_inc(cleared, 1)
            own(V.memset(record[:, :, EXPERTS:], 0.0))
            dve.wait_ge(params_in, 80)
            dve.wait_ge(w_hi, 1)
            V.scalar_tensor_tensor(gwp[:, LO, :], gw1[:, :], W_SCALE_ROUTER, gwp[:, HI, :], ALU.mult, ALU.subtract).then_inc(w_parts, 1)
            dve.wait_ge(logits_psum, SEQS)
            gb2_b = gb2[:, :].rearrange("p (a e) -> p a e", a=1).broadcast_to([P, TILES, EXPERTS])
            wide = lambda x: x.rearrange("p (t a) -> p t a", a=1).broadcast_to([P, TILES, EXPERTS])
            own.link(V.tensor_tensor(scores[:, :, :], psL[:, 0:TILES * EXPERTS].rearrange("p (t e) -> p t e", e=EXPERTS), gb2_b, ALU.add))
            own.link(V.tensor_reduce(m1[:, :], scores[:, :, :], AX.X, ALU.max))
            V.tensor_tensor(scores[:, :, :], scores[:, :, :], wide(m1[:, :]), ALU.subtract).then_inc(shifted, 1)
            dve.wait_ge(exped, 1)
            own.link(V.tensor_reduce(work[:, :], first[:, :, :], AX.X, ALU.add))
            own.link(V.reciprocal(work[:, :], work[:, :]))
            own.link(V.tensor_tensor(scores[:, :, :], first[:, :, :], wide(work[:, :]), ALU.mult))
            top_two(V, own, scores[:, :, :], rank[:, :], first[:, :, :], second[:, :, :], m1[:, :], m2[:, :], work[:, :])
            V.tensor_tensor(e[:, :], m2[:, :], m1[:, :], ALU.subtract).then_inc(gap_ready, 1)
            dve.wait_ge(exp_ready, 1)
            own.link(V.tensor_scalar(r1[:, :], e[:, :], 1.0, None, ALU.add))
            own.link(V.reciprocal(r1[:, :], r1[:, :]))
            own(V.tensor_tensor(e[:, :], e[:, :], r1[:, :], ALU.mult))
            own.link(V.tensor_tensor(first[:, :, :], first[:, :, :], wide(r1[:, :]), ALU.mult))
            own.link(V.tensor_tensor(second[:, :, :], second[:, :, :], wide(e[:, :]), ALU.mult))
            own.link(V.tensor_tensor(record[:, :, 0:EXPERTS], first[:, :, :], second[:, :, :], ALU.add))
            V.tensor_scalar(combine[:, :, :], record[:, :, 0:EXPERTS], 1.0 / (G_SCALE * W2_SCALE), None, ALU.mult).then_inc(record_ready, 1)
            for b in range(SEQS):
                dve.wait_ge(bias_psum, b + 1)
                here = H[:, b * CHUNKS:(b + 1) * CHUNKS, :].rearrange("p c d -> p (c d)")
                V.tensor_tensor(here, psB[:, b % 2, :], here, ALU.add).then_inc(bias_added, 1)


def gated_experts(nc, H, XT, d, combine):
    BW = BLOCKS * D
    with ExitStack() as ctx:
        m = Memory(nc, "ffn", ctx)
        raw1 = m.sbuf("w1", [P, EXPERTS, BW])
        raw2 = m.sbuf("w2", [P, EXPERTS, BLOCKS, D])
        w1 = m.sbuf("w1_parts", [P, PARTS, EXPERTS, BW], F16)
        w2 = m.sbuf("w2_parts", [P, PARTS, EXPERTS, BW], F16)
        b1 = m.sbuf("b1", [P, EXPERTS * BLOCKS])
        act_out = m.sbuf("gelu", [P, 2, BLOCKS, SEQ])
        gp = m.sbuf("gelu_parts", [P, 2, PARTS, BLOCKS, SEQ], F16)
        psH = m.psum("psH", [P, 2, BLOCKS, SEQ])
        psY = m.psum("psY", [P, 2, CHUNKS * D])
        weights_in = [m.sem(f"weights_in{e}") for e in range(EXPERTS)]
        bias_in = m.sem("bias_in")
        hi_weights, weights_ready, h_psum, gelu_ready, hi_ready, lo_ready, y_psum, y_added = (m.sem(n) for n in (
            "hi_weights", "weights_ready", "h_psum", "gelu_ready", "hi_ready", "lo_ready", "y_psum", "y_added"))
        block = ctx.enter_context(nc.Block())
        known = lambda u, least: isinstance(u, int) and u < least

        @block.sync
        def _(sp):
            sp.dma_start(b1[:, :], d["be1"]).then_inc(bias_in, 16)
            for e in range(EXPERTS):
                sp.dma_start(raw1[:, e, :], d["we1"][e * P:(e + 1) * P, :]).then_inc(weights_in[e], 16)
                sp.dma_start(raw2[:, e, :, :], d["we2"][e * EXPERT_HIDDEN:(e + 1) * EXPERT_HIDDEN, :].rearrange("(j p) d -> p j d", p=P)).then_inc(weights_in[e], 16)

        @block.tensor
        def _(pe):
            def up(b, e):
                if known(b, 1):
                    pe.wait_ge(weights_ready, e + 1)
                if not known(b * EXPERTS + e, 2):
                    pe.wait_ge(gelu_ready, (b * EXPERTS + e - 1) * BLOCKS)
                for j in range(BLOCKS):
                    split_products(nc.tensor, psH[:, e % 2, j, :], lambda part: w1[:, part, e, j * P:(j + 1) * P],
                                   lambda part: XT[:, bass.ds(b, 1), part, :].rearrange("p a n -> p (a n)"), True, True).then_inc(h_psum, 1)

            def down(b, e):
                u = b * EXPERTS + e
                pe.wait_ge(lo_ready, u + 1)
                if not known(u, 2):
                    pe.wait_ge(y_added, u - 1)
                for c in range(CHUNKS):
                    for j in range(BLOCKS):
                        last = split_products(nc.tensor, psY[:, e % 2, c * D:(c + 1) * D], lambda part: gp[:, e % 2, part, j, c * P:(c + 1) * P],
                                              lambda part: w2[:, part, e, j * D:(j + 1) * D], j == 0, j == BLOCKS - 1)
                last.then_inc(y_psum, 1)

            def sequence(b, last):
                for e in range(EXPERTS):
                    if e + 2 < EXPERTS:
                        up(b, e + 2)
                    elif not last:
                        up(b + 1, e + 2 - EXPERTS)
                    down(b, e)

            up(0, 0)
            up(0, 1)
            sequence(0, False)
            with pe.Fori(1, SEQS - 1) as b:
                sequence(b, False)
            sequence(SEQS - 1, True)

        @block.scalar
        def _(act):
            A = nc.scalar
            A.preload_act_table(ACT.Gelu)
            for e in range(EXPERTS):
                act.wait_ge(weights_in[e], 32)
                A.activation(w1[:, HI, e, :], raw1[:, e, :], ACT.Copy, scale=W1_SCALE).then_inc(hi_weights, 1)
                A.activation(w2[:, HI, e, :], raw2[:, e, :, :].rearrange("p j d -> p (j d)"), ACT.Copy, scale=W2_SCALE).then_inc(hi_weights, 1)
            act.wait_ge(bias_in, 16)

            def sequence(b):
                for e in range(EXPERTS):
                    u = b * EXPERTS + e
                    if not known(u, 2):
                        act.wait_ge(lo_ready, u - 1)
                    for j in range(BLOCKS):
                        act.wait_ge(h_psum, u * BLOCKS + j + 1)
                        A.activation(act_out[:, e % 2, j, :], psH[:, e % 2, j, :], ACT.Gelu, bias=b1[:, e * BLOCKS + j:e * BLOCKS + j + 1],
                                     scale=1.0 / (X_SCALE * W1_SCALE)).then_inc(gelu_ready, 1)
                    act.wait_ge(gelu_ready, (u + 1) * BLOCKS)
                    if not known(u, 2):
                        act.wait_ge(y_psum, u - 1)
                    A.activation(gp[:, e % 2, HI, :, :], act_out[:, e % 2, :, :], ACT.Copy, scale=G_SCALE).then_inc(hi_ready, 1)

            sequence(0)
            with act.Fori(1, SEQS) as b:
                sequence(b)

        @block.vector
        def _(dve):
            V = nc.vector
            for e in range(EXPERTS):
                dve.wait_ge(hi_weights, 2 * (e + 1))
                V.scalar_tensor_tensor(w1[:, LO, e, :], raw1[:, e, :], W1_SCALE, w1[:, HI, e, :], ALU.mult, ALU.subtract)
                V.scalar_tensor_tensor(w2[:, LO, e, :], raw2[:, e, :, :].rearrange("p j d -> p (j d)"), W2_SCALE, w2[:, HI, e, :],
                                       ALU.mult, ALU.subtract).then_inc(weights_ready, 1)

            def low(b, e):
                dve.wait_ge(hi_ready, b * EXPERTS + e + 1)
                V.scalar_tensor_tensor(gp[:, e % 2, LO, :, :], act_out[:, e % 2, :, :], G_SCALE, gp[:, e % 2, HI, :, :],
                                       ALU.mult, ALU.subtract).then_inc(lo_ready, 1)

            def add(b, e):
                u = b * EXPERTS + e
                dve.wait_ge(y_psum, u + 1)
                if not known(u, 1):
                    dve.wait_ge(y_added, u)
                for c in range(CHUNKS):
                    here = H[:, bass.ds(b * CHUNKS + c, 1), :].rearrange("p a d -> p (a d)")
                    last = V.scalar_tensor_tensor(here, psY[:, e % 2, c * D:(c + 1) * D],
                                                  combine[:, bass.ds(b * CHUNKS + c, 1), e:e + 1].rearrange("p a b -> p (a b)"),
                                                  here, ALU.mult, ALU.add)
                last.then_inc(y_added, 1)

            def sequence(b, last):
                for e in range(EXPERTS):
                    if e + 1 < EXPERTS:
                        low(b, e + 1)
                    elif not last:
                        low(b + 1, 0)
                    add(b, e)

            low(0, 0)
            sequence(0, False)
            with dve.Fori(1, SEQS - 1) as b:
                sequence(b, False)
            sequence(SEQS - 1, True)


def store(nc, H, out):
    with ExitStack() as ctx:
        m = Memory(nc, "store", ctx)
        stored = m.sem("stored")
        block = ctx.enter_context(nc.Block())

        @block.sync
        def _(sp):
            sp.dma_start(out.rearrange("b (c p) d -> p (b c) d", p=P), H[:, :, :]).then_inc(stored, 16)
            sp.wait_ge(stored, 16)


def build_program(nc, d, out):
    with ExitStack() as ctx:
        m = Memory(nc, "model", ctx)
        H = m.sbuf("h", [P, TILES, D])
        ident = m.sbuf("ident", [P, P])
        ident16 = m.sbuf("ident16", [P, P], F16)
        combine = m.sbuf("combine", [P, TILES, EXPERTS])
        XT = m.sbuf("xT", [P, SEQS, PARTS, SEQ], F16)
        mask_rows = nc.dram_tensor("mask_rows", (2 * EXPERTS, SEQS * SEQ), F16).ap()
        embed_and_convolve(nc, H, ident, ident16, d)
        normalize(nc, "norm2", H, XT, ident16)
        route_recurrent(nc, H, XT, ident, d, combine, mask_rows)
        recurrent_experts(nc, H, XT, d, combine, mask_rows)
        normalize(nc, "norm3", H, XT, ident16)
        attention(nc, H, XT, ident16, d)
        normalize(nc, "norm4", H, XT, ident16)
        route_gated(nc, H, XT, ident, d, combine)
        gated_experts(nc, H, XT, d, combine)
        store(nc, H, out)


def dft_matrices():
    import numpy as np

    n, half = SEQ, SEQ // 2
    angle = 2 * np.pi * (np.outer(np.arange(n), np.arange(half)) % n) / n
    sign = (-1.0) ** np.arange(n)
    forward = np.concatenate([np.cos(angle), -np.sin(angle)], axis=1)
    forward[:, half] = sign
    inverse = 2 * forward.T / n
    inverse[[0, half]] /= 2
    return forward.astype(np.float32), np.ascontiguousarray(inverse).astype(np.float32)


def kernel(**inputs):
    import numpy as np
    import concourse.bacc as bacc
    from concourse.bass_utils import run_bass_kernel_spmd

    x = {name: np.asarray(a) for name, a in inputs.items()}
    fwd, inv = dft_matrices()
    rows = lambda a: np.ascontiguousarray(np.broadcast_to(a, (P,) + a.shape))
    positions = np.concatenate([np.arange(32), np.arange(0, SEQ, 32), [0.5]]).astype(np.float32)
    arrays = {
        "ids": np.ascontiguousarray(x["x"].reshape(TILES, P).T),
        "table": np.concatenate([x["L0_tok_fine_embed_w"], x["L0_tok_loc_to_cluster_w"].T], axis=1),
        "coarse_w": x["L0_tok_coarse_embed_w"],
        "cluster_b": rows(x["L0_tok_loc_to_cluster_b"]),
        "A_re": x["L0_attn_A_real"], "A_im": x["L0_attn_A_imag"], "B_in": x["L0_attn_B"], "C_in": x["L0_attn_C"],
        "delta": x["L0_attn_delta"].reshape(P, 1),
        "positions": rows(positions), "dft": fwd, "inverse_dft": inv, "ident": np.eye(P, dtype=np.float32),
        "ident16": np.eye(P, dtype=np.float16),
        "rank": rows(np.arange(EXPERTS, 0, -1, dtype=np.float32)),
        "w_q": x["L1_attn_w_q"], "w_k": x["L1_attn_w_k"], "w_v": x["L1_attn_w_v"], "w_out": x["L1_attn_w_out"],
        "b_out": rows(x["L1_attn_b_out"]),
        "router_w": x["L0_ffn_router_w"], "router_b": rows(x["L0_ffn_router_b"]),
        "Wi": x["L0_ffn_Wi"].reshape(EXPERTS * D, GATES * D), "Wh": x["L0_ffn_Wh"].reshape(EXPERTS * D, GATES * D),
        "Wo": x["L0_ffn_Wo"].reshape(EXPERTS * D, D), "bo": x["L0_ffn_bo"],
        "gw1": x["L1_ffn_gw1"], "gb1": x["L1_ffn_gb1"].reshape(GATE_HIDDEN, 1), "gw2": x["L1_ffn_gw2"], "gb2": rows(x["L1_ffn_gb2"]),
        "we1": x["L1_ffn_we1"].reshape(EXPERTS * D, EXPERT_HIDDEN), "we2": x["L1_ffn_we2"].reshape(EXPERTS * EXPERT_HIDDEN, D),
        "be1": np.ascontiguousarray(x["L1_ffn_be1"].reshape(EXPERTS * BLOCKS, P).T), "be2": x["L1_ffn_be2"],
        "lstm_b": np.ascontiguousarray(x["L0_ffn_b"].reshape(EXPERTS * GATES, D).T),
    }
    nc = bacc.Bacc("TRN2", target_bir_lowering=False, num_devices=1)
    d = {n: nc.dram_tensor(f"in_{n}", a.shape, mybir.dt.from_np(a.dtype), kind="ExternalInput").ap() for n, a in arrays.items()}
    out = nc.dram_tensor("out", (SEQS, SEQ, D), F32, kind="ExternalOutput").ap()
    build_program(nc, d, out)
    r = run_bass_kernel_spmd(nc, [{f"in_{n}": a for n, a in arrays.items()}], core_ids=[0])
    return r.results[0]["out"]
```

```python
from contextlib import ExitStack

import concourse.bass as bass
from concourse import mybir

P = 128
TILES, D = 32, 128
SEQS, SEQ = 8, 512
CHUNKS = SEQ // P
STATES = 16
HALF_D = D // 2
F32, F16, I32 = mybir.dt.float32, mybir.dt.float16, mybir.dt.int32
ACT, ALU, AX = mybir.ActivationFunctionType, mybir.AluOpType, mybir.AxisListType
EPS = 1e-5


class Chain:

    def __init__(self, engine, sem, base=0):
        self.engine, self.sem, self.base, self.n = engine, sem, base, 0

    def __call__(self, instruction):
        instruction.then_inc(self.sem, 1)
        self.n += 1

    def done(self, back=0):
        self.engine.wait_ge(self.sem, self.base + (self.n - back))

    def link(self, instruction):
        self(instruction)
        self.done()


class Memory:

    def __init__(self, nc, stage, ctx):
        self.nc, self.stage, self.ctx, self.sems = nc, stage, ctx, []
        ctx.callback(self.clear)

    def sbuf(self, name, shape, dtype=F32):
        return self.ctx.enter_context(self.nc.sbuf_tensor(f"{self.stage}_{name}", shape, dtype))

    def psum(self, name, shape, dtype=F32):
        return self.ctx.enter_context(self.nc.psum_tensor(f"{self.stage}_{name}", shape, dtype))

    def sem(self, name):
        self.sems.append(self.nc.alloc_semaphore(f"{self.stage}_{name}"))
        return self.sems[-1]

    def clear(self):
        if self.sems:
            self.nc.clear_and_free_semaphores(self.sems)
            self.nc.all_engine_barrier()


def token_statistics(nc, dve, chain, H, stats, mean, var, scratch):
    for t in range(TILES):
        chain(nc.vector.bn_stats(stats[:, t, :], H[:, t, :]))
    chain.done()
    chain(nc.vector.tensor_tensor(mean, stats[:, :, 1], stats[:, :, 4], ALU.add))
    chain(nc.vector.tensor_tensor(scratch, stats[:, :, 1], stats[:, :, 4], ALU.subtract))
    chain(nc.vector.tensor_tensor(var, stats[:, :, 2], stats[:, :, 5], ALU.add))
    chain.done()
    chain(nc.vector.tensor_scalar(mean, mean, 0.5, None, ALU.mult))
    chain(nc.vector.scalar_tensor_tensor(scratch, scratch, 0.25, scratch, ALU.mult, ALU.mult))
    chain.done()
    return nc.vector.scalar_tensor_tensor(var, var, 1.0 / D, scratch, ALU.mult, ALU.add)


def embed_and_convolve(nc, H, ident, ident16, d):
    NPOS = d["positions"].shape[1]
    FINE_STEP = 32
    NA, NR = SEQ // FINE_STEP, FINE_STEP
    TWO_PI = 6.283185307179586
    TWO_PI_HI = 6.28125
    ROUND = 1.5 * 2.0 ** 23
    GROUPS, GT = 4, TILES // 4
    SLOTS = 4

    with ExitStack() as ctx:
        m = Memory(nc, "conv", ctx)
        idx = m.sbuf("ids", [P, TILES], I32)
        cb = m.sbuf("cluster_b", [P, HALF_D])
        cw = m.sbuf("coarse_w", [P, D])
        fwd = m.sbuf("dft", [P, CHUNKS, SEQ])
        inv = m.sbuf("inverse_dft", [P, SLOTS, SEQ])
        par = m.sbuf("ssm_params", [P, 4, STATES])
        delta = m.sbuf("delta", [P, 1])
        pos = m.sbuf("positions", [P, NPOS])
        U = m.sbuf("u", [P, TILES, D])
        logits = m.sbuf("logits", [P, GT, HALF_D])
        top = m.sbuf("top", [P, GT])
        total = m.sbuf("total", [P, GT])
        dist = m.sbuf("dist", [P, GT, HALF_D])
        distT = m.sbuf("distT", [P, GT // 2, P])
        dtA = m.sbuf("dtA", [P, 2, STATES])
        phase = m.sbuf("phase", [P, NPOS, STATES])
        turns = m.sbuf("turns", [P, NPOS, STATES])
        sin = m.sbuf("sin", [P, NPOS, STATES])
        cos = m.sbuf("cos", [P, NPOS, STATES])
        mag = m.sbuf("mag", [P, NPOS, STATES])
        small = m.sbuf("small", [P, 16, STATES])
        fine = m.sbuf("fine", [P, NR, 2 * STATES])
        rough = m.sbuf("rough", [P, NA, 2 * STATES])
        prod = m.sbuf("prod", [P, NA // 4, NR, 2 * STATES])
        K = m.sbuf("k", [P, SEQ])
        KT = m.sbuf("kT", [P, CHUNKS, D])
        Kr = m.sbuf("k_re", [P, 2, 2, D])
        Krn = m.sbuf("k_re_nyquist", [P, 2, D])
        Ki = m.sbuf("k_im", [P, 2, 2, D])
        stats = m.sbuf("stats", [P, TILES, 6])
        mean = m.sbuf("mean", [P, TILES])
        var = m.sbuf("var", [P, TILES])
        tmp = m.sbuf("tmp", [P, TILES])
        eps = m.sbuf("eps", [P, 1])
        terms = m.sbuf("terms", [P, 12, 512])
        sums = m.sbuf("sums", [P, 4, 512])
        Y = m.sbuf("y", [P, 2, SLOTS, 2, 512])

        ps = m.psum("ps", [P, 8, 512])

        idx_in, params_in, cw_in, dft_in, inv_in, idn_in = (m.sem(n) for n in (
            "idx_in", "params_in", "cw_in", "dft_in", "inv_in", "ident_in"))
        gathered = [m.sem(f"gathered{g}") for g in range(GROUPS)]
        shifted, exped, dist_ready, turned, distT_ready, coarse_done, coarse_in_h = (m.sem(n) for n in (
            "shifted", "exped", "dist_ready", "turned", "distT_ready", "coarse_done", "coarse_in_h"))
        tanh_ready, mag_in, mag_ready, trig_in, trig_ready, k_ready, kT_psum, kT_ready, kf_psum, kf_ready = (
            m.sem(n) for n in ("tanh_ready", "mag_in", "mag_ready", "trig_in", "trig_ready", "k_ready",
                               "kT_psum", "kT_ready", "kf_psum", "kf_ready"))
        var_ready, std_ready, u_ready, eps_ready, cw_cleared = (
            m.sem(n) for n in ("var_ready", "std_ready", "u_ready", "eps_ready", "cw_cleared"))
        spectrum, terms_ready, y_ready, pool_sums, out_psum, out_done, dve_own = (m.sem(n) for n in (
            "spectrum", "terms_ready", "y_ready", "pool_sums", "out_psum", "out_done", "dve_own"))

        block = ctx.enter_context(nc.Block())

        @block.sync
        def _(sp):
            sp.dma_start(idx[:, :], d["ids"]).then_inc(idx_in, 16)
            for n, source in enumerate((d["A_re"], d["A_im"], d["B_in"], d["C_in"])):
                sp.dma_start(par[:, n, :], source).then_inc(params_in, 16)
            sp.dma_start(delta[:, :], d["delta"]).then_inc(params_in, 16)
            sp.dma_start(pos[:, :], d["positions"]).then_inc(params_in, 16)
            sp.dma_start(cb[:, :], d["cluster_b"]).then_inc(cw_in, 16)
            sp.wait_ge(cw_cleared, 1)
            for half in range(2):
                here = slice(HALF_D * half, HALF_D * (half + 1))
                sp.dma_start(cw[here, here], d["coarse_w"]).then_inc(cw_in, 16)
            sp.dma_start(ident[:, :], d["ident"]).then_inc(idn_in, 16)
            sp.dma_start(ident16[:, :], d["ident16"]).then_inc(idn_in, 16)
            sp.dma_start(fwd[:, :, :], d["dft"].rearrange("(c p) f -> p c f", p=P)).then_inc(dft_in, 16)
            sp.dma_start(inv[:, :, :], d["inverse_dft"].rearrange("(c p) l -> p c l", p=P)).then_inc(inv_in, 16)

        @block.gpsimd
        def _(pool):
            pool.wait_ge(idx_in, 16)
            for t in range(TILES):
                pool.indirect_dma_start(
                    out=H[:, t, :], out_offset=None, in_=d["table"],
                    in_offset=bass.IndirectOffsetOnAxis(ap=idx[:, t:t + 1], axis=0),
                ).then_inc(gathered[t // GT], 16)
            for u in range(4):
                half, b = u // 2, u % 2
                pool.wait_ge(terms_ready, 12 * (u + 1))
                if u >= 1:
                    pool.wait_ge(pool_sums, 8 * u)
                for n, (x, y, op) in enumerate(((4, 5, ALU.subtract), (6, 7, ALU.subtract), (8, 9, ALU.add), (10, 11, ALU.add))):
                    nc.gpsimd.tensor_tensor(sums[:, n, :], terms[:, x, :], terms[:, y, :], op).then_inc(pool_sums, 1)
                nc.gpsimd.tensor_tensor(Y[:, half, b, 0, :], terms[:, 0, :], terms[:, 1, :], ALU.subtract).then_inc(pool_sums, 1)
                nc.gpsimd.tensor_tensor(Y[:, half, 2 + b, 0, :], terms[:, 2, :], terms[:, 3, :], ALU.add).then_inc(pool_sums, 1)
                pool.wait_ge(pool_sums, 8 * u + 4)
                nc.gpsimd.tensor_tensor(Y[:, half, b, 1, :], sums[:, 0, :], sums[:, 1, :], ALU.add).then_inc(pool_sums, 1)
                nc.gpsimd.tensor_tensor(Y[:, half, 2 + b, 1, :], sums[:, 2, :], sums[:, 3, :], ALU.add).then_inc(pool_sums, 1)

        @block.scalar
        def _(act):
            act.wait_ge(mag_in, 1)
            nc.scalar.activation(small[:, 0, :], dtA[:, 0, :], ACT.Tanh, scale=0.5).then_inc(tanh_ready, 1)
            nc.scalar.activation(mag[:, :, :], mag[:, :, :], ACT.Exp).then_inc(mag_ready, 1)
            act.wait_ge(trig_in, 2)
            nc.scalar.activation(sin[:, :, :], phase[:, :, :], ACT.Sin).then_inc(trig_ready, 1)
            nc.scalar.activation(cos[:, :, :], turns[:, :, :], ACT.Sin).then_inc(trig_ready, 1)
            for g in range(GROUPS):
                act.wait_ge(shifted, g + 1)
                if g >= 1:
                    act.wait_ge(dist_ready, g)
                nc.scalar.activation(dist[:, :, :], logits[:, :, :], ACT.Exp).then_inc(exped, 1)
                act.wait_ge(turned, g + 1)
                if g >= 1:
                    act.wait_ge(coarse_done, g)
                nc.scalar.activation(distT[:, :, :], ps[:, 0, :], ACT.Copy).then_inc(distT_ready, 1)
                act.wait_ge(coarse_done, g + 1)
                nc.scalar.activation(H[:, g * GT:(g + 1) * GT, HALF_D:D],
                                     ps[:, 1, :].rearrange("p (t c) -> p t c", c=HALF_D), ACT.Copy).then_inc(coarse_in_h, 1)
            act.wait_ge(kT_psum, 1)
            nc.scalar.activation(KT[:, :, :], ps[:, 2, :], ACT.Copy).then_inc(kT_ready, 1)
            act.wait_ge(kf_psum, 1)
            for w in range(2):
                bank = ps[:, 3 + w, :].rearrange("p (s d) -> p s d", d=D)
                nc.scalar.activation(Kr[:, w, :, :], bank[:, 0:2, :], ACT.Copy).then_inc(kf_ready, 1)
                nc.scalar.activation(Ki[:, w, :, :], bank[:, 2:4, :], ACT.Copy).then_inc(kf_ready, 1)
                nc.scalar.activation(Krn[:, w, :], bank[:, 0, :], ACT.Copy).then_inc(kf_ready, 1)
            act.wait_ge(var_ready, 1)
            act.wait_ge(eps_ready, 1)
            nc.scalar.activation(var[:, :], var[:, :], ACT.Sqrt, bias=eps[:, 0:1]).then_inc(std_ready, 1)

        @block.tensor
        def _(pe):
            pe.wait_ge(idn_in, 32)
            pe.wait_ge(cw_in, 48)
            for g in range(GROUPS):
                pe.wait_ge(dist_ready, g + 1)
                if g >= 1:
                    pe.wait_ge(distT_ready, g)
                for t in range(GT // 2):
                    last = nc.tensor.transpose(ps[:, 0, t * P:(t + 1) * P],
                                               dist[:, 2 * t:2 * t + 2, :].rearrange("p t c -> p (t c)"), ident[:, :])
                last.then_inc(turned, 1)
                pe.wait_ge(distT_ready, g + 1)
                if g >= 1:
                    pe.wait_ge(coarse_in_h, g)
                for t in range(GT // 2):
                    last = nc.tensor.matmul(ps[:, 1, t * D:(t + 1) * D], distT[:, t, :], cw[:, :], start=True, stop=True)
                last.then_inc(coarse_done, 1)
            pe.wait_ge(k_ready, 1)
            for c in range(CHUNKS):
                last = nc.tensor.transpose(ps[:, 2, c * P:(c + 1) * P], K[:, c * P:(c + 1) * P], ident[:, :])
            last.then_inc(kT_psum, 1)
            pe.wait_ge(kT_ready, 1)
            pe.wait_ge(dft_in, 16)
            for w, chunks in enumerate((2, 4)):
                for s in range(SLOTS):
                    for c in range(chunks):
                        last = nc.tensor.matmul(ps[:, 3 + w, s * D:(s + 1) * D], fwd[:, c, s * P:(s + 1) * P], KT[:, c, :],
                                                start=(c == 0), stop=(c == chunks - 1))
            last.then_inc(kf_psum, 1)
            pe.wait_ge(u_ready, 1)
            pe.wait_ge(kf_ready, 6)
            pe.wait_ge(inv_in, 16)
            Uv = U[:, :, :].rearrange("p (b c) d -> p b c d", c=CHUNKS)

            def forward(u):
                half, b = u // 2, u % 2
                if u >= 1:
                    pe.wait_ge(terms_ready, 12 * u)
                for j in range(2):
                    for ri in range(2):
                        for c in range(2):
                            last = nc.tensor.matmul(ps[:, 2 * j + ri, :], fwd[:, 2 * j + c, (2 * ri + b) * P:(2 * ri + b + 1) * P],
                                                    Uv[:, 4 * half:4 * half + 4, 2 * j + c, :], start=(c == 0), stop=(c == 1))
                last.then_inc(spectrum, 1)

            def inverse(half):
                pe.wait_ge(pool_sums, 16 * (half + 1))
                for q in range(CHUNKS):
                    if half:
                        pe.wait_ge(out_done, q + 1)
                    for s in range(SLOTS):
                        last = nc.tensor.matmul(ps[:, 4 + q, :], inv[:, s, q * P:(q + 1) * P], Y[:, half, s, q // 2, :],
                                                start=(s == 0), stop=(s == SLOTS - 1))
                    last.then_inc(out_psum, 1)

            for u in range(3):
                forward(u)
            inverse(0)
            forward(3)
            inverse(1)

        @block.vector
        def _(dve):
            V = nc.vector
            own = Chain(dve, dve_own)
            V.memset(cw[:, :], 0.0).then_inc(cw_cleared, 1)
            V.memset(eps[:, :], EPS).then_inc(eps_ready, 1)
            dve.wait_ge(params_in, 96)
            own(V.tensor_scalar(dtA[:, 0, :], par[:, 0, :], delta[:, 0:1], None, ALU.mult))
            own.link(V.tensor_scalar(dtA[:, 1, :], par[:, 1, :], delta[:, 0:1], None, ALU.mult))
            where = pos[:, :].rearrange("p (c a) -> p c a", a=1).broadcast_to([P, NPOS, STATES])
            one = dtA[:, 0, :].rearrange("p (a n) -> p a n", a=1).broadcast_to([P, NPOS, STATES])
            two = dtA[:, 1, :].rearrange("p (a n) -> p a n", a=1).broadcast_to([P, NPOS, STATES])
            V.tensor_tensor(mag[:, :, :], where, one, ALU.mult).then_inc(mag_in, 1)
            own.link(V.tensor_tensor(phase[:, :, :], where, two, ALU.mult))
            own.link(V.tensor_scalar(turns[:, :, :], phase[:, :, :], 1.0 / TWO_PI, ROUND, ALU.mult, ALU.add))
            own.link(V.tensor_scalar(turns[:, :, :], turns[:, :, :], ROUND, None, ALU.subtract))
            own.link(V.scalar_tensor_tensor(phase[:, :, :], turns[:, :, :], -TWO_PI_HI, phase[:, :, :], ALU.mult, ALU.add))
            own.link(V.scalar_tensor_tensor(phase[:, :, :], turns[:, :, :], TWO_PI_HI - TWO_PI, phase[:, :, :], ALU.mult, ALU.add))
            own.link(V.tensor_scalar(phase[:, :, :], phase[:, :, :], 3.1415925, -3.1415925, ALU.min, ALU.max))
            V.scalar_tensor_tensor(turns[:, :, :], phase[:, :, :], -1.0, phase[:, :, :], ALU.mult, ALU.min).then_inc(trig_in, 1)
            dve.wait_ge(trig_in, 1)
            V.tensor_scalar(turns[:, :, :], turns[:, :, :], TWO_PI / 4, None, ALU.add).then_inc(trig_in, 1)
            t, em1, shc, er, ei, den, qr, qi, bc, x1, x2, wr, wi = (small[:, n, :] for n in range(13))
            ar, ai = par[:, 0, :], par[:, 1, :]
            dve.wait_ge(tanh_ready, 1)
            own(V.tensor_scalar(x1, t, -1.0, 1.0, ALU.mult, ALU.add))
            own(V.tensor_tensor(bc, par[:, 2, :], par[:, 3, :], ALU.mult))
            own(V.tensor_tensor(x2, ar, ar, ALU.mult))
            own(V.tensor_tensor(den, ai, ai, ALU.mult))
            own.done()
            own(V.reciprocal(x1, x1))
            own(V.tensor_tensor(den, den, x2, ALU.add))
            own.done()
            own(V.scalar_tensor_tensor(em1, t, 2.0, x1, ALU.mult, ALU.mult))
            own(V.reciprocal(den, den))
            own.done()
            dve.wait_ge(trig_ready, 2)
            dve.wait_ge(mag_ready, 1)
            half_sin, sin1, cos1 = sin[:, NPOS - 1, :], sin[:, 1, :], cos[:, 1, :]
            own(V.scalar_tensor_tensor(shc, half_sin, -2.0, half_sin, ALU.mult, ALU.mult))
            own(V.tensor_tensor(er, em1, cos1, ALU.mult))
            own(V.scalar_tensor_tensor(ei, em1, 1.0, sin1, ALU.add, ALU.mult))
            own.done()
            own.link(V.tensor_tensor(er, er, shc, ALU.add))
            own(V.tensor_tensor(qr, er, ar, ALU.mult))
            own(V.tensor_tensor(x1, ei, ai, ALU.mult))
            own(V.tensor_tensor(qi, ei, ar, ALU.mult))
            own(V.tensor_tensor(x2, er, ai, ALU.mult))
            own(V.tensor_tensor(bc, bc, den, ALU.mult))
            own.done()
            own(V.tensor_tensor(qr, qr, x1, ALU.add))
            own(V.tensor_tensor(qi, qi, x2, ALU.subtract))
            own.done()
            own(V.tensor_tensor(wr, qr, bc, ALU.mult))
            own(V.tensor_tensor(wi, qi, bc, ALU.mult))
            own(V.tensor_tensor(fine[:, :, 0:STATES], mag[:, 0:NR, :], cos[:, 0:NR, :], ALU.mult))
            own(V.tensor_tensor(fine[:, :, STATES:], mag[:, 0:NR, :], sin[:, 0:NR, :], ALU.mult))
            own(V.tensor_tensor(turns[:, 0:NA, :], mag[:, NR:NR + NA, :], cos[:, NR:NR + NA, :], ALU.mult))
            own(V.tensor_tensor(phase[:, 0:NA, :], mag[:, NR:NR + NA, :], sin[:, NR:NR + NA, :], ALU.mult))
            own.done()
            wr_b = wr.rearrange("p (a n) -> p a n", a=1).broadcast_to([P, NA, STATES])
            wi_b = wi.rearrange("p (a n) -> p a n", a=1).broadcast_to([P, NA, STATES])
            vr, vi = turns[:, 0:NA, :], phase[:, 0:NA, :]
            own(V.tensor_tensor(rough[:, :, 0:STATES], vr, wr_b, ALU.mult))
            own(V.tensor_tensor(sin[:, 0:NA, :], vi, wi_b, ALU.mult))
            own(V.tensor_tensor(rough[:, :, STATES:], vi, wr_b, ALU.mult))
            own(V.tensor_tensor(cos[:, 0:NA, :], vr, wi_b, ALU.mult))
            own.done()
            own(V.tensor_tensor(rough[:, :, 0:STATES], rough[:, :, 0:STATES], sin[:, 0:NA, :], ALU.subtract))
            own.link(V.scalar_tensor_tensor(rough[:, :, STATES:], rough[:, :, STATES:], -1.0, cos[:, 0:NA, :], ALU.mult, ALU.subtract))
            for q in range(4):
                shape = [P, NA // 4, NR, 2 * STATES]
                a = rough[:, q * NA // 4:(q + 1) * NA // 4, :].rearrange("p a (b n) -> p a b n", b=1).broadcast_to(shape)
                f = fine[:, :, :].rearrange("p (a r) n -> p a r n", a=1).broadcast_to(shape)
                own.link(V.tensor_tensor(prod[:, :, :, :], a, f, ALU.mult))
                own.link(V.tensor_reduce(K[:, q * P:(q + 1) * P], prod[:, :, :, :].rearrange("p a r n -> p (a r) n"), AX.X, ALU.add))
            V.tensor_copy(tmp[:, 0:1], eps[:, 0:1]).then_inc(k_ready, 1)
            dve.wait_ge(cw_in, 48)
            for g in range(GROUPS):
                dve.wait_ge(gathered[g], 16 * GT)
                if g >= 1:
                    dve.wait_ge(exped, g)
                cb_b = cb[:, :].rearrange("p (a c) -> p a c", a=1).broadcast_to([P, GT, HALF_D])
                own.link(V.tensor_tensor(logits[:, :, :], H[:, g * GT:(g + 1) * GT, HALF_D:D], cb_b, ALU.add))
                own.link(V.tensor_reduce(top[:, :], logits[:, :, :], AX.X, ALU.max))
                top_b = top[:, :].rearrange("p (t a) -> p t a", a=1).broadcast_to([P, GT, HALF_D])
                V.tensor_tensor(logits[:, :, :], logits[:, :, :], top_b, ALU.subtract).then_inc(shifted, 1)
                dve.wait_ge(exped, g + 1)
                own.link(V.tensor_reduce(total[:, :], dist[:, :, :], AX.X, ALU.add))
                own.link(V.reciprocal(total[:, :], total[:, :]))
                total_b = total[:, :].rearrange("p (t a) -> p t a", a=1).broadcast_to([P, GT, HALF_D])
                V.tensor_tensor(dist[:, :, :], dist[:, :, :], total_b, ALU.mult).then_inc(dist_ready, 1)
            dve.wait_ge(coarse_in_h, GROUPS)
            token_statistics(nc, dve, own, H, stats, mean[:, :], var[:, :], tmp[:, :]).then_inc(var_ready, 1)
            dve.wait_ge(kf_ready, 6)
            for w in range(2):
                own(V.tensor_copy(Krn[0:1, w, :], Ki[0:1, w, 0, :]))
            own.done()
            for w in range(2):
                own(V.memset(Ki[0:1, w, 0, :], 0.0))
            dve.wait_ge(std_ready, 1)
            own.link(V.reciprocal(var[:, :], var[:, :]))
            for t in range(TILES):
                last = V.tensor_scalar(U[:, t, :], H[:, t, :], mean[:, t:t + 1], var[:, t:t + 1], ALU.subtract, ALU.mult)
                own(last)
            own.done()
            V.tensor_copy(tmp[:, 0:1], eps[:, 0:1]).then_inc(u_ready, 1)
            Hv = H[:, :, :].rearrange("p (b c) d -> p b c d", c=CHUNKS)

            def add_out(half):
                for q in range(CHUNKS):
                    dve.wait_ge(out_psum, CHUNKS * half + q + 1)
                    V.tensor_tensor(Hv[:, 4 * half:4 * half + 4, q, :], ps[:, 4 + q, :].rearrange("p (b d) -> p b d", d=D),
                                    Hv[:, 4 * half:4 * half + 4, q, :], ALU.add).then_inc(out_done, 1)

            for u in range(4):
                half, b = u // 2, u % 2
                dve.wait_ge(spectrum, u + 1)
                if u >= 1:
                    dve.wait_ge(pool_sums, 8 * u)
                def wide(x):
                    return x.rearrange("p (a d) -> p a d", a=1).broadcast_to([P, 4, D])
                def bank(n):
                    return ps[:, n, :].rearrange("p (a d) -> p a d", d=D)
                real = [wide(Kr[:, w, b, :]) for w in range(2)]
                real_n = [wide(Krn[:, w, :]) if b == 0 else real[w] for w in range(2)]
                imag = [wide(Ki[:, w, b, :]) for w in range(2)]
                HEAD, WHOLE = 0, 1
                pairs = ((0, real[HEAD]), (1, imag[HEAD]), (0, imag[HEAD]), (1, real_n[HEAD]),
                         (0, real[WHOLE]), (1, imag[WHOLE]), (2, real[HEAD]), (3, imag[HEAD]),
                         (0, imag[WHOLE]), (1, real_n[WHOLE]), (2, imag[HEAD]), (3, real_n[HEAD]))
                for n, (source, coefficient) in enumerate(pairs):
                    V.tensor_tensor(terms[:, n, :].rearrange("p (a d) -> p a d", d=D), bank(source), coefficient,
                                    ALU.mult).then_inc(terms_ready, 1)
                if u == 3:
                    add_out(0)
            add_out(1)


X_SCALE = 2.0 ** 6
PARTS = 2
HI, LO = 0, 1


def split_products(pe, out, stationary, moving, start, stop, **options):
    pairs = ((HI, HI), (HI, LO), (LO, HI))
    for n, (a, b) in enumerate(pairs):
        last = pe.matmul(out, stationary(a), moving(b), start=start and n == 0, stop=stop and n == len(pairs) - 1, **options)
    return last


def normalize(nc, stage, H, XT, ident16):
    with ExitStack() as ctx:
        m = Memory(nc, stage, ctx)
        stats = m.sbuf("stats", [P, TILES, 6])
        per_token = m.sbuf("per_token", [P, 3, TILES])
        mean, var, tmp = (per_token[:, n, :] for n in range(3))
        eps = m.sbuf("eps", [P, 1])
        norm = m.sbuf("norm", [P, 2, CHUNKS, D])
        parts = m.sbuf("parts", [P, 2, PARTS, CHUNKS * D], F16)
        ps = m.psum("ps", [P, 2, PARTS, CHUNKS * P], F16)
        (own_sem, eps_ready, var_ready, std_ready, norm_ready, hi_ready, lo_ready, turned, xt_ready) = (m.sem(n) for n in (
            "own", "eps_ready", "var_ready", "std_ready", "norm_ready", "hi_ready", "lo_ready", "turned", "xt_ready"))
        block = ctx.enter_context(nc.Block())

        @block.vector
        def _(dve):
            V = nc.vector
            own = Chain(dve, own_sem)
            V.memset(eps[:, :], EPS / X_SCALE ** 2).then_inc(eps_ready, 1)
            token_statistics(nc, dve, own, H, stats, mean[:, :], var[:, :], tmp[:, :]).then_inc(var_ready, 1)
            dve.wait_ge(std_ready, 1)
            own.link(V.reciprocal(var[:, :], var[:, :]))
            with dve.Fori(0, SEQS // 2) as i:
                for p in range(2):
                    b = i * 2 + p
                    for c in range(CHUNKS):
                        last = V.tensor_scalar(norm[:, p, c, :], H[:, bass.ds(b * CHUNKS + c, 1), :].rearrange("p a d -> p (a d)"),
                                               mean[:, bass.ds(b * CHUNKS + c, 1)], var[:, bass.ds(b * CHUNKS + c, 1)],
                                               ALU.subtract, ALU.mult)
                        last.then_inc(norm_ready, 1)
                    dve.wait_ge(norm_ready, (b + 1) * CHUNKS)
                    dve.wait_ge(hi_ready, b + 1)
                    V.tensor_tensor(parts[:, p, LO, :], norm[:, p, :, :].rearrange("p c d -> p (c d)"),
                                    parts[:, p, HI, :], ALU.subtract).then_inc(lo_ready, 1)

        @block.scalar
        def _(act):
            A = nc.scalar
            act.wait_ge(var_ready, 1)
            act.wait_ge(eps_ready, 1)
            A.activation(var[:, :], var[:, :], ACT.Sqrt, bias=eps[:, 0:1], scale=X_SCALE ** -2).then_inc(std_ready, 1)

            def high(b, p):
                act.wait_ge(norm_ready, (b + 1) * CHUNKS)
                A.activation(parts[:, p, HI, :], norm[:, p, :, :].rearrange("p c d -> p (c d)"), ACT.Copy).then_inc(hi_ready, 1)

            def out(b, p):
                act.wait_ge(turned, b + 1)
                act.wait_ge(var_ready, 1)
                A.activation(XT[:, bass.ds(b, 1), :, :], ps[:, p, :, :], ACT.Copy).then_inc(xt_ready, 1)

            high(0, 0)
            high(1, 1)
            with act.Fori(0, SEQS // 2 - 1) as i:
                for p in range(2):
                    out(i * 2 + p, p)
                    high(i * 2 + p + 2, p)
            out(SEQS - 2, 0)
            out(SEQS - 1, 1)

        @block.tensor
        def _(pe):
            def turn(b, p, first):
                pe.wait_ge(lo_ready, b + 1)
                if not first:
                    pe.wait_ge(xt_ready, b - 1)
                for part in range(PARTS):
                    for c in range(CHUNKS):
                        last = nc.tensor.transpose(ps[:, p, part, c * P:(c + 1) * P], parts[:, p, part, c * D:(c + 1) * D], ident16[:, :])
                last.then_inc(turned, 1)

            for p in range(2):
                turn(p, p, True)
            with pe.Fori(1, SEQS // 2) as i:
                for p in range(2):
                    turn(i * 2 + p, p, False)


EXPERTS = 8
NEVER = -3.0e38


def top_two(V, own, scores, rank, first, second, m1, m2, work):
    shape = scores.shape
    T = shape[1]
    rank_b = rank.rearrange("p (a e) -> p a e", a=1).broadcast_to(shape)
    wide = lambda x: x.rearrange("p (t a) -> p t a", a=1).broadcast_to(shape)
    picked = work[:, 0:T]
    own.link(V.tensor_reduce(m1, scores, AX.X, ALU.max))
    for onehot, best in ((first, m1), (second, m2)):
        own.link(V.tensor_tensor(onehot, scores, wide(best), ALU.is_equal))
        own.link(V.tensor_tensor(onehot, onehot, rank_b, ALU.mult))
        own.link(V.tensor_reduce(picked, onehot, AX.X, ALU.max))
        own.link(V.tensor_tensor(onehot, onehot, wide(picked), ALU.is_equal))
        if onehot is first:
            own.link(V.scalar_tensor_tensor(scores, first, NEVER, scores, ALU.mult, ALU.add))
            own.link(V.tensor_reduce(m2, scores, AX.X, ALU.max))


def load_bias_blocks(sp, blocks, bias, cleared, loaded):
    sp.wait_ge(cleared, 1)
    for t in range(CHUNKS):
        sp.dma_start(blocks[32 * t:32 * t + EXPERTS, t * D:(t + 1) * D], bias).then_inc(loaded, 16)


def route_recurrent(nc, H, XT, ident, d, combine, mask_rows):
    COLS = 32
    with ExitStack() as ctx:
        m = Memory(nc, "route", ctx)
        rw = m.sbuf("router_w", [P, EXPERTS])
        rws = m.sbuf("router_w_parts", [P, PARTS, EXPERTS], F16)
        rb = m.sbuf("router_b", [P, EXPERTS])
        rank = m.sbuf("rank", [P, EXPERTS])
        bias_blocks = m.sbuf("bias_blocks", [P, CHUNKS * D])
        logits = m.sbuf("logits", [P, TILES, EXPERTS])
        first = m.sbuf("first", [P, TILES, EXPERTS])
        second = m.sbuf("second", [P, TILES, EXPERTS])
        per_token = m.sbuf("per_token", [P, 5, TILES])
        m1, m2, e, r1, work = (per_token[:, n, :] for n in range(5))
        share = m.sbuf("share", [P, TILES, EXPERTS])
        record = m.sbuf("record", [P, TILES, COLS])
        rows = m.sbuf("rows", [P, SEQS, P])
        rows16 = m.sbuf("rows16", [P, SEQS, P], F16)
        psL = m.psum("psL", [P, 512])
        psR = m.psum("psR", [P, SEQS, P])
        psB = m.psum("psB", [P, 2, CHUNKS * D])
        (params_in, w_hi, w_parts, cleared, bias_in, logits_psum, own_sem, gap_ready, exp_ready, record_ready, rows_psum,
         rows_ready, rows16_ready, stored, bias_psum, bias_added) = (m.sem(n) for n in (
             "params_in", "w_hi", "w_parts", "cleared", "bias_in", "logits_psum", "own", "gap_ready", "exp_ready", "record_ready",
             "rows_psum", "rows_ready", "rows16_ready", "stored", "bias_psum", "bias_added"))
        block = ctx.enter_context(nc.Block())

        @block.sync
        def _(sp):
            sp.dma_start(rw[:, :], d["router_w"]).then_inc(params_in, 16)
            sp.dma_start(rb[:, :], d["router_b"]).then_inc(params_in, 16)
            sp.dma_start(rank[:, :], d["rank"]).then_inc(params_in, 16)
            load_bias_blocks(sp, bias_blocks, d["bo"], cleared, bias_in)
            sp.wait_ge(rows16_ready, 1)
            for t in range(CHUNKS):
                sp.dma_start(mask_rows.rearrange("j (b c q) -> j b c q", b=SEQS, c=CHUNKS)[:, :, t, :],
                             rows16[COLS * t + EXPERTS:COLS * t + 3 * EXPERTS, :, :]).then_inc(stored, 16)
            sp.wait_ge(stored, 16 * CHUNKS)

        @block.scalar
        def _(act):
            A = nc.scalar
            act.wait_ge(params_in, 48)
            A.activation(rws[:, HI, :], rw[:, :], ACT.Copy, scale=W_SCALE_ROUTER).then_inc(w_hi, 1)
            act.wait_ge(gap_ready, 1)
            A.activation(e[:, :], e[:, :], ACT.Exp).then_inc(exp_ready, 1)
            act.wait_ge(rows_psum, 1)
            A.activation(rows[:, :, :], psR[:, :, :], ACT.Copy).then_inc(rows_ready, 1)
            A.activation(rows16[:, :, :], psR[:, :, :], ACT.Copy).then_inc(rows16_ready, 1)

        @block.tensor
        def _(pe):
            pe.wait_ge(w_parts, 1)
            with pe.Fori(0, SEQS) as b:
                for c in range(CHUNKS):
                    last = split_products(
                        nc.tensor, psL[:, bass.ds((b * CHUNKS + c) * EXPERTS, EXPERTS)],
                        lambda part: XT[:, bass.ds(b, 1), part, c * P:(c + 1) * P].rearrange("p a n -> p (a n)"),
                        lambda part: rws[:, part, :], True, True)
                last.then_inc(logits_psum, 1)
            pe.wait_ge(record_ready, 1)
            for b in range(SEQS):
                last = nc.tensor.transpose(psR[:, b, :], record[:, b * CHUNKS:(b + 1) * CHUNKS, :].rearrange("p c j -> p (c j)"), ident[:, :])
            last.then_inc(rows_psum, 1)
            pe.wait_ge(rows_ready, 1)
            pe.wait_ge(bias_in, 16 * CHUNKS)
            for b in range(SEQS):
                if b >= 2:
                    pe.wait_ge(bias_added, b - 1)
                nc.tensor.matmul(psB[:, b % 2, :], rows[:, b, :], bias_blocks[:, :], start=True, stop=True).then_inc(bias_psum, 1)

        @block.vector
        def _(dve):
            V = nc.vector
            own = Chain(dve, own_sem)
            V.memset(bias_blocks[:, :], 0.0).then_inc(cleared, 1)
            own(V.memset(record[:, :, 3 * EXPERTS:], 0.0))
            dve.wait_ge(params_in, 48)
            dve.wait_ge(w_hi, 1)
            V.scalar_tensor_tensor(rws[:, LO, :], rw[:, :], W_SCALE_ROUTER, rws[:, HI, :], ALU.mult, ALU.subtract).then_inc(w_parts, 1)
            dve.wait_ge(logits_psum, SEQS)
            rb_b = rb[:, :].rearrange("p (a e) -> p a e", a=1).broadcast_to([P, TILES, EXPERTS])
            own.link(V.scalar_tensor_tensor(logits[:, :, :], psL[:, 0:TILES * EXPERTS].rearrange("p (t e) -> p t e", e=EXPERTS),
                                            1.0 / (X_SCALE * W_SCALE_ROUTER), rb_b, ALU.mult, ALU.add))
            top_two(V, own, logits[:, :, :], rank[:, :], first[:, :, :], second[:, :, :], m1[:, :], m2[:, :], work[:, :])
            V.tensor_tensor(e[:, :], m2[:, :], m1[:, :], ALU.subtract).then_inc(gap_ready, 1)
            dve.wait_ge(exp_ready, 1)
            own.link(V.tensor_scalar(r1[:, :], e[:, :], 1.0, None, ALU.add))
            own.link(V.reciprocal(r1[:, :], r1[:, :]))
            own(V.tensor_tensor(e[:, :], e[:, :], r1[:, :], ALU.mult))
            wide = lambda x: x.rearrange("p (t a) -> p t a", a=1).broadcast_to([P, TILES, EXPERTS])
            own(V.tensor_tensor(share[:, :, :], first[:, :, :], wide(r1[:, :]), ALU.mult))
            own(V.tensor_copy(record[:, :, EXPERTS:2 * EXPERTS], first[:, :, :]))
            own(V.tensor_copy(record[:, :, 2 * EXPERTS:3 * EXPERTS], second[:, :, :]))
            own.done()
            own.link(V.tensor_tensor(second[:, :, :], second[:, :, :], wide(e[:, :]), ALU.mult))
            own.link(V.tensor_tensor(record[:, :, 0:EXPERTS], share[:, :, :], second[:, :, :], ALU.add))
            V.tensor_scalar(combine[:, :, :], record[:, :, 0:EXPERTS], 1.0 / OUT_SCALE, None, ALU.mult).then_inc(record_ready, 1)
            for b in range(SEQS):
                dve.wait_ge(bias_psum, b + 1)
                here = H[:, b * CHUNKS:(b + 1) * CHUNKS, :].rearrange("p c d -> p (c d)")
                V.tensor_tensor(here, psB[:, b % 2, :], here, ALU.add).then_inc(bias_added, 1)


W_SCALE_ROUTER = 2.0 ** 8
H_SCALE = 2.0 ** 8
WI_SCALE = 2.0 ** 8
WH_SCALE = X_SCALE * WI_SCALE / H_SCALE
WO_SCALE = 2.0 ** 6
GATE_SCALE = X_SCALE * WI_SCALE
OUT_SCALE = H_SCALE * WO_SCALE
STEPS, WIDTH = SEQS, SEQ
GATES = 4
IN, FORGET, CELL, OUT = range(GATES)


def recurrent_experts(nc, H, XT, d, combine, mask_rows):
    GD = GATES * D
    ORDER = (IN, CELL, FORGET, OUT)
    with ExitStack() as ctx:
        m = Memory(nc, "lstm", ctx)
        biases = m.sbuf("biases", [P, EXPERTS * GATES])
        bias = m.sbuf("bias", [P, 2, GATES])
        raw = m.sbuf("weights", [P, 2, 2 * GD + D])
        wp = m.sbuf("weight_parts", [P, 2, PARTS, 2 * GD], F16)
        wo = m.sbuf("output_weight_parts", [P, 2, PARTS, D], F16)
        mask = m.sbuf("mask", [P, 2, 2, STEPS * WIDTH], F16)
        xm = m.sbuf("masked_x", [P, 2, 2, PARTS, WIDTH], F16)
        gates = m.sbuf("gates", [P, 2, GATES, WIDTH])
        cell = m.sbuf("cell", [P, 2, WIDTH])
        tc = m.sbuf("tanh_cell", [P, 2, WIDTH])
        hid = m.sbuf("hidden", [P, 2, WIDTH])
        hp = m.sbuf("hidden_parts", [P, 2, PARTS, WIDTH], F16)
        z1 = m.sbuf("second_choice", [P, PARTS, WIDTH], F16)
        z = m.sbuf("chosen", [P, 2, STEPS, PARTS, WIDTH], F16)
        ps = m.psum("ps", [P, 8, WIDTH])
        bias_in = m.sem("bias_in")
        weights_in = [m.sem(f"weights_in{p}") for p in range(2)]
        mask_in = [m.sem(f"mask_in{p}") for p in range(2)]
        (bias_ready, hi_weights, weights_ready, hi_output_weights, output_weights_ready, xm_ready, gate_psum, gate_ready, own_sem, cell_ready, tc_ready, hidden_ready,
         hidden_hi, hidden_lo, z0_ready, z1_ready, z_ready, wo_psum, wo_added) = (m.sem(n) for n in (
             "bias_ready", "hi_weights", "weights_ready", "hi_output_weights", "output_weights_ready", "xm_ready", "gate_psum", "gate_ready", "own", "cell_ready", "tc_ready",
             "hidden_ready", "hidden_hi", "hidden_lo", "z0_ready", "z1_ready", "z_ready", "wo_psum", "wo_added"))
        block = ctx.enter_context(nc.Block())

        skip = lambda *a: None

        def schedule(engine, step, extra=skip, before=skip):
            def rest(e, parity):
                before(e, parity)
                step(e, parity, 1, 1)
                extra(e, parity)
                with engine.Fori(1, STEPS // 2) as j:
                    for p in range(2):
                        step(e, parity, j * 2 + p, p)

            step(0, 0, 0, 0)
            rest(0, 0)
            step(1, 1, 0, 0)
            with engine.Fori(0, EXPERTS // 2 - 1) as i:
                for n in (1, 2):
                    rest(i * 2 + n, n % 2)
                    step(i * 2 + n + 1, 1 - n % 2, 0, 0)
            rest(EXPERTS - 1, 1)

        is_first = lambda e, s: isinstance(s, int) and isinstance(e, int) and e == 0 and s == 0
        at_start = lambda e, s: isinstance(s, int) and s == 0
        has_output = lambda e: not (isinstance(e, int) and e == 0)

        @block.sync
        def _(sp):
            sp.dma_start(biases[:, :], d["lstm_b"]).then_inc(bias_in, 16)

            def load_weights(e, parity):
                for n, (name, at, width) in enumerate((("Wi", 0, GD), ("Wh", GD, GD), ("Wo", 2 * GD, D))):
                    sp.dma_start(raw[:, parity, at:at + width], d[name][bass.ds(e * P, P), :]).then_inc(weights_in[parity], 16)

            def load_masks(e, parity):
                for k in range(2):
                    row = mask_rows[bass.ds(e + k * EXPERTS, 1), :]
                    sp.dma_start(mask[:, parity, k, :], row.partition_broadcast(P)).then_inc(mask_in[parity], 16)

            def before(e, parity):
                if not (isinstance(e, int) and e == EXPERTS - 1):
                    if not (isinstance(e, int) and e == 0):
                        sp.wait_ge(z_ready, e * STEPS)
                    load_weights(e + 1, 1 - parity)
                    load_masks(e + 1, 1 - parity)

            load_masks(0, 0)
            load_weights(0, 0)
            schedule(sp, skip, before=before)

        @block.gpsimd
        def _(pool):
            def z0(n_s, e_parity, s):
                pool.wait_ge(hidden_lo, n_s * 2 + 1)
                m0 = mask[:, e_parity, 0, bass.ds(s * WIDTH, WIDTH)].rearrange("p (a n) -> p a n", a=1).broadcast_to([P, PARTS, WIDTH])
                nc.gpsimd.tensor_tensor(z[:, e_parity, bass.ds(s, 1), :, :].rearrange("p a h n -> p (a h) n"), hp[:, 0, :, :], m0,
                                        ALU.mult).then_inc(z0_ready, 1)

            def step(e, parity, s, p):
                n_s = e * STEPS + s
                if at_start(e, s):
                    pool.wait_ge(mask_in[parity], (e - parity) * 16 + 32)
                if not (isinstance(n_s, int) and n_s < 2):
                    pool.wait_ge(gate_psum, (n_s - 1) * 2 * GATES)
                shape = [P, 2, PARTS, WIDTH]
                m_b = mask[:, parity, :, bass.ds(s * WIDTH, WIDTH)].rearrange("p k (a n) -> p k a n", a=1).broadcast_to(shape)
                x_b = XT[:, bass.ds(s, 1), :, :].broadcast_to(shape)
                nc.gpsimd.tensor_tensor(xm[:, p, :, :, :], x_b, m_b, ALU.mult).then_inc(xm_ready, 1)
                if at_start(e, s):
                    if not is_first(e, s):
                        z0(n_s - 1, 1 - parity, STEPS - 1)
                else:
                    z0(n_s - 1, parity, s - 1)

            schedule(pool, step)
            z0(EXPERTS * STEPS - 1, 1, STEPS - 1)

        @block.tensor
        def _(pe):
            def w(parity, part, at, gate):
                return wp[:, parity, part, at + gate * D:at + (gate + 1) * D]

            def output_product(e, parity, s, bank):
                pe.wait_ge(output_weights_ready, e + 1)
                pe.wait_ge(z_ready, e * STEPS + s + 1)
                for c in range(CHUNKS):
                    last = split_products(
                        nc.tensor, ps[:, bank, c * P:(c + 1) * P],
                        lambda part: z[:, parity, bass.ds(s, 1), part, c * P:(c + 1) * P].rearrange("p a n -> p (a n)"),
                        lambda part: wo[:, parity, part, :], True, True)
                last.then_inc(wo_psum, 1)

            def step(e, parity, s, p):
                n_s = e * STEPS + s
                for k in range(2):
                    n_u = n_s * 2 + k
                    if at_start(e, s) and k == 0:
                        pe.wait_ge(weights_ready, e + 1)
                    pe.wait_ge(xm_ready, n_s + 1)
                    if not is_first(e, s):
                        pe.wait_ge(gate_ready, (n_u - 1) * GATES)
                    for g in ORDER:
                        if k == 0 and g == OUT and has_output(e) and not (isinstance(e, int) and e == 1 and at_start(e, s)):
                            pe.wait_ge(wo_added, (e - 1) * STEPS + s)
                        last = split_products(nc.tensor, ps[:, 4 * k + g, :], lambda part: w(parity, part, 0, g),
                                              lambda part: xm[:, p, k, part, :], True, at_start(e, s))
                        if at_start(e, s):
                            last.then_inc(gate_psum, 1)
                    if k == 1 and has_output(e):
                        pe.wait_ge(gate_ready, n_u * GATES)
                        output_product(e - 1, 1 - parity, s, OUT)
                    if not at_start(e, s):
                        pe.wait_ge(hidden_lo, n_u - 1)
                        for g in ORDER:
                            split_products(nc.tensor, ps[:, 4 * k + g, :], lambda part: w(parity, part, GD, g),
                                           lambda part: hp[:, k, part, :], False, True).then_inc(gate_psum, 1)

            schedule(pe, step)
            pe.wait_ge(gate_ready, EXPERTS * STEPS * 2 * GATES)
            pe.wait_ge(wo_added, (EXPERTS - 1) * STEPS)
            for s in range(STEPS):
                output_product(EXPERTS - 1, 1, s, s)

        @block.scalar
        def _(act):
            A = nc.scalar
            A.preload_act_table(ACT.Sigmoid)
            def split_high(e, parity):
                act.wait_ge(weights_in[parity], (e - parity) * 24 + 48)
                for at, scale in ((0, WI_SCALE), (GD, WH_SCALE)):
                    A.activation(wp[:, parity, HI, at:at + GD], raw[:, parity, at:at + GD], ACT.Copy, scale=scale).then_inc(hi_weights, 1)

            def split_output_high(e, parity):
                A.activation(wo[:, parity, HI, :], raw[:, parity, 2 * GD:], ACT.Copy, scale=WO_SCALE).then_inc(hi_output_weights, 1)

            split_high(0, 0)
            act.wait_ge(bias_in, 16)

            def take_bias(e, parity):
                A.activation(bias[:, parity, :], biases[:, bass.ds(e * GATES, GATES)], ACT.Copy).then_inc(bias_ready, 1)

            take_bias(0, 0)

            def step(e, parity, s, p):
                n_s = e * STEPS + s
                for k in range(2):
                    n_u = n_s * 2 + k
                    if at_start(e, s):
                        act.wait_ge(bias_ready, e + 1)
                    if not is_first(e, s):
                        act.wait_ge(hidden_ready, n_u - 1)
                    for n, g in enumerate(ORDER):
                        act.wait_ge(gate_psum, n_u * GATES + n + 1)
                        done = A.activation(gates[:, k, g, :], ps[:, 4 * k + g, :], ACT.Tanh if g == CELL else ACT.Sigmoid,
                                            bias=bias[:, parity, g:g + 1], scale=1.0 / GATE_SCALE)
                        done.then_inc(gate_ready, 1)
                    act.wait_ge(cell_ready, n_u + 1)
                    A.activation(tc[:, k, :], cell[:, k, :], ACT.Tanh).then_inc(tc_ready, 1)
                    act.wait_ge(hidden_ready, n_u + 1)
                    if not is_first(e, s):
                        act.wait_ge(z1_ready if k else z0_ready, n_s)
                    A.activation(hp[:, k, HI, :], hid[:, k, :], ACT.Copy).then_inc(hidden_hi, 1)

            def extra(e, parity):
                split_output_high(e, parity)
                if not (isinstance(e, int) and e == EXPERTS - 1):
                    split_high(e + 1, 1 - parity)
                    take_bias(e + 1, 1 - parity)

            schedule(act, step, extra=extra)

        @block.vector
        def _(dve):
            V = nc.vector

            def split_low(e, parity):
                dve.wait_ge(hi_weights, e * 2 + 2)
                for at, scale in ((0, WI_SCALE), (GD, WH_SCALE)):
                    last = V.scalar_tensor_tensor(wp[:, parity, LO, at:at + GD], raw[:, parity, at:at + GD], scale,
                                                  wp[:, parity, HI, at:at + GD], ALU.mult, ALU.subtract)
                last.then_inc(weights_ready, 1)

            def split_output_low(e, parity):
                dve.wait_ge(hi_output_weights, e + 1)
                V.scalar_tensor_tensor(wo[:, parity, LO, :], raw[:, parity, 2 * GD:], WO_SCALE, wo[:, parity, HI, :],
                                       ALU.mult, ALU.subtract).then_inc(output_weights_ready, 1)

            split_low(0, 0)

            def add_output(e, s, bank):
                dve.wait_ge(wo_psum, e * STEPS + s + 1)
                for c in range(CHUNKS):
                    here = H[:, bass.ds(s * CHUNKS + c, 1), :].rearrange("p a d -> p (a d)")
                    share = combine[:, bass.ds(s * CHUNKS + c, 1), bass.ds(e, 1)].rearrange("p a b -> p (a b)")
                    last = V.scalar_tensor_tensor(here, ps[:, bank, c * P:(c + 1) * P], share, here, ALU.mult, ALU.add)
                last.then_inc(wo_added, 1)

            def second_share(n_s, e_parity, s):
                m1 = mask[:, e_parity, 1, bass.ds(s * WIDTH, WIDTH)].rearrange("p (a n) -> p a n", a=1).broadcast_to([P, PARTS, WIDTH])
                if not (isinstance(n_s, int) and n_s == 0):
                    dve.wait_ge(z_ready, n_s)
                dve.wait_ge(hidden_lo, n_s * 2 + 2)
                V.tensor_tensor(z1[:, :, :], hp[:, 1, :, :], m1, ALU.mult).then_inc(z1_ready, 1)

            def choose(n_s, e_parity, s):
                zs = z[:, e_parity, bass.ds(s, 1), :, :].rearrange("p a h n -> p (a h) n")
                dve.wait_ge(z1_ready, n_s + 1)
                dve.wait_ge(z0_ready, n_s + 1)
                V.tensor_tensor(zs, zs, z1[:, :, :], ALU.add).then_inc(z_ready, 1)

            def step(e, parity, s, p):
                n_s = e * STEPS + s
                first_step = at_start(e, s)
                for k in range(2):
                    n_u = n_s * 2 + k
                    g = lambda gate: gates[:, k, gate, :]
                    dve.wait_ge(gate_ready, n_u * GATES + 2)
                    if first_step:
                        V.tensor_tensor(cell[:, k, :], g(IN), g(CELL), ALU.mult).then_inc(cell_ready, 1)
                    else:
                        V.tensor_tensor(g(IN), g(IN), g(CELL), ALU.mult).then_inc(own_sem, 1)
                        dve.wait_ge(gate_ready, n_u * GATES + 3)
                        V.tensor_tensor(cell[:, k, :], g(FORGET), cell[:, k, :], ALU.mult).then_inc(own_sem, 1)
                        dve.wait_ge(own_sem, e * (STEPS - 1) * 4 + s * 4 + (2 * k - 2))
                        V.tensor_tensor(cell[:, k, :], cell[:, k, :], g(IN), ALU.add).then_inc(cell_ready, 1)
                    dve.wait_ge(gate_ready, n_u * GATES + 4)
                    dve.wait_ge(tc_ready, n_u + 1)
                    V.scalar_tensor_tensor(hid[:, k, :], g(OUT), H_SCALE, tc[:, k, :], ALU.mult, ALU.mult).then_inc(hidden_ready, 1)
                    last_step_of = (second_share, choose)[k]
                    if not first_step:
                        last_step_of(n_s - 1, parity, s - 1)
                    elif not is_first(e, s):
                        last_step_of(n_s - 1, 1 - parity, STEPS - 1)
                    dve.wait_ge(hidden_hi, n_u + 1)
                    V.tensor_tensor(hp[:, k, LO, :], hid[:, k, :], hp[:, k, HI, :], ALU.subtract).then_inc(hidden_lo, 1)
                    if k == 0 and has_output(e):
                        add_output(e - 1, s, OUT)

            def extra(e, parity):
                split_output_low(e, parity)
                if not (isinstance(e, int) and e == EXPERTS - 1):
                    split_low(e + 1, 1 - parity)

            schedule(dve, step, extra=extra)
            second_share(EXPERTS * STEPS - 1, 1, STEPS - 1)
            choose(EXPERTS * STEPS - 1, 1, STEPS - 1)
            for s in range(STEPS):
                add_output(EXPERTS - 1, s, s)


HEADS, HEAD = 8, 64
INNER = HEADS * HEAD
PAIRS = HEADS // 2
QK_SCALE = 2.0 ** 8
V_SCALE = 2.0 ** 8
ATT_WO_SCALE = 2.0 ** 6
SHIFT = 256.0
PROB_GAIN = 6.931471805599453
STEPS_A = HEADS * CHUNKS


FIRST_MAX = 11
SPLIT, TURN = (1, 5, 9, 13), (12, 16, 20, 24)


def background_tasks():
    tasks = [[] for _ in range(STEPS_A)]
    for c in range(CHUNKS):
        tasks[SPLIT[c]].append(("split", c))
        tasks[SPLIT[c] + 2].append(("split_low", c))
        tasks[8 + c].append(("v", c))
        tasks[TURN[c]].append(("turn", c))
        tasks[TURN[c] + 1].append(("turned", c))
    for t in range(2 * PAIRS):
        tasks[t].append(("qk", t))
    for c in range(CHUNKS):
        tasks[28 + c].append(("out", c))
    for j in range(STEPS_A):
        tasks[FIRST_MAX + j // 2].append(("max", j))
    tasks[FIRST_MAX + 16].append(("shift", 0))
    return tasks


def attention(nc, H, XT, ident16, d):
    with ExitStack() as ctx:
        m = Memory(nc, "att", ctx)
        wp = m.sbuf("weight_parts", [P, PARTS, 3 * INNER + CHUNKS * D], F16)
        b_out = m.sbuf("b_out", [P, D])
        qk = m.sbuf("qk", [P, 2, PARTS, 2 * PAIRS, SEQ], F16)
        QS = m.sbuf("q_twice", [P, 2, HEADS, SEQ], F16)
        Q2 = m.sbuf("q_lo_shift", [P, 2, HEADS, SEQ], F16)
        KS = m.sbuf("k_parts", [P, 2, HEADS, SEQ], F16)
        K2 = m.sbuf("k_hi_ones", [P, 2, HEADS, SEQ], F16)
        V1 = m.sbuf("v_ones", [P, 2, PARTS, CHUNKS, HEADS, HEAD + 1], F16)
        prob = m.sbuf("prob", [P, 4, SEQ])
        pp = m.sbuf("prob_parts", [P, 4, PARTS, SEQ], F16)
        gain = m.sbuf("prob_gain", [P, 1])
        zero = m.sbuf("zero", [P, 1])
        mx = m.sbuf("max", [P, STEPS_A])
        nm = m.sbuf("shift", [P, STEPS_A], F16)
        nmT = m.sbuf("shiftT", [STEPS_A, 2, P], F16)
        rec = m.sbuf("reciprocal", [P, 2, CHUNKS])
        O = m.sbuf("o", [P, 2, CHUNKS, INNER])
        raw = O[:, :, :, :].rearrange("p a c n -> p (a c n)")
        op = m.sbuf("o_parts", [P, PARTS, CHUNKS, INNER], F16)
        OT = m.sbuf("oT", [P, CHUNKS, PARTS, CHUNKS, P], F16)
        psS = m.psum("psS", [P, 2, SEQ])
        psV = m.psum("psV", [P, 2, SEQ])
        psM = m.psum("psM", [P, 2, SEQ])
        psT = m.psum("psT", [P, PARTS, CHUNKS, P], F16)
        psX = m.psum("psX", [P, SEQ])
        weights_in, consts_in, bias_added, v_ones, gain_ready = (m.sem(n) for n in (
            "weights_in", "consts_in", "bias_added", "v_ones", "gain_ready"))
        placed = [m.sem(f"placed{p}") for p in range(2)]
        shift_in = [m.sem(f"shift_in{p}") for p in range(2)]
        (weights_hi, weights_ready, ones_ready, qk_full, qk_hi, qk_lo, v_full, v_hi, v_ready, max_full, max_done, shift_ready,
         shift_turned, shiftT_ready, s_full, p_full, p_ready, p_lo, av_done, rec_ready, o_ready, o_hi, o_lo, turn_full, turn_done,
         out_full, out_done) = (m.sem(n) for n in (
             "weights_hi", "weights_ready", "ones_ready", "qk_full", "qk_hi", "qk_lo", "v_full", "v_hi", "v_ready", "max_full", "max_done",
             "shift_ready", "shift_turned", "shiftT_ready", "s_full", "p_full", "p_ready", "p_lo", "av_done", "rec_ready", "o_ready", "o_hi",
             "o_lo", "turn_full", "turn_done", "out_full", "out_done"))
        block = ctx.enter_context(nc.Block())
        TASKS = background_tasks()
        AHEAD, BEHIND = ("qk", "v", "max", "shift"), ("split", "split_low", "turn", "turned", "out")

        def schedule(engine, task, step, tasks_first=False, lag=0):
            def sequence(b, parity, ahead, behind):
                def run(n, chosen):
                    for kind, j in TASKS[n] if n >= 0 else ():
                        if kind in AHEAD and ahead and chosen(kind, j):
                            task(kind, j, b + 1, 1 - parity)
                        if kind in BEHIND and behind and chosen(kind, j):
                            task(kind, j, b - 1, 1 - parity)

                second_max = lambda kind, j: kind == "max" and j % 2 == 1
                for n in range(STEPS_A):
                    if tasks_first:
                        run(n, lambda kind, j: not second_max(kind, j))
                    step(b, parity, n)
                    if tasks_first:
                        run(n, second_max)
                    else:
                        run(n - lag, lambda kind, j: True)

            def alone(kinds, b, parity):
                for n in range(STEPS_A):
                    for kind, j in TASKS[n]:
                        if kind in kinds:
                            task(kind, j, b, parity)

            alone(AHEAD, 0, 0)
            sequence(0, 0, True, False)
            with engine.Fori(0, SEQS // 2 - 1) as i:
                for n in (1, 2):
                    sequence(i * 2 + n, n % 2, True, True)
            sequence(SEQS - 1, 1, False, True)
            step(SEQS, 0, 0)
            alone(BEHIND, SEQS - 1, 1)

        nothing = lambda *a: None
        ended = lambda b: isinstance(b, int) and b == SEQS
        known = lambda b, least: isinstance(b, int) and b < least

        @block.sync
        def _(sp):
            for n, name in enumerate(("w_q", "w_k", "w_v")):
                sp.dma_start(raw[:, n * INNER:(n + 1) * INNER], d[name]).then_inc(weights_in, 16)
            sp.dma_start(raw[:, 3 * INNER:3 * INNER + CHUNKS * D].rearrange("p (c d) -> p c d", d=D), d["w_out"].rearrange("(c p) d -> p c d", p=P)).then_inc(weights_in, 16)
            sp.dma_start(b_out[:, :], d["b_out"]).then_inc(consts_in, 16)

            def task(kind, j, b, p):
                if kind == "qk" and j % PAIRS == PAIRS - 1:
                    sp.wait_ge(qk_lo, b * 2 * PAIRS + j + 1)
                    top, low = slice(0, HEAD), slice(HEAD, P)
                    copies = (((QS, top, HI), (QS, low, HI), (Q2, top, LO)), ((KS, top, HI), (KS, low, LO), (K2, top, HI)))[j // PAIRS]
                    for odd in range(2):
                        rows = slice(HEAD * odd, HEAD * (odd + 1))
                        for to, there, part in copies:
                            heads = to[there, p, :, :].rearrange("r (c o) n -> r c o n", o=2)[:, :, odd, :]
                            sp.dma_start(heads, qk[rows, p, part, j + 1 - PAIRS:j + 1, :]).then_inc(placed[p], 16)
                if kind == "shift":
                    sp.wait_ge(shiftT_ready, b + 1)
                    sp.dma_start(Q2[HEAD:HEAD + 1, p, :, :].rearrange("a h (c q) -> a (h c) q", q=P), nmT[:, p, :]).then_inc(shift_in[p], 16)

            schedule(sp, task, nothing)

        @block.tensor
        def _(pe):
            T = nc.tensor

            def score(b, p, n):
                h, c = n // CHUNKS, n % CHUNKS
                if not known(b * STEPS_A + n, 2):
                    pe.wait_ge(p_ready, b * STEPS_A + n - 1)
                keys = slice(c * P, (c + 1) * P)
                T.matmul(psS[:, n % 2, :], KS[:, p, h, keys], QS[:, p, h, :], start=True, stop=False)
                T.matmul(psS[:, n % 2, :], K2[0:HEAD + 1, p, h, keys], Q2[0:HEAD + 1, p, h, :], start=False, stop=True).then_inc(s_full, 1)

            def task(kind, j, b, p):
                x = lambda part, c: XT[:, bass.ds(b, 1), part, c].rearrange("p a n -> p (a n)")
                if kind == "qk":
                    if j >= 2:
                        pe.wait_ge(qk_lo, b * 2 * PAIRS + j - 1)
                    elif not known(b, 1):
                        pe.wait_ge(max_done, b * STEPS_A)
                    split_products(T, psM[:, j % 2, :], lambda part: wp[:, part, j * P:(j + 1) * P], lambda part: x(part, slice(0, SEQ)),
                                   True, True).then_inc(qk_full, 1)
                if kind == "v":
                    if j >= 2:
                        pe.wait_ge(v_ready, b * CHUNKS + j - 1)
                    else:
                        pe.wait_ge(qk_lo, b * 2 * PAIRS + 2 * PAIRS - 1 + j)
                    split_products(T, psM[:, j % 2, :], lambda part: x(part, slice(j * P, (j + 1) * P)),
                                   lambda part: wp[:, part, 2 * INNER:3 * INNER], True, True).then_inc(v_full, 1)
                if kind == "max":
                    if j == 0:
                        pe.wait_ge(placed[p], (b - p) * 96 + 192)
                    if j >= 2:
                        pe.wait_ge(max_done, b * STEPS_A + j - 1)
                    else:
                        pe.wait_ge(v_ready, b * CHUNKS + CHUNKS - 1 + j)
                    h, c = j // CHUNKS, j % CHUNKS
                    T.matmul(psM[:, j % 2, :], QS[:, p, h, c * P:(c + 1) * P], KS[:, p, h, :], start=True, stop=True).then_inc(max_full, 1)
                if kind == "shift":
                    pe.wait_ge(shift_ready, b + 1)
                    T.transpose(psX[:, 0:P // 2].bitcast(F16)[0:STEPS_A, :], nm[:, :], ident16[:, :]).then_inc(shift_turned, 1)
                if kind == "turn":
                    pe.wait_ge(o_lo, b * CHUNKS + j + 1)
                    if not (known(b, 1) and j == 0):
                        pe.wait_ge(turn_done, b * CHUNKS + j)
                    for part in range(PARTS):
                        for i in range(CHUNKS):
                            last = T.transpose(psT[:, part, i, :], op[:, part, j, i * P:(i + 1) * P], ident16[:, :])
                    last.then_inc(turn_full, 1)
                if kind == "out":
                    if j == 0:
                        pe.wait_ge(turn_done, (b + 1) * CHUNKS)
                        pe.wait_ge(shiftT_ready, SEQS if isinstance(b, int) and b >= SEQS - 3 else b + 3)
                        if not known(b, 1):
                            pe.wait_ge(out_done, b)
                    for i in range(CHUNKS):
                        last = split_products(T, psX[:, j * D:(j + 1) * D], lambda part: OT[:, j, part, i, :],
                                              lambda part: wp[:, part, 3 * INNER + i * D:3 * INNER + (i + 1) * D],
                                              i == 0, i == CHUNKS - 1)
                    if j == CHUNKS - 1:
                        last.then_inc(out_full, 1)

            def values(b, p, n):
                h, c = n // CHUNKS, n % CHUNKS
                pe.wait_ge(p_lo, b * STEPS_A + n + 1)
                if c == 0 and not known(b * HEADS + h, 2):
                    pe.wait_ge(o_ready, b * HEADS + h - 1)
                for i in range(CHUNKS):
                    for x, (a, v) in enumerate(((HI, HI), (HI, LO), (LO, HI))):
                        last = T.matmul(psV[:, h % 2, i * (HEAD + 1):(i + 1) * (HEAD + 1)], pp[:, n % 4, a, i * P:(i + 1) * P],
                                        V1[:, p, v, c, h, :], start=(c == 0 and i == 0 and x == 0), stop=(c == CHUNKS - 1 and x == 2),
                                        skip_group_check=True)
                last.then_inc(av_done, 1)

            def first_scores(b, p):
                pe.wait_ge(shift_in[p], (b - p) * 8 + 16)
                score(b, p, 0)
                score(b, p, 1)

            def step(b, p, n):
                if known(b, 1) and n == 0:
                    first_scores(b, p)
                if ended(b):
                    values(b - 1, 1 - p, STEPS_A - 1)
                    return
                if n + 2 < STEPS_A:
                    score(b, p, n + 2)
                elif n + 2 == STEPS_A and not (isinstance(b, int) and b == SEQS - 1):
                    pe.wait_ge(shift_in[1 - p], (b + 1 - (1 - p)) * 8 + 16)
                    score(b + 1, 1 - p, 0)
                elif not (isinstance(b, int) and b == SEQS - 1):
                    score(b + 1, 1 - p, 1)
                if n > 0:
                    values(b, p, n - 1)
                elif not known(b, 1):
                    values(b - 1, 1 - p, STEPS_A - 1)

            pe.wait_ge(weights_ready, 1)
            pe.wait_ge(ones_ready, 2)
            pe.wait_ge(v_ones, 2)
            schedule(pe, task, step, tasks_first=True)

        @block.scalar
        def _(act):
            A = nc.scalar
            act.wait_ge(weights_in, 64)
            A.activation(wp[:, HI, 0:3 * INNER], raw[:, 0:3 * INNER], ACT.Copy, scale=QK_SCALE).then_inc(weights_hi, 1)
            A.activation(wp[:, HI, 3 * INNER:3 * INNER + CHUNKS * D], raw[:, 3 * INNER:3 * INNER + CHUNKS * D], ACT.Copy, scale=ATT_WO_SCALE).then_inc(weights_hi, 1)
            A.preload_act_table(ACT.Exp)

            def task(kind, j, b, p):
                if kind == "qk":
                    act.wait_ge(qk_full, b * 2 * PAIRS + j + 1)
                    if j == 0 and not known(b, 2):
                        act.wait_ge(placed[p], (b - p) * 96)
                    A.activation(qk[:, p, HI, j, :], psM[:, j % 2, :], ACT.Copy, scale=1.0 / (X_SCALE * QK_SCALE)).then_inc(qk_hi, 1)
                if kind == "v":
                    act.wait_ge(v_full, b * CHUNKS + j + 1)
                    A.activation(V1[:, p, HI, j, :, 0:HEAD], psM[:, j % 2, :].rearrange("p (h e) -> p h e", e=HEAD), ACT.Copy,
                                 scale=V_SCALE / (X_SCALE * QK_SCALE)).then_inc(v_hi, 1)
                if kind == "turned":
                    act.wait_ge(turn_full, b * CHUNKS + j + 1)
                    if not known(b, 1):
                        act.wait_ge(out_full, b)
                    A.activation(OT[:, j, :, :, :], psT[:, :, :, :], ACT.Copy).then_inc(turn_done, 1)

            def step(b, p, n):
                if ended(b):
                    return
                act.wait_ge(s_full, b * STEPS_A + n + 1)
                if not known(b * STEPS_A + n, 4):
                    act.wait_ge(av_done, b * STEPS_A + n - 3)
                A.activation(prob[:, n % 4, :], psS[:, n % 2, :], ACT.Exp, scale=HEAD ** -0.5, bias=gain[:, 0:1]).then_inc(p_full, 1)
                A.activation(pp[:, n % 4, HI, :], psS[:, n % 2, :], ACT.Exp, scale=HEAD ** -0.5, bias=gain[:, 0:1]).then_inc(p_ready, 1)

            act.wait_ge(gain_ready, 2)
            schedule(act, task, step)

        @block.gpsimd
        def _(pool):
            for p in range(2):
                nc.gpsimd.memset(K2[HEAD:HEAD + 1, p, :, :], SHIFT).then_inc(ones_ready, 1)

            def step(b, p, n):
                if ended(b):
                    return
                pool.wait_ge(p_full, b * STEPS_A + n + 1)
                pool.wait_ge(p_ready, b * STEPS_A + n + 1)
                nc.gpsimd.tensor_tensor(pp[:, n % 4, LO, :], prob[:, n % 4, :], pp[:, n % 4, HI, :], ALU.subtract).then_inc(p_lo, 1)

            def task(kind, j, b, p):
                if kind == "split":
                    pool.wait_ge(o_ready, (b + 1) * HEADS)
                    if not known(b, 1):
                        pool.wait_ge(turn_full, b * CHUNKS)
                    nc.gpsimd.tensor_tensor(op[:, HI, j, :], O[:, p, j, :], zero[:, :].broadcast_to([P, INNER]), ALU.add).then_inc(o_hi, 1)

            pool.wait_ge(ones_ready, 2)
            pool.wait_ge(consts_in, 16)
            b_b = b_out[:, :].rearrange("p (a d) -> p a d", a=1).broadcast_to([P, TILES, D])
            nc.gpsimd.tensor_tensor(H[:, :, :], H[:, :, :], b_b, ALU.add).then_inc(bias_added, 1)
            pool.wait_ge(bias_added, 1)
            pool.wait_ge(gain_ready, 2)
            schedule(pool, task, step, lag=1)

        @block.vector
        def _(dve):
            V = nc.vector
            V.memset(V1[:, :, HI, :, :, HEAD:], 1.0).then_inc(v_ones, 1)
            V.memset(V1[:, :, LO, :, :, HEAD:], 0.0).then_inc(v_ones, 1)
            V.memset(gain[:, :], PROB_GAIN).then_inc(gain_ready, 1)
            V.memset(zero[:, :], 0.0).then_inc(gain_ready, 1)
            dve.wait_ge(weights_hi, 2)
            for at, width, scale in ((0, 3 * INNER, QK_SCALE), (3 * INNER, CHUNKS * D, ATT_WO_SCALE)):
                last = V.scalar_tensor_tensor(wp[:, LO, at:at + width], raw[:, at:at + width], scale, wp[:, HI, at:at + width],
                                              ALU.mult, ALU.subtract)
            last.then_inc(weights_ready, 1)

            def task(kind, j, b, p):
                if kind == "qk":
                    dve.wait_ge(qk_hi, b * 2 * PAIRS + j + 1)
                    V.scalar_tensor_tensor(qk[:, p, LO, j, :], psM[:, j % 2, :], 1.0 / (X_SCALE * QK_SCALE), qk[:, p, HI, j, :],
                                           ALU.mult, ALU.subtract).then_inc(qk_lo, 1)
                if kind == "v":
                    dve.wait_ge(v_hi, b * CHUNKS + j + 1)
                    V.scalar_tensor_tensor(V1[:, p, LO, j, :, 0:HEAD], psM[:, j % 2, :].rearrange("p (h e) -> p h e", e=HEAD),
                                           V_SCALE / (X_SCALE * QK_SCALE), V1[:, p, HI, j, :, 0:HEAD],
                                           ALU.mult, ALU.subtract).then_inc(v_ready, 1)
                if kind == "max":
                    dve.wait_ge(max_full, b * STEPS_A + j + 1)
                    V.tensor_reduce(mx[:, j:j + 1], psM[:, j % 2, :], AX.X, ALU.max).then_inc(max_done, 1)
                if kind == "shift":
                    dve.wait_ge(max_done, (b + 1) * STEPS_A)
                    V.tensor_scalar(nm[:, :], mx[:, :], -1.0 / SHIFT, None, ALU.mult).then_inc(shift_ready, 1)
                    dve.wait_ge(shift_turned, b + 1)
                    if not known(b, 2):
                        dve.wait_ge(shift_in[p], (b - p) * 8)
                    V.tensor_copy(nmT[:, p, :], psX[:, 0:P // 2].bitcast(F16)[0:STEPS_A, :]).then_inc(shiftT_ready, 1)
                if kind == "split_low":
                    dve.wait_ge(o_hi, b * CHUNKS + j + 1)
                    V.tensor_tensor(op[:, LO, j, :], O[:, p, j, :], op[:, HI, j, :], ALU.subtract).then_inc(o_lo, 1)
                if kind == "out" and j == CHUNKS - 1:
                    dve.wait_ge(bias_added, 1)
                    dve.wait_ge(out_full, b + 1)
                    here = H[:, bass.ds(b * CHUNKS, CHUNKS), :].rearrange("p c d -> p (c d)")
                    V.scalar_tensor_tensor(here, psX[:, :], 1.0 / (V_SCALE * ATT_WO_SCALE), here, ALU.mult, ALU.add).then_inc(out_done, 1)

            def head_output(b, p, h):
                dve.wait_ge(av_done, b * STEPS_A + (h + 1) * CHUNKS)
                if h == 0 and not known(b, 2):
                    dve.wait_ge(o_lo, (b - 1) * CHUNKS)
                sums = psV[:, h % 2, 0:CHUNKS * (HEAD + 1)].rearrange("p (c e) -> p c e", e=HEAD + 1)
                if not known(b * HEADS + h, 2):
                    dve.wait_ge(o_ready, b * HEADS + h - 1)
                V.reciprocal(rec[:, h % 2, :], sums[:, :, HEAD]).then_inc(rec_ready, 1)
                dve.wait_ge(rec_ready, b * HEADS + h + 1)
                V.tensor_tensor(O[:, p, :, h * HEAD:(h + 1) * HEAD], sums[:, :, 0:HEAD],
                                rec[:, h % 2, :].rearrange("p (c a) -> p c a", a=1).broadcast_to([P, CHUNKS, HEAD]), ALU.mult).then_inc(o_ready, 1)

            def step(b, p, n):
                if n > 0 and n % CHUNKS == 0:
                    head_output(b, p, n // CHUNKS - 1)
                elif n == 0 and not known(b, 1):
                    head_output(b - 1, 1 - p, HEADS - 1)

            schedule(dve, task, step, tasks_first=True)


GATE_HIDDEN = D // 2
EXPERT_HIDDEN = 2 * D
BLOCKS = EXPERT_HIDDEN // P
W1_SCALE = 2.0 ** 8
G_SCALE = 2.0 ** 6
W2_SCALE = 2.0 ** 8


def route_gated(nc, H, XT, ident, d, combine):
    COLS = 32
    with ExitStack() as ctx:
        m = Memory(nc, "gate", ctx)
        gw1 = m.sbuf("gw1", [P, GATE_HIDDEN])
        gwp = m.sbuf("gw1_parts", [P, PARTS, GATE_HIDDEN], F16)
        gb1 = m.sbuf("gb1", [GATE_HIDDEN, 1])
        gw2 = m.sbuf("gw2", [GATE_HIDDEN, EXPERTS])
        gb2 = m.sbuf("gb2", [P, EXPERTS])
        rank = m.sbuf("rank", [P, EXPERTS])
        bias_blocks = m.sbuf("bias_blocks", [P, CHUNKS * D])
        hidden = m.sbuf("hidden", [GATE_HIDDEN, 2, SEQ])
        scores = m.sbuf("scores", [P, TILES, EXPERTS])
        first = m.sbuf("first", [P, TILES, EXPERTS])
        second = m.sbuf("second", [P, TILES, EXPERTS])
        per_token = m.sbuf("per_token", [P, 5, TILES])
        m1, m2, e, r1, work = (per_token[:, n, :] for n in range(5))
        record = m.sbuf("record", [P, TILES, COLS])
        rows = m.sbuf("rows", [P, SEQS, P])
        psG = m.psum("psG", [P, 2, SEQ])
        psL = m.psum("psL", [P, 512])
        psR = m.psum("psR", [P, SEQS, P])
        psB = m.psum("psB", [P, 2, CHUNKS * D])
        (params_in, w_hi, w_parts, cleared, bias_in, hidden_psum, hidden_ready, logits_psum, own_sem, shifted, exped, gap_ready,
         exp_ready, record_ready, rows_psum, rows_ready, bias_psum, bias_added) = (m.sem(n) for n in (
             "params_in", "w_hi", "w_parts", "cleared", "bias_in", "hidden_psum", "hidden_ready", "logits_psum", "own", "shifted",
             "exped", "gap_ready", "exp_ready", "record_ready", "rows_psum", "rows_ready", "bias_psum", "bias_added"))
        block = ctx.enter_context(nc.Block())

        @block.sync
        def _(sp):
            for to, name in ((gw1, "gw1"), (gb1, "gb1"), (gw2, "gw2"), (gb2, "gb2"), (rank, "rank")):
                sp.dma_start(to[:, :], d[name]).then_inc(params_in, 16)
            load_bias_blocks(sp, bias_blocks, d["be2"], cleared, bias_in)

        @block.scalar
        def _(act):
            A = nc.scalar
            act.wait_ge(params_in, 80)
            A.activation(gwp[:, HI, :], gw1[:, :], ACT.Copy, scale=W_SCALE_ROUTER).then_inc(w_hi, 1)

            def relu(b, p, first_use):
                act.wait_ge(hidden_psum, b + 1)
                if not first_use:
                    act.wait_ge(logits_psum, b - 1)
                A.activation(hidden[:, p, :], psG[0:GATE_HIDDEN, p, :], ACT.Relu, bias=gb1[:, 0:1],
                             scale=1.0 / (X_SCALE * W_SCALE_ROUTER)).then_inc(hidden_ready, 1)

            relu(0, 0, True)
            relu(1, 1, True)
            with act.Fori(1, SEQS // 2) as i:
                for p in range(2):
                    relu(i * 2 + p, p, False)
            act.wait_ge(shifted, 1)
            A.activation(first[:, :, :], scores[:, :, :], ACT.Exp).then_inc(exped, 1)
            act.wait_ge(gap_ready, 1)
            A.activation(e[:, :], e[:, :], ACT.Exp).then_inc(exp_ready, 1)
            act.wait_ge(rows_psum, 1)
            A.activation(rows[:, :, :], psR[:, :, :], ACT.Copy).then_inc(rows_ready, 1)

        @block.tensor
        def _(pe):
            pe.wait_ge(w_parts, 1)

            def hidden_product(b, p):
                split_products(nc.tensor, psG[0:GATE_HIDDEN, p, :], lambda part: gwp[:, part, :],
                               lambda part: XT[:, bass.ds(b, 1), part, :].rearrange("p a n -> p (a n)"), True, True).then_inc(hidden_psum, 1)

            def logits_product(b, p):
                pe.wait_ge(hidden_ready, b + 1)
                for c in range(CHUNKS):
                    last = nc.tensor.matmul(psL[:, bass.ds((b * CHUNKS + c) * EXPERTS, EXPERTS)],
                                            hidden[:, p, c * P:(c + 1) * P], gw2[:, :], start=True, stop=True)
                last.then_inc(logits_psum, 1)

            hidden_product(0, 0)
            hidden_product(1, 1)
            with pe.Fori(0, SEQS // 2 - 1) as i:
                for p in range(2):
                    logits_product(i * 2 + p, p)
                    hidden_product(i * 2 + p + 2, p)
            logits_product(SEQS - 2, 0)
            logits_product(SEQS - 1, 1)
            pe.wait_ge(record_ready, 1)
            for b in range(SEQS):
                last = nc.tensor.transpose(psR[:, b, :], record[:, b * CHUNKS:(b + 1) * CHUNKS, :].rearrange("p c j -> p (c j)"), ident[:, :])
            last.then_inc(rows_psum, 1)
            pe.wait_ge(rows_ready, 1)
            pe.wait_ge(bias_in, 16 * CHUNKS)
            for b in range(SEQS):
                if b >= 2:
                    pe.wait_ge(bias_added, b - 1)
                nc.tensor.matmul(psB[:, b % 2, :], rows[:, b, :], bias_blocks[:, :], start=True, stop=True).then_inc(bias_psum, 1)

        @block.vector
        def _(dve):
            V = nc.vector
            own = Chain(dve, own_sem)
            V.memset(bias_blocks[:, :], 0.0).then_inc(cleared, 1)
            own(V.memset(record[:, :, EXPERTS:], 0.0))
            dve.wait_ge(params_in, 80)
            dve.wait_ge(w_hi, 1)
            V.scalar_tensor_tensor(gwp[:, LO, :], gw1[:, :], W_SCALE_ROUTER, gwp[:, HI, :], ALU.mult, ALU.subtract).then_inc(w_parts, 1)
            dve.wait_ge(logits_psum, SEQS)
            gb2_b = gb2[:, :].rearrange("p (a e) -> p a e", a=1).broadcast_to([P, TILES, EXPERTS])
            wide = lambda x: x.rearrange("p (t a) -> p t a", a=1).broadcast_to([P, TILES, EXPERTS])
            own.link(V.tensor_tensor(scores[:, :, :], psL[:, 0:TILES * EXPERTS].rearrange("p (t e) -> p t e", e=EXPERTS), gb2_b, ALU.add))
            own.link(V.tensor_reduce(m1[:, :], scores[:, :, :], AX.X, ALU.max))
            V.tensor_tensor(scores[:, :, :], scores[:, :, :], wide(m1[:, :]), ALU.subtract).then_inc(shifted, 1)
            dve.wait_ge(exped, 1)
            own.link(V.tensor_reduce(work[:, :], first[:, :, :], AX.X, ALU.add))
            own.link(V.reciprocal(work[:, :], work[:, :]))
            own.link(V.tensor_tensor(scores[:, :, :], first[:, :, :], wide(work[:, :]), ALU.mult))
            top_two(V, own, scores[:, :, :], rank[:, :], first[:, :, :], second[:, :, :], m1[:, :], m2[:, :], work[:, :])
            V.tensor_tensor(e[:, :], m2[:, :], m1[:, :], ALU.subtract).then_inc(gap_ready, 1)
            dve.wait_ge(exp_ready, 1)
            own.link(V.tensor_scalar(r1[:, :], e[:, :], 1.0, None, ALU.add))
            own.link(V.reciprocal(r1[:, :], r1[:, :]))
            own(V.tensor_tensor(e[:, :], e[:, :], r1[:, :], ALU.mult))
            own.link(V.tensor_tensor(first[:, :, :], first[:, :, :], wide(r1[:, :]), ALU.mult))
            own.link(V.tensor_tensor(second[:, :, :], second[:, :, :], wide(e[:, :]), ALU.mult))
            own.link(V.tensor_tensor(record[:, :, 0:EXPERTS], first[:, :, :], second[:, :, :], ALU.add))
            V.tensor_scalar(combine[:, :, :], record[:, :, 0:EXPERTS], 1.0 / (G_SCALE * W2_SCALE), None, ALU.mult).then_inc(record_ready, 1)
            for b in range(SEQS):
                dve.wait_ge(bias_psum, b + 1)
                here = H[:, b * CHUNKS:(b + 1) * CHUNKS, :].rearrange("p c d -> p (c d)")
                V.tensor_tensor(here, psB[:, b % 2, :], here, ALU.add).then_inc(bias_added, 1)


def gated_experts(nc, H, XT, d, combine):
    BW = BLOCKS * D
    with ExitStack() as ctx:
        m = Memory(nc, "ffn", ctx)
        raw1 = m.sbuf("w1", [P, EXPERTS, BW])
        raw2 = m.sbuf("w2", [P, EXPERTS, BLOCKS, D])
        w1 = m.sbuf("w1_parts", [P, PARTS, EXPERTS, BW], F16)
        w2 = m.sbuf("w2_parts", [P, PARTS, EXPERTS, BW], F16)
        b1 = m.sbuf("b1", [P, EXPERTS * BLOCKS])
        act_out = m.sbuf("gelu", [P, 2, BLOCKS, SEQ])
        gp = m.sbuf("gelu_parts", [P, 2, PARTS, BLOCKS, SEQ], F16)
        psH = m.psum("psH", [P, 2, BLOCKS, SEQ])
        psY = m.psum("psY", [P, 2, CHUNKS * D])
        weights_in = [m.sem(f"weights_in{e}") for e in range(EXPERTS)]
        bias_in = m.sem("bias_in")
        hi_weights, weights_ready, h_psum, gelu_ready, hi_ready, lo_ready, y_psum, y_added = (m.sem(n) for n in (
            "hi_weights", "weights_ready", "h_psum", "gelu_ready", "hi_ready", "lo_ready", "y_psum", "y_added"))
        block = ctx.enter_context(nc.Block())
        known = lambda u, least: isinstance(u, int) and u < least

        @block.sync
        def _(sp):
            sp.dma_start(b1[:, :], d["be1"]).then_inc(bias_in, 16)
            for e in range(EXPERTS):
                sp.dma_start(raw1[:, e, :], d["we1"][e * P:(e + 1) * P, :]).then_inc(weights_in[e], 16)
                sp.dma_start(raw2[:, e, :, :], d["we2"][e * EXPERT_HIDDEN:(e + 1) * EXPERT_HIDDEN, :].rearrange("(j p) d -> p j d", p=P)).then_inc(weights_in[e], 16)

        @block.tensor
        def _(pe):
            def up(b, e):
                if known(b, 1):
                    pe.wait_ge(weights_ready, e + 1)
                if not known(b * EXPERTS + e, 2):
                    pe.wait_ge(gelu_ready, (b * EXPERTS + e - 1) * BLOCKS)
                for j in range(BLOCKS):
                    split_products(nc.tensor, psH[:, e % 2, j, :], lambda part: w1[:, part, e, j * P:(j + 1) * P],
                                   lambda part: XT[:, bass.ds(b, 1), part, :].rearrange("p a n -> p (a n)"), True, True).then_inc(h_psum, 1)

            def down(b, e):
                u = b * EXPERTS + e
                pe.wait_ge(lo_ready, u + 1)
                if not known(u, 2):
                    pe.wait_ge(y_added, u - 1)
                for c in range(CHUNKS):
                    for j in range(BLOCKS):
                        last = split_products(nc.tensor, psY[:, e % 2, c * D:(c + 1) * D], lambda part: gp[:, e % 2, part, j, c * P:(c + 1) * P],
                                              lambda part: w2[:, part, e, j * D:(j + 1) * D], j == 0, j == BLOCKS - 1)
                last.then_inc(y_psum, 1)

            def sequence(b, last):
                for e in range(EXPERTS):
                    if e + 2 < EXPERTS:
                        up(b, e + 2)
                    elif not last:
                        up(b + 1, e + 2 - EXPERTS)
                    down(b, e)

            up(0, 0)
            up(0, 1)
            sequence(0, False)
            with pe.Fori(1, SEQS - 1) as b:
                sequence(b, False)
            sequence(SEQS - 1, True)

        @block.scalar
        def _(act):
            A = nc.scalar
            A.preload_act_table(ACT.Gelu)
            for e in range(EXPERTS):
                act.wait_ge(weights_in[e], 32)
                A.activation(w1[:, HI, e, :], raw1[:, e, :], ACT.Copy, scale=W1_SCALE).then_inc(hi_weights, 1)
                A.activation(w2[:, HI, e, :], raw2[:, e, :, :].rearrange("p j d -> p (j d)"), ACT.Copy, scale=W2_SCALE).then_inc(hi_weights, 1)
            act.wait_ge(bias_in, 16)

            def sequence(b):
                for e in range(EXPERTS):
                    u = b * EXPERTS + e
                    if not known(u, 2):
                        act.wait_ge(lo_ready, u - 1)
                    for j in range(BLOCKS):
                        act.wait_ge(h_psum, u * BLOCKS + j + 1)
                        A.activation(act_out[:, e % 2, j, :], psH[:, e % 2, j, :], ACT.Gelu, bias=b1[:, e * BLOCKS + j:e * BLOCKS + j + 1],
                                     scale=1.0 / (X_SCALE * W1_SCALE)).then_inc(gelu_ready, 1)
                    act.wait_ge(gelu_ready, (u + 1) * BLOCKS)
                    if not known(u, 2):
                        act.wait_ge(y_psum, u - 1)
                    A.activation(gp[:, e % 2, HI, :, :], act_out[:, e % 2, :, :], ACT.Copy, scale=G_SCALE).then_inc(hi_ready, 1)

            sequence(0)
            with act.Fori(1, SEQS) as b:
                sequence(b)

        @block.vector
        def _(dve):
            V = nc.vector
            for e in range(EXPERTS):
                dve.wait_ge(hi_weights, 2 * (e + 1))
                V.scalar_tensor_tensor(w1[:, LO, e, :], raw1[:, e, :], W1_SCALE, w1[:, HI, e, :], ALU.mult, ALU.subtract)
                V.scalar_tensor_tensor(w2[:, LO, e, :], raw2[:, e, :, :].rearrange("p j d -> p (j d)"), W2_SCALE, w2[:, HI, e, :],
                                       ALU.mult, ALU.subtract).then_inc(weights_ready, 1)

            def low(b, e):
                dve.wait_ge(hi_ready, b * EXPERTS + e + 1)
                V.scalar_tensor_tensor(gp[:, e % 2, LO, :, :], act_out[:, e % 2, :, :], G_SCALE, gp[:, e % 2, HI, :, :],
                                       ALU.mult, ALU.subtract).then_inc(lo_ready, 1)

            def add(b, e):
                u = b * EXPERTS + e
                dve.wait_ge(y_psum, u + 1)
                if not known(u, 1):
                    dve.wait_ge(y_added, u)
                for c in range(CHUNKS):
                    here = H[:, bass.ds(b * CHUNKS + c, 1), :].rearrange("p a d -> p (a d)")
                    last = V.scalar_tensor_tensor(here, psY[:, e % 2, c * D:(c + 1) * D],
                                                  combine[:, bass.ds(b * CHUNKS + c, 1), e:e + 1].rearrange("p a b -> p (a b)"),
                                                  here, ALU.mult, ALU.add)
                last.then_inc(y_added, 1)

            def sequence(b, last):
                for e in range(EXPERTS):
                    if e + 1 < EXPERTS:
                        low(b, e + 1)
                    elif not last:
                        low(b + 1, 0)
                    add(b, e)

            low(0, 0)
            sequence(0, False)
            with dve.Fori(1, SEQS - 1) as b:
                sequence(b, False)
            sequence(SEQS - 1, True)


def store(nc, H, out):
    with ExitStack() as ctx:
        m = Memory(nc, "store", ctx)
        stored = m.sem("stored")
        block = ctx.enter_context(nc.Block())

        @block.sync
        def _(sp):
            sp.dma_start(out.rearrange("b (c p) d -> p (b c) d", p=P), H[:, :, :]).then_inc(stored, 16)
            sp.wait_ge(stored, 16)


def build_program(nc, d, out):
    with ExitStack() as ctx:
        m = Memory(nc, "model", ctx)
        H = m.sbuf("h", [P, TILES, D])
        ident = m.sbuf("ident", [P, P])
        ident16 = m.sbuf("ident16", [P, P], F16)
        combine = m.sbuf("combine", [P, TILES, EXPERTS])
        XT = m.sbuf("xT", [P, SEQS, PARTS, SEQ], F16)
        mask_rows = nc.dram_tensor("mask_rows", (2 * EXPERTS, SEQS * SEQ), F16).ap()
        embed_and_convolve(nc, H, ident, ident16, d)
        normalize(nc, "norm2", H, XT, ident16)
        route_recurrent(nc, H, XT, ident, d, combine, mask_rows)
        recurrent_experts(nc, H, XT, d, combine, mask_rows)
        normalize(nc, "norm3", H, XT, ident16)
        attention(nc, H, XT, ident16, d)
        normalize(nc, "norm4", H, XT, ident16)
        route_gated(nc, H, XT, ident, d, combine)
        gated_experts(nc, H, XT, d, combine)
        store(nc, H, out)


def dft_matrices():
    import numpy as np

    n, half = SEQ, SEQ // 2
    angle = 2 * np.pi * (np.outer(np.arange(n), np.arange(half)) % n) / n
    sign = (-1.0) ** np.arange(n)
    forward = np.concatenate([np.cos(angle), -np.sin(angle)], axis=1)
    forward[:, half] = sign
    inverse = 2 * forward.T / n
    inverse[[0, half]] /= 2
    return forward.astype(np.float32), np.ascontiguousarray(inverse).astype(np.float32)


def kernel(**inputs):
    import numpy as np
    import concourse.bacc as bacc
    from concourse.bass_utils import run_bass_kernel_spmd

    x = {name: np.asarray(a) for name, a in inputs.items()}
    fwd, inv = dft_matrices()
    rows = lambda a: np.ascontiguousarray(np.broadcast_to(a, (P,) + a.shape))
    positions = np.concatenate([np.arange(32), np.arange(0, SEQ, 32), [0.5]]).astype(np.float32)
    arrays = {
        "ids": np.ascontiguousarray(x["x"].reshape(TILES, P).T),
        "table": np.concatenate([x["L0_tok_fine_embed_w"], x["L0_tok_loc_to_cluster_w"].T], axis=1),
        "coarse_w": x["L0_tok_coarse_embed_w"],
        "cluster_b": rows(x["L0_tok_loc_to_cluster_b"]),
        "A_re": x["L0_attn_A_real"], "A_im": x["L0_attn_A_imag"], "B_in": x["L0_attn_B"], "C_in": x["L0_attn_C"],
        "delta": x["L0_attn_delta"].reshape(P, 1),
        "positions": rows(positions), "dft": fwd, "inverse_dft": inv, "ident": np.eye(P, dtype=np.float32),
        "ident16": np.eye(P, dtype=np.float16),
        "rank": rows(np.arange(EXPERTS, 0, -1, dtype=np.float32)),
        "w_q": x["L1_attn_w_q"], "w_k": x["L1_attn_w_k"], "w_v": x["L1_attn_w_v"], "w_out": x["L1_attn_w_out"],
        "b_out": rows(x["L1_attn_b_out"]),
        "router_w": x["L0_ffn_router_w"], "router_b": rows(x["L0_ffn_router_b"]),
        "Wi": x["L0_ffn_Wi"].reshape(EXPERTS * D, GATES * D), "Wh": x["L0_ffn_Wh"].reshape(EXPERTS * D, GATES * D),
        "Wo": x["L0_ffn_Wo"].reshape(EXPERTS * D, D), "bo": x["L0_ffn_bo"],
        "gw1": x["L1_ffn_gw1"], "gb1": x["L1_ffn_gb1"].reshape(GATE_HIDDEN, 1), "gw2": x["L1_ffn_gw2"], "gb2": rows(x["L1_ffn_gb2"]),
        "we1": x["L1_ffn_we1"].reshape(EXPERTS * D, EXPERT_HIDDEN), "we2": x["L1_ffn_we2"].reshape(EXPERTS * EXPERT_HIDDEN, D),
        "be1": np.ascontiguousarray(x["L1_ffn_be1"].reshape(EXPERTS * BLOCKS, P).T), "be2": x["L1_ffn_be2"],
        "lstm_b": np.ascontiguousarray(x["L0_ffn_b"].reshape(EXPERTS * GATES, D).T),
    }
    nc = bacc.Bacc("TRN2", target_bir_lowering=False, num_devices=1)
    d = {n: nc.dram_tensor(f"in_{n}", a.shape, mybir.dt.from_np(a.dtype), kind="ExternalInput").ap() for n, a in arrays.items()}
    out = nc.dram_tensor("out", (SEQS, SEQ, D), F32, kind="ExternalOutput").ap()
    build_program(nc, d, out)
    r = run_bass_kernel_spmd(nc, [{f"in_{n}": a for n, a in arrays.items()}], core_ids=[0])
    return r.results[0]["out"]
```

```python
from contextlib import ExitStack

import concourse.bass as bass
from concourse import mybir

P = 128
TILES, D = 32, 128
SEQS, SEQ = 8, 512
CHUNKS = SEQ // P
STATES = 16
HALF_D = D // 2
F32, F16, I32 = mybir.dt.float32, mybir.dt.float16, mybir.dt.int32
ACT, ALU, AX = mybir.ActivationFunctionType, mybir.AluOpType, mybir.AxisListType
EPS = 1e-5


class Chain:

    def __init__(self, engine, sem, base=0):
        self.engine, self.sem, self.base, self.n = engine, sem, base, 0

    def __call__(self, instruction):
        instruction.then_inc(self.sem, 1)
        self.n += 1

    def done(self, back=0):
        self.engine.wait_ge(self.sem, self.base + (self.n - back))

    def link(self, instruction):
        self(instruction)
        self.done()


class Memory:

    def __init__(self, nc, stage, ctx):
        self.nc, self.stage, self.ctx, self.sems = nc, stage, ctx, []
        ctx.callback(self.clear)

    def sbuf(self, name, shape, dtype=F32):
        return self.ctx.enter_context(self.nc.sbuf_tensor(f"{self.stage}_{name}", shape, dtype))

    def psum(self, name, shape, dtype=F32):
        return self.ctx.enter_context(self.nc.psum_tensor(f"{self.stage}_{name}", shape, dtype))

    def sem(self, name):
        self.sems.append(self.nc.alloc_semaphore(f"{self.stage}_{name}"))
        return self.sems[-1]

    def clear(self):
        if self.sems:
            self.nc.clear_and_free_semaphores(self.sems)
            self.nc.all_engine_barrier()


def token_statistics(nc, dve, chain, H, stats, mean, var, scratch):
    for t in range(TILES):
        chain(nc.vector.bn_stats(stats[:, t, :], H[:, t, :]))
    chain.done()
    chain(nc.vector.tensor_tensor(mean, stats[:, :, 1], stats[:, :, 4], ALU.add))
    chain(nc.vector.tensor_tensor(scratch, stats[:, :, 1], stats[:, :, 4], ALU.subtract))
    chain(nc.vector.tensor_tensor(var, stats[:, :, 2], stats[:, :, 5], ALU.add))
    chain.done()
    chain(nc.vector.tensor_scalar(mean, mean, 0.5, None, ALU.mult))
    chain(nc.vector.scalar_tensor_tensor(scratch, scratch, 0.25, scratch, ALU.mult, ALU.mult))
    chain.done()
    return nc.vector.scalar_tensor_tensor(var, var, 1.0 / D, scratch, ALU.mult, ALU.add)


def embed_and_convolve(nc, H, ident, ident16, d):
    NPOS = d["positions"].shape[1]
    FINE_STEP = 32
    NA, NR = SEQ // FINE_STEP, FINE_STEP
    TWO_PI = 6.283185307179586
    TWO_PI_HI = 6.28125
    ROUND = 1.5 * 2.0 ** 23
    GROUPS, GT = 4, TILES // 4
    SLOTS = 4

    with ExitStack() as ctx:
        m = Memory(nc, "conv", ctx)
        idx = m.sbuf("ids", [P, TILES], I32)
        cb = m.sbuf("cluster_b", [P, HALF_D])
        cw = m.sbuf("coarse_w", [P, D])
        fwd = m.sbuf("dft", [P, CHUNKS, SEQ])
        inv = m.sbuf("inverse_dft", [P, SLOTS, SEQ])
        par = m.sbuf("ssm_params", [P, 4, STATES])
        delta = m.sbuf("delta", [P, 1])
        pos = m.sbuf("positions", [P, NPOS])
        U = m.sbuf("u", [P, TILES, D])
        logits = m.sbuf("logits", [P, GT, HALF_D])
        top = m.sbuf("top", [P, GT])
        total = m.sbuf("total", [P, GT])
        dist = m.sbuf("dist", [P, GT, HALF_D])
        distT = m.sbuf("distT", [P, GT // 2, P])
        dtA = m.sbuf("dtA", [P, 2, STATES])
        phase = m.sbuf("phase", [P, NPOS, STATES])
        turns = m.sbuf("turns", [P, NPOS, STATES])
        sin = m.sbuf("sin", [P, NPOS, STATES])
        cos = m.sbuf("cos", [P, NPOS, STATES])
        mag = m.sbuf("mag", [P, NPOS, STATES])
        small = m.sbuf("small", [P, 16, STATES])
        fine = m.sbuf("fine", [P, NR, 2 * STATES])
        rough = m.sbuf("rough", [P, NA, 2 * STATES])
        prod = m.sbuf("prod", [P, NA // 4, NR, 2 * STATES])
        K = m.sbuf("k", [P, SEQ])
        KT = m.sbuf("kT", [P, CHUNKS, D])
        Kr = m.sbuf("k_re", [P, 2, 2, D])
        Krn = m.sbuf("k_re_nyquist", [P, 2, D])
        Ki = m.sbuf("k_im", [P, 2, 2, D])
        stats = m.sbuf("stats", [P, TILES, 6])
        mean = m.sbuf("mean", [P, TILES])
        offset = m.sbuf("offset", [P, TILES])
        var = m.sbuf("var", [P, TILES])
        tmp = m.sbuf("tmp", [P, TILES])
        eps = m.sbuf("eps", [P, 1])
        terms = m.sbuf("terms", [P, 2, 12, 512])
        Y = m.sbuf("y", [P, 2, SLOTS, 2, 512])

        flat = prod[:, :, :, :].rearrange("p a r n -> p (a r n)")
        sums = lambda parity, n: flat[:, (4 * parity + n) * 512:(4 * parity + n + 1) * 512]

        ps = m.psum("ps", [P, 8, 512])

        idx_in, params_in, cw_in, dft_in, inv_in, idn_in = (m.sem(n) for n in (
            "idx_in", "params_in", "cw_in", "dft_in", "inv_in", "ident_in"))
        gathered = [m.sem(f"gathered{g}") for g in range(GROUPS)]
        shifted, exped, dist_ready, turned, distT_ready, coarse_done, coarse_in_h = (m.sem(n) for n in (
            "shifted", "exped", "dist_ready", "turned", "distT_ready", "coarse_done", "coarse_in_h"))
        tanh_ready, mag_in, mag_ready, trig_in, trig_ready, k_ready, kT_psum, kT_ready, kf_psum, kf_ready = (
            m.sem(n) for n in ("tanh_ready", "mag_in", "mag_ready", "trig_in", "trig_ready", "k_ready",
                               "kT_psum", "kT_ready", "kf_psum", "kf_ready"))
        u_ready = [m.sem(f"u_ready{half}") for half in range(2)]
        var_ready, std_ready, eps_ready, cw_cleared = (m.sem(n) for n in ("var_ready", "std_ready", "eps_ready", "cw_cleared"))
        spectrum, terms_ready, y_ready, dve_sums, pool_sums, offset_ready, out_psum, out_done, dve_own = (m.sem(n) for n in (
            "spectrum", "terms_ready", "y_ready", "dve_sums", "pool_sums", "offset_ready", "out_psum", "out_done", "dve_own"))

        block = ctx.enter_context(nc.Block())

        @block.sync
        def _(sp):
            sp.dma_start(idx[:, :], d["ids"]).then_inc(idx_in, 16)
            for n, source in enumerate((d["A_re"], d["A_im"], d["B_in"], d["C_in"])):
                sp.dma_start(par[:, n, :], source).then_inc(params_in, 16)
            sp.dma_start(delta[:, :], d["delta"]).then_inc(params_in, 16)
            sp.dma_start(pos[:, :], d["positions"]).then_inc(params_in, 16)
            sp.dma_start(cb[:, :], d["cluster_b"]).then_inc(cw_in, 16)
            sp.wait_ge(cw_cleared, 1)
            for half in range(2):
                here = slice(HALF_D * half, HALF_D * (half + 1))
                sp.dma_start(cw[here, here], d["coarse_w"]).then_inc(cw_in, 16)
            sp.dma_start(ident[:, :], d["ident"]).then_inc(idn_in, 16)
            sp.dma_start(ident16[:, :], d["ident16"]).then_inc(idn_in, 16)
            sp.dma_start(fwd[:, :, :], d["dft"].rearrange("(c p) f -> p c f", p=P)).then_inc(dft_in, 16)
            sp.dma_start(inv[:, :, :], d["inverse_dft"].rearrange("(c p) l -> p c l", p=P)).then_inc(inv_in, 16)

        @block.gpsimd
        def _(pool):
            pool.wait_ge(idx_in, 16)
            for t in range(TILES):
                pool.indirect_dma_start(
                    out=H[:, t, :], out_offset=None, in_=d["table"],
                    in_offset=bass.IndirectOffsetOnAxis(ap=idx[:, t:t + 1], axis=0),
                ).then_inc(gathered[t // GT], 16)
            for u in range(4):
                half, b, p = u // 2, u % 2, u % 2
                if u >= 1:
                    pool.wait_ge(pool_sums, 6 * u)
                for n, (x, y, op) in enumerate(((4, 5, ALU.subtract), (6, 7, ALU.subtract), (8, 9, ALU.add), (10, 11, ALU.add))):
                    pool.wait_ge(terms_ready, 12 * u + y + 1)
                    nc.gpsimd.tensor_tensor(sums(p, n), terms[:, p, x, :], terms[:, p, y, :], op).then_inc(pool_sums, 1)
                    if n % 2:
                        pool.wait_ge(pool_sums, 6 * u + (2 if n == 1 else 5))
                        nc.gpsimd.tensor_tensor(Y[:, half, (0, 2)[n // 2] + b, 1, :], sums(p, n - 1), sums(p, n),
                                                ALU.add).then_inc(pool_sums, 1)

        @block.scalar
        def _(act):
            act.wait_ge(mag_in, 1)
            nc.scalar.activation(small[:, 0, :], dtA[:, 0, :], ACT.Tanh, scale=0.5).then_inc(tanh_ready, 1)
            nc.scalar.activation(mag[:, :, :], mag[:, :, :], ACT.Exp).then_inc(mag_ready, 1)
            act.wait_ge(trig_in, 2)
            nc.scalar.activation(sin[:, :, :], phase[:, :, :], ACT.Sin).then_inc(trig_ready, 1)
            nc.scalar.activation(cos[:, :, :], turns[:, :, :], ACT.Sin).then_inc(trig_ready, 1)
            for g in range(GROUPS):
                act.wait_ge(shifted, g + 1)
                if g >= 1:
                    act.wait_ge(dist_ready, g)
                nc.scalar.activation(dist[:, :, :], logits[:, :, :], ACT.Exp).then_inc(exped, 1)
                act.wait_ge(turned, g + 1)
                if g >= 1:
                    act.wait_ge(coarse_done, g)
                nc.scalar.activation(distT[:, :, :], ps[:, 0, :], ACT.Copy).then_inc(distT_ready, 1)
                act.wait_ge(coarse_done, g + 1)
                nc.scalar.activation(H[:, g * GT:(g + 1) * GT, HALF_D:D],
                                     ps[:, 1, :].rearrange("p (t c) -> p t c", c=HALF_D), ACT.Copy).then_inc(coarse_in_h, 1)
            act.wait_ge(kT_psum, 1)
            nc.scalar.activation(KT[:, :, :], ps[:, 2, :], ACT.Copy).then_inc(kT_ready, 1)
            act.wait_ge(kf_psum, 1)
            for w in range(2):
                bank = ps[:, 3 + w, :].rearrange("p (s d) -> p s d", d=D)
                nc.scalar.activation(Kr[:, w, :, :], bank[:, 0:2, :], ACT.Copy).then_inc(kf_ready, 1)
                nc.scalar.activation(Ki[:, w, :, :], bank[:, 2:4, :], ACT.Copy).then_inc(kf_ready, 1)
                nc.scalar.activation(Krn[:, w, :], bank[:, 0, :], ACT.Copy).then_inc(kf_ready, 1)
            act.wait_ge(var_ready, 1)
            act.wait_ge(eps_ready, 1)
            nc.scalar.activation(var[:, :], var[:, :], ACT.Sqrt, bias=eps[:, 0:1]).then_inc(std_ready, 1)
            act.wait_ge(offset_ready, 1)
            for t in range(TILES // 2, TILES):
                last = nc.scalar.activation(U[:, t, :], H[:, t, :], ACT.Identity, bias=offset[:, t:t + 1], scale=var[:, t:t + 1])
            last.then_inc(u_ready[1], 1)

        @block.tensor
        def _(pe):
            pe.wait_ge(idn_in, 32)
            pe.wait_ge(cw_in, 48)
            for g in range(GROUPS):
                pe.wait_ge(dist_ready, g + 1)
                if g >= 1:
                    pe.wait_ge(distT_ready, g)
                for t in range(GT // 2):
                    last = nc.tensor.transpose(ps[:, 0, t * P:(t + 1) * P],
                                               dist[:, 2 * t:2 * t + 2, :].rearrange("p t c -> p (t c)"), ident[:, :])
                last.then_inc(turned, 1)
                pe.wait_ge(distT_ready, g + 1)
                if g >= 1:
                    pe.wait_ge(coarse_in_h, g)
                for t in range(GT // 2):
                    last = nc.tensor.matmul(ps[:, 1, t * D:(t + 1) * D], distT[:, t, :], cw[:, :], start=True, stop=True)
                last.then_inc(coarse_done, 1)
            pe.wait_ge(k_ready, 1)
            for c in range(CHUNKS):
                last = nc.tensor.transpose(ps[:, 2, c * P:(c + 1) * P], K[:, c * P:(c + 1) * P], ident[:, :])
            last.then_inc(kT_psum, 1)
            pe.wait_ge(kT_ready, 1)
            pe.wait_ge(dft_in, 16)
            for w, chunks in enumerate((2, 4)):
                for s in range(SLOTS):
                    for c in range(chunks):
                        last = nc.tensor.matmul(ps[:, 3 + w, s * D:(s + 1) * D], fwd[:, c, s * P:(s + 1) * P], KT[:, c, :],
                                                start=(c == 0), stop=(c == chunks - 1))
            last.then_inc(kf_psum, 1)
            pe.wait_ge(kf_ready, 6)
            Uv = U[:, :, :].rearrange("p (b c) d -> p b c d", c=CHUNKS)
            for u in range(4):
                half, b, bank = u // 2, u % 2, 4 * (u % 2)
                pe.wait_ge(u_ready[half], 1)
                if u >= 2:
                    pe.wait_ge(terms_ready, 12 * (u - 1))
                for j in range(2):
                    for ri in range(2):
                        for c in range(2):
                            last = nc.tensor.matmul(ps[:, bank + 2 * j + ri, :], fwd[:, 2 * j + c, (2 * ri + b) * P:(2 * ri + b + 1) * P],
                                                    Uv[:, 4 * half:4 * half + 4, 2 * j + c, :], start=(c == 0), stop=(c == 1))
                last.then_inc(spectrum, 1)
            pe.wait_ge(inv_in, 16)
            for half in range(2):
                pe.wait_ge(terms_ready, 12 * (3 + half))
                pe.wait_ge(dve_sums, 4 * (half + 1))
                pe.wait_ge(pool_sums, 12 * (half + 1))
                for q in range(CHUNKS):
                    for s in range(SLOTS):
                        last = nc.tensor.matmul(ps[:, 4 * half + q, :], inv[:, s, q * P:(q + 1) * P], Y[:, half, s, q // 2, :],
                                                start=(s == 0), stop=(s == SLOTS - 1))
                    last.then_inc(out_psum, 1)

        @block.vector
        def _(dve):
            V = nc.vector
            own = Chain(dve, dve_own)
            V.memset(cw[:, :], 0.0).then_inc(cw_cleared, 1)
            V.memset(eps[:, :], EPS).then_inc(eps_ready, 1)
            dve.wait_ge(params_in, 96)
            own(V.tensor_scalar(dtA[:, 0, :], par[:, 0, :], delta[:, 0:1], None, ALU.mult))
            own.link(V.tensor_scalar(dtA[:, 1, :], par[:, 1, :], delta[:, 0:1], None, ALU.mult))
            where = pos[:, :].rearrange("p (c a) -> p c a", a=1).broadcast_to([P, NPOS, STATES])
            one = dtA[:, 0, :].rearrange("p (a n) -> p a n", a=1).broadcast_to([P, NPOS, STATES])
            two = dtA[:, 1, :].rearrange("p (a n) -> p a n", a=1).broadcast_to([P, NPOS, STATES])
            V.tensor_tensor(mag[:, :, :], where, one, ALU.mult).then_inc(mag_in, 1)
            own.link(V.tensor_tensor(phase[:, :, :], where, two, ALU.mult))
            own.link(V.tensor_scalar(turns[:, :, :], phase[:, :, :], 1.0 / TWO_PI, ROUND, ALU.mult, ALU.add))
            own.link(V.tensor_scalar(turns[:, :, :], turns[:, :, :], ROUND, None, ALU.subtract))
            own.link(V.scalar_tensor_tensor(phase[:, :, :], turns[:, :, :], -TWO_PI_HI, phase[:, :, :], ALU.mult, ALU.add))
            own.link(V.scalar_tensor_tensor(phase[:, :, :], turns[:, :, :], TWO_PI_HI - TWO_PI, phase[:, :, :], ALU.mult, ALU.add))
            own.link(V.tensor_scalar(phase[:, :, :], phase[:, :, :], 3.1415925, -3.1415925, ALU.min, ALU.max))
            V.scalar_tensor_tensor(turns[:, :, :], phase[:, :, :], -1.0, phase[:, :, :], ALU.mult, ALU.min).then_inc(trig_in, 1)
            dve.wait_ge(trig_in, 1)
            V.tensor_scalar(turns[:, :, :], turns[:, :, :], TWO_PI / 4, None, ALU.add).then_inc(trig_in, 1)
            t, em1, shc, er, ei, den, qr, qi, bc, x1, x2, wr, wi = (small[:, n, :] for n in range(13))
            ar, ai = par[:, 0, :], par[:, 1, :]
            dve.wait_ge(tanh_ready, 1)
            own(V.tensor_scalar(x1, t, -1.0, 1.0, ALU.mult, ALU.add))
            own(V.tensor_tensor(bc, par[:, 2, :], par[:, 3, :], ALU.mult))
            own(V.tensor_tensor(x2, ar, ar, ALU.mult))
            own(V.tensor_tensor(den, ai, ai, ALU.mult))
            own.done()
            own(V.reciprocal(x1, x1))
            own(V.tensor_tensor(den, den, x2, ALU.add))
            own.done()
            own(V.scalar_tensor_tensor(em1, t, 2.0, x1, ALU.mult, ALU.mult))
            own(V.reciprocal(den, den))
            own.done()
            dve.wait_ge(trig_ready, 2)
            dve.wait_ge(mag_ready, 1)
            half_sin, sin1, cos1 = sin[:, NPOS - 1, :], sin[:, 1, :], cos[:, 1, :]
            own(V.scalar_tensor_tensor(shc, half_sin, -2.0, half_sin, ALU.mult, ALU.mult))
            own(V.tensor_tensor(er, em1, cos1, ALU.mult))
            own(V.scalar_tensor_tensor(ei, em1, 1.0, sin1, ALU.add, ALU.mult))
            own.done()
            own.link(V.tensor_tensor(er, er, shc, ALU.add))
            own(V.tensor_tensor(qr, er, ar, ALU.mult))
            own(V.tensor_tensor(x1, ei, ai, ALU.mult))
            own(V.tensor_tensor(qi, ei, ar, ALU.mult))
            own(V.tensor_tensor(x2, er, ai, ALU.mult))
            own(V.tensor_tensor(bc, bc, den, ALU.mult))
            own.done()
            own(V.tensor_tensor(qr, qr, x1, ALU.add))
            own(V.tensor_tensor(qi, qi, x2, ALU.subtract))
            own.done()
            own(V.tensor_tensor(wr, qr, bc, ALU.mult))
            own(V.tensor_tensor(wi, qi, bc, ALU.mult))
            own(V.tensor_tensor(fine[:, :, 0:STATES], mag[:, 0:NR, :], cos[:, 0:NR, :], ALU.mult))
            own(V.tensor_tensor(fine[:, :, STATES:], mag[:, 0:NR, :], sin[:, 0:NR, :], ALU.mult))
            own(V.tensor_tensor(turns[:, 0:NA, :], mag[:, NR:NR + NA, :], cos[:, NR:NR + NA, :], ALU.mult))
            own(V.tensor_tensor(phase[:, 0:NA, :], mag[:, NR:NR + NA, :], sin[:, NR:NR + NA, :], ALU.mult))
            own.done()
            wr_b = wr.rearrange("p (a n) -> p a n", a=1).broadcast_to([P, NA, STATES])
            wi_b = wi.rearrange("p (a n) -> p a n", a=1).broadcast_to([P, NA, STATES])
            vr, vi = turns[:, 0:NA, :], phase[:, 0:NA, :]
            own(V.tensor_tensor(rough[:, :, 0:STATES], vr, wr_b, ALU.mult))
            own(V.tensor_tensor(sin[:, 0:NA, :], vi, wi_b, ALU.mult))
            own(V.tensor_tensor(rough[:, :, STATES:], vi, wr_b, ALU.mult))
            own(V.tensor_tensor(cos[:, 0:NA, :], vr, wi_b, ALU.mult))
            own.done()
            own(V.tensor_tensor(rough[:, :, 0:STATES], rough[:, :, 0:STATES], sin[:, 0:NA, :], ALU.subtract))
            own.link(V.scalar_tensor_tensor(rough[:, :, STATES:], rough[:, :, STATES:], -1.0, cos[:, 0:NA, :], ALU.mult, ALU.subtract))
            dve.wait_ge(cw_in, 48)
            for q in range(4):
                shape = [P, NA // 4, NR, 2 * STATES]
                a = rough[:, q * NA // 4:(q + 1) * NA // 4, :].rearrange("p a (b n) -> p a b n", b=1).broadcast_to(shape)
                f = fine[:, :, :].rearrange("p (a r) n -> p a r n", a=1).broadcast_to(shape)
                g = q
                dve.wait_ge(gathered[g], 16 * GT)
                if g >= 1:
                    dve.wait_ge(exped, g)
                cb_b = cb[:, :].rearrange("p (a c) -> p a c", a=1).broadcast_to([P, GT, HALF_D])
                own.link(V.tensor_tensor(logits[:, :, :], H[:, g * GT:(g + 1) * GT, HALF_D:D], cb_b, ALU.add))
                own.link(V.tensor_reduce(top[:, :], logits[:, :, :], AX.X, ALU.max))
                top_b = top[:, :].rearrange("p (t a) -> p t a", a=1).broadcast_to([P, GT, HALF_D])
                V.tensor_tensor(logits[:, :, :], logits[:, :, :], top_b, ALU.subtract).then_inc(shifted, 1)
                own.link(V.tensor_tensor(prod[:, :, :, :], a, f, ALU.mult))
                dve.wait_ge(exped, g + 1)
                own.link(V.tensor_reduce(total[:, :], dist[:, :, :], AX.X, ALU.add))
                own.link(V.reciprocal(total[:, :], total[:, :]))
                total_b = total[:, :].rearrange("p (t a) -> p t a", a=1).broadcast_to([P, GT, HALF_D])
                V.tensor_tensor(dist[:, :, :], dist[:, :, :], total_b, ALU.mult).then_inc(dist_ready, 1)
                last = V.tensor_reduce(K[:, q * P:(q + 1) * P], prod[:, :, :, :].rearrange("p a r n -> p (a r) n"), AX.X, ALU.add)
                if q < 3:
                    own.link(last)
            last.then_inc(k_ready, 1)
            dve.wait_ge(coarse_in_h, GROUPS)
            token_statistics(nc, dve, own, H, stats, mean[:, :], var[:, :], tmp[:, :]).then_inc(var_ready, 1)
            dve.wait_ge(kf_ready, 6)
            for w in range(2):
                own(V.tensor_copy(Krn[0:1, w, :], Ki[0:1, w, 0, :]))
            own.done()
            for w in range(2):
                own(V.memset(Ki[0:1, w, 0, :], 0.0))
            dve.wait_ge(std_ready, 1)
            own.link(V.reciprocal(var[:, :], var[:, :]))
            V.scalar_tensor_tensor(offset[:, :], mean[:, :], -1.0, var[:, :], ALU.mult, ALU.mult).then_inc(offset_ready, 1)
            for t in range(TILES // 2):
                last = V.tensor_scalar(U[:, t, :], H[:, t, :], mean[:, t:t + 1], var[:, t:t + 1], ALU.subtract, ALU.mult)
            last.then_inc(u_ready[0], 1)
            Hv = H[:, :, :].rearrange("p (b c) d -> p b c d", c=CHUNKS)

            def add_out(half):
                for q in range(CHUNKS):
                    dve.wait_ge(out_psum, CHUNKS * half + q + 1)
                    V.tensor_tensor(Hv[:, 4 * half:4 * half + 4, q, :], ps[:, 4 * half + q, :].rearrange("p (b d) -> p b d", d=D),
                                    Hv[:, 4 * half:4 * half + 4, q, :], ALU.add).then_inc(out_done, 1)

            def wide(x):
                return x.rearrange("p (a d) -> p a d", a=1).broadcast_to([P, 4, D])

            HEAD, WHOLE = 0, 1
            for u in range(4):
                half, b, p = u // 2, u % 2, u % 2
                dve.wait_ge(spectrum, u + 1)
                if u >= 2:
                    dve.wait_ge(pool_sums, 6 * (u - 1))
                    dve.wait_ge(dve_sums, 2 * (u - 1))
                real = [wide(Kr[:, w, b, :]) for w in range(2)]
                real_n = [wide(Krn[:, w, :]) if b == 0 else real[w] for w in range(2)]
                imag = [wide(Ki[:, w, b, :]) for w in range(2)]
                pairs = ((0, real[HEAD]), (1, imag[HEAD]), (0, imag[HEAD]), (1, real_n[HEAD]),
                         (0, real[WHOLE]), (1, imag[WHOLE]), (2, real[HEAD]), (3, imag[HEAD]),
                         (0, imag[WHOLE]), (1, real_n[WHOLE]), (2, imag[HEAD]), (3, real_n[HEAD]))
                for n, (source, coefficient) in enumerate(pairs):
                    bank = ps[:, 4 * p + source, :].rearrange("p (a d) -> p a d", d=D)
                    V.tensor_tensor(terms[:, p, n, :].rearrange("p (a d) -> p a d", d=D), bank, coefficient,
                                    ALU.mult).then_inc(terms_ready, 1)
                dve.wait_ge(terms_ready, 12 * u + 4)
                V.tensor_tensor(Y[:, half, b, 0, :], terms[:, p, 0, :], terms[:, p, 1, :], ALU.subtract).then_inc(dve_sums, 1)
                V.tensor_tensor(Y[:, half, 2 + b, 0, :], terms[:, p, 2, :], terms[:, p, 3, :], ALU.add).then_inc(dve_sums, 1)
            add_out(0)
            add_out(1)


X_SCALE = 2.0 ** 6
PARTS = 2
HI, LO = 0, 1


def split_products(pe, out, stationary, moving, start, stop, **options):
    pairs = ((HI, HI), (HI, LO), (LO, HI))
    for n, (a, b) in enumerate(pairs):
        last = pe.matmul(out, stationary(a), moving(b), start=start and n == 0, stop=stop and n == len(pairs) - 1, **options)
    return last


def normalize(nc, stage, H, XT, ident16, gate=None):
    with ExitStack() as ctx:
        m = Memory(nc, stage, ctx)
        stats = m.sbuf("stats", [P, TILES, 6])
        per_token = m.sbuf("per_token", [P, 3, TILES])
        mean, var, tmp = (per_token[:, n, :] for n in range(3))
        eps = m.sbuf("eps", [P, 1])
        norm = m.sbuf("norm", [P, 2, CHUNKS, D])
        parts = m.sbuf("parts", [P, 2, PARTS, CHUNKS * D], F16)
        ps = m.psum("ps", [P, 2, PARTS, CHUNKS * P], F16)
        (own_sem, eps_ready, var_ready, std_ready, norm_ready, hi_ready, lo_ready, turned, xt_ready) = (m.sem(n) for n in (
            "own", "eps_ready", "var_ready", "std_ready", "norm_ready", "hi_ready", "lo_ready", "turned", "xt_ready"))
        if gate:
            gate.prepare(m)
        block = ctx.enter_context(nc.Block())

        @block.sync
        def _(sp):
            if gate:
                gate.load(sp)

        @block.vector
        def _(dve):
            V = nc.vector
            own = Chain(dve, own_sem)
            V.memset(eps[:, :], EPS / X_SCALE ** 2).then_inc(eps_ready, 1)
            token_statistics(nc, dve, own, H, stats, mean[:, :], var[:, :], tmp[:, :]).then_inc(var_ready, 1)
            if gate:
                gate.split_low(dve)
            dve.wait_ge(std_ready, 1)
            own.link(V.reciprocal(var[:, :], var[:, :]))

            def center(b, p):
                for c in range(CHUNKS):
                    t = b * CHUNKS + c
                    V.tensor_scalar(norm[:, p, c, :], H[:, t, :], mean[:, t:t + 1], var[:, t:t + 1],
                                    ALU.subtract, ALU.mult).then_inc(norm_ready, 1)

            for b in range(SEQS):
                if b >= 2:
                    dve.wait_ge(lo_ready, b - 1)
                center(b, b % 2)
                if gate:
                    gate.split_expert_low(dve, b)

        @block.gpsimd
        def _(pool):
            for b in range(SEQS):
                pool.wait_ge(norm_ready, (b + 1) * CHUNKS)
                pool.wait_ge(hi_ready, b + 1)
                nc.gpsimd.tensor_tensor(parts[:, b % 2, LO, :], norm[:, b % 2, :, :].rearrange("p c d -> p (c d)"),
                                        parts[:, b % 2, HI, :], ALU.subtract).then_inc(lo_ready, 1)

        @block.scalar
        def _(act):
            A = nc.scalar
            if gate:
                gate.split_high(act)
            act.wait_ge(var_ready, 1)
            act.wait_ge(eps_ready, 1)
            A.activation(var[:, :], var[:, :], ACT.Sqrt, bias=eps[:, 0:1], scale=X_SCALE ** -2).then_inc(std_ready, 1)

            def high(b):
                act.wait_ge(norm_ready, (b + 1) * CHUNKS)
                A.activation(parts[:, b % 2, HI, :], norm[:, b % 2, :, :].rearrange("p c d -> p (c d)"), ACT.Copy).then_inc(hi_ready, 1)

            high(0)
            high(1)
            for b in range(SEQS):
                act.wait_ge(turned, b + 1)
                A.activation(XT[:, b, :, :], ps[:, b % 2, :, :], ACT.Copy).then_inc(xt_ready, 1)
                if b + 2 < SEQS:
                    high(b + 2)
                if gate:
                    gate.split_expert_high(act, b)
                    if b >= 1:
                        gate.relu(act, b - 1)
            if gate:
                gate.relu(act, SEQS - 1)

        @block.tensor
        def _(pe):
            for b in range(SEQS):
                pe.wait_ge(lo_ready, b + 1)
                if b >= 2:
                    pe.wait_ge(xt_ready, b - 1)
                for part in range(PARTS):
                    for c in range(CHUNKS):
                        last = nc.tensor.transpose(ps[:, b % 2, part, c * P:(c + 1) * P], parts[:, b % 2, part, c * D:(c + 1) * D], ident16[:, :])
                last.then_inc(turned, 1)
                if gate and b >= 1:
                    pe.wait_ge(xt_ready, b)
                    gate.hidden_product(pe, XT, b - 1)
                if gate and b >= 2:
                    gate.logits_product(pe, b - 2)
            if gate:
                pe.wait_ge(xt_ready, SEQS)
                gate.hidden_product(pe, XT, SEQS - 1)
                gate.logits_product(pe, SEQS - 2)
                gate.logits_product(pe, SEQS - 1)


EXPERTS = 8
NEVER = -3.0e38


def top_two(V, own, scores, rank, first, second, m1, m2, work):
    shape = scores.shape
    T = shape[1]
    rank_b = rank.rearrange("p (a e) -> p a e", a=1).broadcast_to(shape)
    wide = lambda x: x.rearrange("p (t a) -> p t a", a=1).broadcast_to(shape)
    picked = work[:, 0:T]
    own.link(V.tensor_reduce(m1, scores, AX.X, ALU.max))
    for onehot, best in ((first, m1), (second, m2)):
        own.link(V.tensor_tensor(onehot, scores, wide(best), ALU.is_equal))
        own.link(V.tensor_tensor(onehot, onehot, rank_b, ALU.mult))
        own.link(V.tensor_reduce(picked, onehot, AX.X, ALU.max))
        own.link(V.tensor_tensor(onehot, onehot, wide(picked), ALU.is_equal))
        if onehot is first:
            own.link(V.scalar_tensor_tensor(scores, first, NEVER, scores, ALU.mult, ALU.add))
            own.link(V.tensor_reduce(m2, scores, AX.X, ALU.max))


def load_bias_blocks(sp, blocks, bias, cleared, loaded):
    sp.wait_ge(cleared, 1)
    for t in range(CHUNKS):
        sp.dma_start(blocks[32 * t:32 * t + EXPERTS, t * D:(t + 1) * D], bias).then_inc(loaded, 16)


def bias_share_products(pe, nc, banks, rows, bias_blocks, bias_psum, bias_added):
    for b in range(SEQS):
        if b >= 2:
            pe.wait_ge(bias_added, b - 1)
        nc.tensor.matmul(banks[b % 2], rows[:, b, :], bias_blocks[:, :], start=True, stop=True).then_inc(bias_psum, 1)


def add_bias_shares(dve, nc, H, banks, bias_psum, bias_added):
    for b in range(SEQS):
        dve.wait_ge(bias_psum, b + 1)
        here = H[:, b * CHUNKS:(b + 1) * CHUNKS, :].rearrange("p c d -> p (c d)")
        nc.vector.tensor_tensor(here, banks[b % 2], here, ALU.add).then_inc(bias_added, 1)


class RecurrentGate:

    def __init__(self, nc, d, routing):
        self.nc, self.d = nc, d
        self.logits = routing.psum("logits", [P, 512])
        self.bias, self.rank = routing.sbuf("router_b", [P, EXPERTS]), routing.sbuf("rank", [P, EXPERTS])

    def prepare(self, m):
        self.later_in = m.sem("later_in")
        self.w = m.sbuf("router_w", [P, EXPERTS])
        self.parts = m.sbuf("router_w_parts", [P, PARTS, EXPERTS], F16)
        self.w_in, self.w_hi, self.w_parts = (m.sem(n) for n in ("w_in", "w_hi", "w_parts"))

    def load(self, sp):
        sp.dma_start(self.w[:, :], self.d["router_w"]).then_inc(self.w_in, 16)
        for to, name in ((self.bias, "router_b"), (self.rank, "rank")):
            sp.dma_start(to[:, :], self.d[name]).then_inc(self.later_in, 16)
        sp.wait_ge(self.later_in, 32)

    def split_high(self, act):
        act.wait_ge(self.w_in, 16)
        self.nc.scalar.activation(self.parts[:, HI, :], self.w[:, :], ACT.Copy, scale=W_SCALE_ROUTER).then_inc(self.w_hi, 1)

    def split_low(self, dve):
        dve.wait_ge(self.w_hi, 1)
        self.nc.vector.scalar_tensor_tensor(self.parts[:, LO, :], self.w[:, :], W_SCALE_ROUTER, self.parts[:, HI, :],
                                            ALU.mult, ALU.subtract).then_inc(self.w_parts, 1)

    def hidden_product(self, pe, XT, b):
        if b == 0:
            pe.wait_ge(self.w_parts, 1)
        for c in range(CHUNKS):
            at = (b * CHUNKS + c) * EXPERTS
            split_products(self.nc.tensor, self.logits[:, at:at + EXPERTS], lambda part: XT[:, b, part, c * P:(c + 1) * P],
                           lambda part: self.parts[:, part, :], True, True)

    def split_expert_high(self, act, e):
        pass

    def split_expert_low(self, dve, e):
        pass

    def relu(self, act, b):
        pass

    def logits_product(self, pe, b):
        pass


def route_recurrent(nc, ident, d, combine, mask_rows, rows, bias_blocks, gate):
    COLS = 32
    with ExitStack() as ctx:
        m = Memory(nc, "route", ctx)
        rb, rank = gate.bias, gate.rank
        logits = m.sbuf("logits", [P, TILES, EXPERTS])
        first = m.sbuf("first", [P, TILES, EXPERTS])
        second = m.sbuf("second", [P, TILES, EXPERTS])
        per_token = m.sbuf("per_token", [P, 5, TILES])
        m1, m2, e, r1, work = (per_token[:, n, :] for n in range(5))
        share = m.sbuf("share", [P, TILES, EXPERTS])
        record = m.sbuf("record", [P, TILES, COLS])
        rows16 = m.sbuf("rows16", [P, SEQS, P], F16)
        psR = m.psum("psR", [P, SEQS, P])
        (cleared, bias_in, own_sem, gap_ready, exp_ready, record_ready, rows_psum, rows16_ready, stored) = (
            m.sem(n) for n in ("cleared", "bias_in", "own", "gap_ready", "exp_ready", "record_ready", "rows_psum",
                               "rows16_ready", "stored"))
        block = ctx.enter_context(nc.Block())

        @block.sync
        def _(sp):
            load_bias_blocks(sp, bias_blocks, d["bo"], cleared, bias_in)
            sp.wait_ge(rows16_ready, 1)
            for t in range(CHUNKS):
                sp.dma_start(mask_rows.rearrange("j (b c q) -> j b c q", b=SEQS, c=CHUNKS)[:, :, t, :],
                             rows16[COLS * t + EXPERTS:COLS * t + 3 * EXPERTS, :, :]).then_inc(stored, 16)
            sp.wait_ge(stored, 16 * CHUNKS)
            sp.wait_ge(bias_in, 16 * CHUNKS)

        @block.scalar
        def _(act):
            A = nc.scalar
            A.preload_act_table(ACT.Exp)
            act.wait_ge(gap_ready, 1)
            A.activation(e[:, :], e[:, :], ACT.Exp).then_inc(exp_ready, 1)
            act.wait_ge(rows_psum, 1)
            A.activation(rows16[:, :, :], psR[:, :, :], ACT.Copy).then_inc(rows16_ready, 1)
            A.activation(rows[:, :, :], psR[:, :, :], ACT.Copy)

        @block.tensor
        def _(pe):
            pe.wait_ge(record_ready, 1)
            for b in range(SEQS):
                last = nc.tensor.transpose(psR[:, b, :], record[:, b * CHUNKS:(b + 1) * CHUNKS, :].rearrange("p c j -> p (c j)"), ident[:, :])
            last.then_inc(rows_psum, 1)

        @block.vector
        def _(dve):
            V = nc.vector
            own = Chain(dve, own_sem)
            V.memset(bias_blocks[:, :], 0.0).then_inc(cleared, 1)
            own(V.memset(record[:, :, 3 * EXPERTS:], 0.0))
            rb_b = rb[:, :].rearrange("p (a e) -> p a e", a=1).broadcast_to([P, TILES, EXPERTS])
            own.link(V.scalar_tensor_tensor(logits[:, :, :], gate.logits[:, 0:TILES * EXPERTS].rearrange("p (t e) -> p t e", e=EXPERTS),
                                            1.0 / (X_SCALE * W_SCALE_ROUTER), rb_b, ALU.mult, ALU.add))
            top_two(V, own, logits[:, :, :], rank[:, :], first[:, :, :], second[:, :, :], m1[:, :], m2[:, :], work[:, :])
            V.tensor_tensor(e[:, :], m2[:, :], m1[:, :], ALU.subtract).then_inc(gap_ready, 1)
            dve.wait_ge(exp_ready, 1)
            own.link(V.tensor_scalar(r1[:, :], e[:, :], 1.0, None, ALU.add))
            own.link(V.reciprocal(r1[:, :], r1[:, :]))
            own(V.tensor_tensor(e[:, :], e[:, :], r1[:, :], ALU.mult))
            wide = lambda x: x.rearrange("p (t a) -> p t a", a=1).broadcast_to([P, TILES, EXPERTS])
            own(V.tensor_tensor(share[:, :, :], first[:, :, :], wide(r1[:, :]), ALU.mult))
            own(V.tensor_copy(record[:, :, EXPERTS:2 * EXPERTS], first[:, :, :]))
            own(V.tensor_copy(record[:, :, 2 * EXPERTS:3 * EXPERTS], second[:, :, :]))
            own.done()
            own.link(V.tensor_tensor(second[:, :, :], second[:, :, :], wide(e[:, :]), ALU.mult))
            own.link(V.tensor_tensor(record[:, :, 0:EXPERTS], share[:, :, :], second[:, :, :], ALU.add))
            V.tensor_scalar(combine[:, :, :], record[:, :, 0:EXPERTS], 1.0 / OUT_SCALE, None, ALU.mult).then_inc(record_ready, 1)


W_SCALE_ROUTER = 2.0 ** 8
H_SCALE = 2.0 ** 8
WI_SCALE = 2.0 ** 8
WH_SCALE = X_SCALE * WI_SCALE / H_SCALE
WO_SCALE = 2.0 ** 6
GATE_SCALE = X_SCALE * WI_SCALE
OUT_SCALE = H_SCALE * WO_SCALE
STEPS, WIDTH = SEQS, SEQ
GATES = 4
IN, FORGET, CELL, OUT = range(GATES)


def recurrent_experts(nc, H, XT, d, combine, mask_rows, rows, bias_blocks):
    GD = GATES * D
    ORDER = (IN, CELL, FORGET, OUT)
    with ExitStack() as ctx:
        m = Memory(nc, "lstm", ctx)
        biases = m.sbuf("biases", [P, EXPERTS * GATES])
        bias = m.sbuf("bias", [P, 2, GATES])
        raw = m.sbuf("weights", [P, 2, 2 * GD + D])
        wp = m.sbuf("weight_parts", [P, 2, PARTS, 2 * GD], F16)
        wo = m.sbuf("output_weight_parts", [P, 2, PARTS, D], F16)
        mask = m.sbuf("mask", [P, 2, 2, STEPS * WIDTH], F16)
        xm = m.sbuf("masked_x", [P, 2, 2, PARTS, WIDTH], F16)
        gates = m.sbuf("gates", [P, 2, GATES, WIDTH])
        cell = m.sbuf("cell", [P, 2, WIDTH])
        tc = m.sbuf("tanh_cell", [P, 2, WIDTH])
        hid = m.sbuf("hidden", [P, 2, WIDTH])
        hp = m.sbuf("hidden_parts", [P, 2, PARTS, WIDTH], F16)
        z1 = m.sbuf("second_choice", [P, PARTS, WIDTH], F16)
        z = m.sbuf("chosen", [P, 2, STEPS, PARTS, WIDTH], F16)
        ps = m.psum("ps", [P, 8, WIDTH])
        bias_in = m.sem("bias_in")
        weights_in = [m.sem(f"weights_in{p}") for p in range(2)]
        mask_in = [m.sem(f"mask_in{p}") for p in range(2)]
        first_mask_in = m.sem("first_mask_in")
        (bias_ready, hi_weights, weights_ready, hi_output_weights, output_weights_ready, xm_ready, gate_psum, gate_ready, own_sem, cell_ready, tc_ready, hidden_ready,
         hidden_hi, hidden_lo, z0_ready, z1_ready, z_ready, wo_psum, wo_added) = (m.sem(n) for n in (
             "bias_ready", "hi_weights", "weights_ready", "hi_output_weights", "output_weights_ready", "xm_ready", "gate_psum", "gate_ready", "own", "cell_ready", "tc_ready",
             "hidden_ready", "hidden_hi", "hidden_lo", "z0_ready", "z1_ready", "z_ready", "wo_psum", "wo_added"))
        bias_psum, bias_added, weighed, pool_added = (m.sem(n) for n in ("bias_psum", "bias_added", "weighed", "pool_added"))
        bias_banks = [ps[:, 4 + g, :] for g in (FORGET, OUT)]
        block = ctx.enter_context(nc.Block())

        skip = lambda *a: None

        def schedule(engine, step, extra=skip, before=skip):
            def rest(e, parity):
                before(e, parity)
                step(e, parity, 1, 1)
                extra(e, parity)
                with engine.Fori(1, STEPS // 2) as j:
                    for p in range(2):
                        step(e, parity, j * 2 + p, p)

            step(0, 0, 0, 0)
            rest(0, 0)
            step(1, 1, 0, 0)
            with engine.Fori(0, EXPERTS // 2 - 1) as i:
                for n in (1, 2):
                    rest(i * 2 + n, n % 2)
                    step(i * 2 + n + 1, 1 - n % 2, 0, 0)
            rest(EXPERTS - 1, 1)

        is_first = lambda e, s: isinstance(s, int) and isinstance(e, int) and e == 0 and s == 0
        at_start = lambda e, s: isinstance(s, int) and s == 0
        has_output = lambda e: not (isinstance(e, int) and e == 0)

        @block.sync
        def _(sp):
            sp.dma_start(biases[:, :], d["lstm_b"]).then_inc(bias_in, 16)

            def load_weights(e, parity):
                for n, (name, at, width) in enumerate((("Wi", 0, GD), ("Wh", GD, GD), ("Wo", 2 * GD, D))):
                    sp.dma_start(raw[:, parity, at:at + width], d[name][bass.ds(e * P, P), :]).then_inc(weights_in[parity], 16)

            def load_masks(e, parity, start, end, loaded):
                for k in range(2):
                    row = mask_rows[bass.ds(e + k * EXPERTS, 1), start:end]
                    sp.dma_start(mask[:, parity, k, start:end], row.partition_broadcast(P)).then_inc(loaded, 16)

            def before(e, parity):
                if not (isinstance(e, int) and e == EXPERTS - 1):
                    if not (isinstance(e, int) and e == 0):
                        sp.wait_ge(z_ready, e * STEPS)
                    load_weights(e + 1, 1 - parity)
                    load_masks(e + 1, 1 - parity, 0, STEPS * WIDTH, mask_in[1 - parity])

            load_masks(0, 0, 0, WIDTH, first_mask_in)
            load_weights(0, 0)
            load_masks(0, 0, WIDTH, STEPS * WIDTH, mask_in[0])
            schedule(sp, skip, before=before)

        @block.gpsimd
        def _(pool):
            def z0(n_s, e_parity, s):
                pool.wait_ge(hidden_lo, n_s * 2 + 1)
                m0 = mask[:, e_parity, 0, bass.ds(s * WIDTH, WIDTH)].rearrange("p (a n) -> p a n", a=1).broadcast_to([P, PARTS, WIDTH])
                nc.gpsimd.tensor_tensor(z[:, e_parity, bass.ds(s, 1), :, :].rearrange("p a h n -> p (a h) n"), hp[:, 0, :, :], m0,
                                        ALU.mult).then_inc(z0_ready, 1)

            def step(e, parity, s, p):
                n_s = e * STEPS + s
                if is_first(e, s):
                    pool.wait_ge(first_mask_in, 32)
                elif at_start(e, s):
                    pool.wait_ge(mask_in[parity], (e - parity) * 16 + 32)
                elif isinstance(n_s, int) and n_s == 1:
                    pool.wait_ge(mask_in[0], 32)
                if not (isinstance(n_s, int) and n_s < 2):
                    pool.wait_ge(gate_psum, (n_s - 1) * 2 * GATES)
                shape = [P, 2, PARTS, WIDTH]
                m_b = mask[:, parity, :, bass.ds(s * WIDTH, WIDTH)].rearrange("p k (a n) -> p k a n", a=1).broadcast_to(shape)
                x_b = XT[:, bass.ds(s, 1), :, :].broadcast_to(shape)
                nc.gpsimd.tensor_tensor(xm[:, p, :, :, :], x_b, m_b, ALU.mult).then_inc(xm_ready, 1)
                if at_start(e, s):
                    if not is_first(e, s):
                        z0(n_s - 1, 1 - parity, STEPS - 1)
                else:
                    z0(n_s - 1, parity, s - 1)

            schedule(pool, step)
            z0(EXPERTS * STEPS - 1, 1, STEPS - 1)
            for s in range(1, STEPS, 2):
                pool.wait_ge(weighed, s // 2 + 1)
                here = H[:, s * CHUNKS:(s + 1) * CHUNKS, :].rearrange("p c d -> p (c d)")
                nc.gpsimd.tensor_tensor(here, gates[:, 0, s // 2, :], here, ALU.add).then_inc(pool_added, 1)

        @block.tensor
        def _(pe):
            def w(parity, part, at, gate):
                return wp[:, parity, part, at + gate * D:at + (gate + 1) * D]

            def output_product(e, parity, s, bank):
                pe.wait_ge(output_weights_ready, e + 1)
                pe.wait_ge(z_ready, e * STEPS + s + 1)
                for c in range(CHUNKS):
                    last = split_products(
                        nc.tensor, ps[:, bank, c * P:(c + 1) * P],
                        lambda part: z[:, parity, bass.ds(s, 1), part, c * P:(c + 1) * P].rearrange("p a n -> p (a n)"),
                        lambda part: wo[:, parity, part, :], True, True)
                last.then_inc(wo_psum, 1)

            def step(e, parity, s, p):
                n_s = e * STEPS + s
                for k in range(2):
                    n_u = n_s * 2 + k
                    if at_start(e, s) and k == 0:
                        pe.wait_ge(weights_ready, e + 1)
                    pe.wait_ge(xm_ready, n_s + 1)
                    if not is_first(e, s):
                        pe.wait_ge(gate_ready, (n_u - 1) * GATES)
                    for g in ORDER:
                        if is_first(e, s) and k == 1 and g == FORGET:
                            pe.wait_ge(bias_added, SEQS)
                        if k == 0 and g == OUT and has_output(e) and not (isinstance(e, int) and e == 1 and at_start(e, s)):
                            pe.wait_ge(wo_added, (e - 1) * STEPS + s)
                        last = split_products(nc.tensor, ps[:, 4 * k + g, :], lambda part: w(parity, part, 0, g),
                                              lambda part: xm[:, p, k, part, :], True, at_start(e, s))
                        if at_start(e, s):
                            last.then_inc(gate_psum, 1)
                    if k == 1 and has_output(e):
                        pe.wait_ge(gate_ready, n_u * GATES)
                        output_product(e - 1, 1 - parity, s, OUT)
                    if not at_start(e, s):
                        pe.wait_ge(hidden_lo, n_u - 1)
                        for g in ORDER:
                            split_products(nc.tensor, ps[:, 4 * k + g, :], lambda part: w(parity, part, GD, g),
                                           lambda part: hp[:, k, part, :], False, True).then_inc(gate_psum, 1)

            bias_share_products(pe, nc, bias_banks, rows, bias_blocks, bias_psum, bias_added)
            schedule(pe, step)
            pe.wait_ge(gate_ready, EXPERTS * STEPS * 2 * GATES)
            pe.wait_ge(wo_added, (EXPERTS - 1) * STEPS)
            for s in range(STEPS):
                output_product(EXPERTS - 1, 1, s, s)

        @block.scalar
        def _(act):
            A = nc.scalar
            A.preload_act_table(ACT.Sigmoid)
            def split_high(e, parity):
                act.wait_ge(weights_in[parity], (e - parity) * 24 + 48)
                for at, scale in ((0, WI_SCALE), (GD, WH_SCALE)):
                    A.activation(wp[:, parity, HI, at:at + GD], raw[:, parity, at:at + GD], ACT.Copy, scale=scale).then_inc(hi_weights, 1)

            def split_output_high(e, parity):
                A.activation(wo[:, parity, HI, :], raw[:, parity, 2 * GD:], ACT.Copy, scale=WO_SCALE).then_inc(hi_output_weights, 1)

            split_high(0, 0)
            act.wait_ge(bias_in, 16)

            def take_bias(e, parity):
                A.activation(bias[:, parity, :], biases[:, bass.ds(e * GATES, GATES)], ACT.Copy).then_inc(bias_ready, 1)

            take_bias(0, 0)

            def step(e, parity, s, p):
                n_s = e * STEPS + s
                for k in range(2):
                    n_u = n_s * 2 + k
                    if at_start(e, s):
                        act.wait_ge(bias_ready, e + 1)
                    if not is_first(e, s):
                        act.wait_ge(hidden_ready, n_u - 1)
                    for n, g in enumerate(ORDER):
                        act.wait_ge(gate_psum, n_u * GATES + n + 1)
                        done = A.activation(gates[:, k, g, :], ps[:, 4 * k + g, :], ACT.Tanh if g == CELL else ACT.Sigmoid,
                                            bias=bias[:, parity, g:g + 1], scale=1.0 / GATE_SCALE)
                        done.then_inc(gate_ready, 1)
                    act.wait_ge(cell_ready, n_u + 1)
                    A.activation(tc[:, k, :], cell[:, k, :], ACT.Tanh).then_inc(tc_ready, 1)
                    act.wait_ge(hidden_ready, n_u + 1)
                    if not is_first(e, s):
                        act.wait_ge(z1_ready if k else z0_ready, n_s)
                    A.activation(hp[:, k, HI, :], hid[:, k, :], ACT.Copy).then_inc(hidden_hi, 1)

            def extra(e, parity):
                split_output_high(e, parity)
                if not (isinstance(e, int) and e == EXPERTS - 1):
                    split_high(e + 1, 1 - parity)
                    take_bias(e + 1, 1 - parity)

            schedule(act, step, extra=extra)
            act.wait_ge(hidden_ready, EXPERTS * STEPS * 2)
            for s in range(1, STEPS, 2):
                act.wait_ge(wo_psum, (EXPERTS - 1) * STEPS + s + 1)
                for c in range(CHUNKS):
                    tile = s * CHUNKS + c
                    last = A.activation(gates[:, 0, s // 2, c * P:(c + 1) * P], ps[:, s, c * P:(c + 1) * P], ACT.Copy,
                                        scale=combine[:, tile, EXPERTS - 1:EXPERTS])
                last.then_inc(weighed, 1)

        @block.vector
        def _(dve):
            V = nc.vector

            def split_low(e, parity):
                dve.wait_ge(hi_weights, e * 2 + 2)
                for at, scale in ((0, WI_SCALE), (GD, WH_SCALE)):
                    last = V.scalar_tensor_tensor(wp[:, parity, LO, at:at + GD], raw[:, parity, at:at + GD], scale,
                                                  wp[:, parity, HI, at:at + GD], ALU.mult, ALU.subtract)
                last.then_inc(weights_ready, 1)

            def split_output_low(e, parity):
                dve.wait_ge(hi_output_weights, e + 1)
                V.scalar_tensor_tensor(wo[:, parity, LO, :], raw[:, parity, 2 * GD:], WO_SCALE, wo[:, parity, HI, :],
                                       ALU.mult, ALU.subtract).then_inc(output_weights_ready, 1)

            add_bias_shares(dve, nc, H, bias_banks, bias_psum, bias_added)
            split_low(0, 0)

            def add_output(e, s, bank):
                dve.wait_ge(wo_psum, e * STEPS + s + 1)
                for c in range(CHUNKS):
                    here = H[:, bass.ds(s * CHUNKS + c, 1), :].rearrange("p a d -> p (a d)")
                    share = combine[:, bass.ds(s * CHUNKS + c, 1), bass.ds(e, 1)].rearrange("p a b -> p (a b)")
                    last = V.scalar_tensor_tensor(here, ps[:, bank, c * P:(c + 1) * P], share, here, ALU.mult, ALU.add)
                last.then_inc(wo_added, 1)

            def second_share(n_s, e_parity, s):
                m1 = mask[:, e_parity, 1, bass.ds(s * WIDTH, WIDTH)].rearrange("p (a n) -> p a n", a=1).broadcast_to([P, PARTS, WIDTH])
                if not (isinstance(n_s, int) and n_s == 0):
                    dve.wait_ge(z_ready, n_s)
                dve.wait_ge(hidden_lo, n_s * 2 + 2)
                V.tensor_tensor(z1[:, :, :], hp[:, 1, :, :], m1, ALU.mult).then_inc(z1_ready, 1)

            def choose(n_s, e_parity, s):
                zs = z[:, e_parity, bass.ds(s, 1), :, :].rearrange("p a h n -> p (a h) n")
                dve.wait_ge(z1_ready, n_s + 1)
                dve.wait_ge(z0_ready, n_s + 1)
                V.tensor_tensor(zs, zs, z1[:, :, :], ALU.add).then_inc(z_ready, 1)

            def step(e, parity, s, p):
                n_s = e * STEPS + s
                first_step = at_start(e, s)
                for k in range(2):
                    n_u = n_s * 2 + k
                    g = lambda gate: gates[:, k, gate, :]
                    dve.wait_ge(gate_ready, n_u * GATES + 2)
                    if first_step:
                        V.tensor_tensor(cell[:, k, :], g(IN), g(CELL), ALU.mult).then_inc(cell_ready, 1)
                    else:
                        V.tensor_tensor(g(IN), g(IN), g(CELL), ALU.mult).then_inc(own_sem, 1)
                        dve.wait_ge(gate_ready, n_u * GATES + 3)
                        V.tensor_tensor(cell[:, k, :], g(FORGET), cell[:, k, :], ALU.mult).then_inc(own_sem, 1)
                        dve.wait_ge(own_sem, e * (STEPS - 1) * 4 + s * 4 + (2 * k - 2))
                        V.tensor_tensor(cell[:, k, :], cell[:, k, :], g(IN), ALU.add).then_inc(cell_ready, 1)
                    dve.wait_ge(gate_ready, n_u * GATES + 4)
                    dve.wait_ge(tc_ready, n_u + 1)
                    V.scalar_tensor_tensor(hid[:, k, :], g(OUT), H_SCALE, tc[:, k, :], ALU.mult, ALU.mult).then_inc(hidden_ready, 1)
                    last_step_of = (second_share, choose)[k]
                    if not first_step:
                        last_step_of(n_s - 1, parity, s - 1)
                    elif not is_first(e, s):
                        last_step_of(n_s - 1, 1 - parity, STEPS - 1)
                    dve.wait_ge(hidden_hi, n_u + 1)
                    V.tensor_tensor(hp[:, k, LO, :], hid[:, k, :], hp[:, k, HI, :], ALU.subtract).then_inc(hidden_lo, 1)
                    if k == 0 and has_output(e):
                        add_output(e - 1, s, OUT)

            def extra(e, parity):
                split_output_low(e, parity)
                if not (isinstance(e, int) and e == EXPERTS - 1):
                    split_low(e + 1, 1 - parity)

            schedule(dve, step, extra=extra)
            second_share(EXPERTS * STEPS - 1, 1, STEPS - 1)
            choose(EXPERTS * STEPS - 1, 1, STEPS - 1)
            for s in range(0, STEPS, 2):
                add_output(EXPERTS - 1, s, s)


HEADS, HEAD = 8, 64
INNER = HEADS * HEAD
PAIRS = HEADS // 2
QK_SCALE = 2.0 ** 8
V_SCALE = 2.0 ** 8
ATT_WO_SCALE = 2.0 ** 6
SHIFT = 256.0
PROB_GAIN = 6.931471805599453
STEPS_A = HEADS * CHUNKS


FIRST_MAX = 11
SPLIT, TURN = (2, 4, 6, 9), (11, 17, 21, 25)


def background_tasks():
    tasks = [[] for _ in range(STEPS_A)]
    for c in range(CHUNKS):
        tasks[SPLIT[c]].append(("split", c))
        tasks[SPLIT[c] + 2].append(("split_low", c))
        tasks[8 + c].append(("v", c))
        tasks[TURN[c]].append(("turn", c))
        tasks[TURN[c] + 1].append(("turned", c))
    for t in range(2 * PAIRS):
        tasks[t].append(("qk", t))
    for c in range(CHUNKS):
        tasks[28 + c].append(("out", c))
    for j in range(STEPS_A):
        tasks[FIRST_MAX + j // 2].append(("max", j))
    tasks[FIRST_MAX + 16].append(("shift", 0))
    return tasks


def attention(nc, H, XT, ident16, d):
    with ExitStack() as ctx:
        m = Memory(nc, "att", ctx)
        wp = m.sbuf("weight_parts", [P, PARTS, 3 * INNER + CHUNKS * D], F16)
        b_out = m.sbuf("b_out", [P, D])
        qk = m.sbuf("qk", [P, 2, PARTS, 2 * PAIRS, SEQ], F16)
        QS = m.sbuf("q_twice", [P, 2, HEADS, SEQ], F16)
        Q2 = m.sbuf("q_lo_shift", [P, 2, HEADS, SEQ], F16)
        KS = m.sbuf("k_parts", [P, 2, HEADS, SEQ], F16)
        K2 = m.sbuf("k_hi_ones", [P, 2, HEADS, SEQ], F16)
        V1 = m.sbuf("v_ones", [P, 2, PARTS, CHUNKS, HEADS, HEAD + 1], F16)
        prob = m.sbuf("prob", [P, 4, SEQ])
        pp = m.sbuf("prob_parts", [P, 4, PARTS, SEQ], F16)
        gain = m.sbuf("prob_gain", [P, 1])
        zero = m.sbuf("zero", [P, 1])
        mx = m.sbuf("max", [P, STEPS_A])
        nm = m.sbuf("shift", [P, STEPS_A], F16)
        nmT = m.sbuf("shiftT", [STEPS_A, 2, P], F16)
        rec = m.sbuf("reciprocal", [P, 2, CHUNKS])
        O = m.sbuf("o", [P, 2, CHUNKS, INNER])
        raw = O[:, :, :, :].rearrange("p a c n -> p (a c n)")
        op = m.sbuf("o_parts", [P, PARTS, CHUNKS, INNER], F16)
        OT = m.sbuf("oT", [P, CHUNKS, PARTS, CHUNKS, P], F16)
        psS = m.psum("psS", [P, 3, SEQ])
        psV = m.psum("psV", [P, 2, SEQ])
        psM = m.psum("psM", [P, 2, SEQ])
        psX = m.psum("psX", [P, SEQ])
        turned16 = psX[:, :].bitcast(F16)
        weights_in = [m.sem(f"weights_in{n}") for n in range(4)]
        consts_in, bias_added, v_ones, gain_ready = (m.sem(n) for n in (
            "consts_in", "bias_added", "v_ones", "gain_ready"))
        placed = [m.sem(f"placed{p}") for p in range(2)]
        shift_in = [m.sem(f"shift_in{p}") for p in range(2)]
        (weights_hi, weights_ready, ones_ready, qk_full, qk_hi, qk_lo, v_full, v_hi, v_ready, max_full, max_done, shift_ready,
         shift_turned, shiftT_ready, s_full, p_full, p_ready, p_lo, av_done, rec_ready, o_ready, o_hi, o_lo, turn_full, turn_done,
         out_full, out_done) = (m.sem(n) for n in (
             "weights_hi", "weights_ready", "ones_ready", "qk_full", "qk_hi", "qk_lo", "v_full", "v_hi", "v_ready", "max_full", "max_done",
             "shift_ready", "shift_turned", "shiftT_ready", "s_full", "p_full", "p_ready", "p_lo", "av_done", "rec_ready", "o_ready", "o_hi",
             "o_lo", "turn_full", "turn_done", "out_full", "out_done"))
        block = ctx.enter_context(nc.Block())
        TASKS = background_tasks()
        AHEAD, BEHIND = ("qk", "v", "max", "shift"), ("split", "split_low", "turn", "turned", "out")

        def schedule(engine, task, step, tasks_first=False, lag=0):
            def sequence(b, parity, ahead, behind):
                def run(n, chosen):
                    for kind, j in TASKS[n] if n >= 0 else ():
                        if kind in AHEAD and ahead and chosen(kind, j):
                            task(kind, j, b + 1, 1 - parity)
                        if kind in BEHIND and behind and chosen(kind, j):
                            task(kind, j, b - 1, 1 - parity)

                second_max = lambda kind, j: kind == "max" and j % 2 == 1
                for n in range(STEPS_A):
                    if tasks_first:
                        run(n, lambda kind, j: not second_max(kind, j))
                    step(b, parity, n)
                    if tasks_first:
                        run(n, second_max)
                    else:
                        run(n - lag, lambda kind, j: True)

            for kind, j in (t for tasks in TASKS for t in tasks):
                if kind in AHEAD:
                    task(kind, j, 0, 0)
            sequence(0, 0, True, False)
            with engine.Fori(0, SEQS // 2 - 1) as i:
                for n in (1, 2):
                    sequence(i * 2 + n, n % 2, True, True)
            sequence(SEQS - 1, 1, False, True)
            step(SEQS, 0, 0)
            for kinds, tiles in (("split", "split_low"), range(CHUNKS)), (("turn", "turned"), (0, 1)), (("out",), (0,)), (
                    ("turn", "turned"), (2,)), (("out",), (1,)), (("turn", "turned"), (3,)), (("out",), (2, 3)):
                for j in tiles:
                    for kind in kinds:
                        task(kind, j, SEQS - 1, 1)

        nothing = lambda *a: None
        ended = lambda b: isinstance(b, int) and b == SEQS
        is_last = lambda b: isinstance(b, int) and b == SEQS - 1
        out_bank = lambda b: psM[:, 0, :] if is_last(b) else psX[:, :]
        known = lambda b, least: isinstance(b, int) and b < least

        @block.sync
        def _(sp):
            for n, name in enumerate(("w_q", "w_k", "w_v")):
                sp.dma_start(raw[:, n * INNER:(n + 1) * INNER], d[name]).then_inc(weights_in[n], 16)
            sp.dma_start(raw[:, 3 * INNER:3 * INNER + CHUNKS * D].rearrange("p (c d) -> p c d", d=D), d["w_out"].rearrange("(c p) d -> p c d", p=P)).then_inc(weights_in[3], 16)
            sp.dma_start(b_out[:, :], d["b_out"]).then_inc(consts_in, 16)

            def task(kind, j, b, p):
                if kind == "qk" and j % PAIRS == PAIRS - 1:
                    sp.wait_ge(qk_lo, b * 2 * PAIRS + j + 1)
                    top, low = slice(0, HEAD), slice(HEAD, P)
                    copies = (((QS, top, HI), (QS, low, HI), (Q2, top, LO)), ((KS, top, HI), (KS, low, LO), (K2, top, HI)))[j // PAIRS]
                    for odd in range(2):
                        rows = slice(HEAD * odd, HEAD * (odd + 1))
                        for to, there, part in copies:
                            heads = to[there, p, :, :].rearrange("r (c o) n -> r c o n", o=2)[:, :, odd, :]
                            sp.dma_start(heads, qk[rows, p, part, j + 1 - PAIRS:j + 1, :]).then_inc(placed[p], 16)
                if kind == "shift":
                    sp.wait_ge(shiftT_ready, b + 1)
                    sp.dma_start(Q2[HEAD:HEAD + 1, p, :, :].rearrange("a h (c q) -> a (h c) q", q=P), nmT[:, p, :]).then_inc(shift_in[p], 16)

            schedule(sp, task, nothing)

        @block.tensor
        def _(pe):
            T = nc.tensor

            def score(b, p, n):
                h, c = n // CHUNKS, n % CHUNKS
                if n >= 3:
                    pe.wait_ge(p_ready, b * STEPS_A + n - 2)
                elif n < 2 and not known(b, 1):
                    pe.wait_ge(p_ready, b * STEPS_A + n - 1)
                keys = slice(c * P, (c + 1) * P)
                T.matmul(psS[:, n % 3, :], KS[:, p, h, keys], QS[:, p, h, :], start=True, stop=False)
                T.matmul(psS[:, n % 3, :], K2[0:HEAD + 1, p, h, keys], Q2[0:HEAD + 1, p, h, :], start=False, stop=True).then_inc(s_full, 1)

            def task(kind, j, b, p):
                x = lambda part, c: XT[:, bass.ds(b, 1), part, c].rearrange("p a n -> p (a n)")
                if kind in ("qk", "v", "out") and known(b, 1) and j % PAIRS == 0:
                    pe.wait_ge(weights_ready, {"qk": 1 + j // PAIRS, "v": 3, "out": 4}[kind])
                if kind == "qk":
                    if j >= 2:
                        pe.wait_ge(qk_lo, b * 2 * PAIRS + j - 1)
                    elif not known(b, 1):
                        pe.wait_ge(max_done, b * STEPS_A)
                    split_products(T, psM[:, j % 2, :], lambda part: wp[:, part, j * P:(j + 1) * P], lambda part: x(part, slice(0, SEQ)),
                                   True, True).then_inc(qk_full, 1)
                if kind == "v":
                    if j >= 2:
                        pe.wait_ge(v_ready, b * CHUNKS + j - 1)
                    else:
                        pe.wait_ge(qk_lo, b * 2 * PAIRS + 2 * PAIRS - 1 + j)
                    split_products(T, psM[:, j % 2, :], lambda part: x(part, slice(j * P, (j + 1) * P)),
                                   lambda part: wp[:, part, 2 * INNER:3 * INNER], True, True).then_inc(v_full, 1)
                if kind == "max":
                    if j == 0:
                        pe.wait_ge(placed[p], (b - p) * 96 + 192)
                    if j >= 2:
                        pe.wait_ge(max_done, b * STEPS_A + j - 1)
                    else:
                        pe.wait_ge(v_ready, b * CHUNKS + CHUNKS - 1 + j)
                    h, c = j // CHUNKS, j % CHUNKS
                    T.matmul(psM[:, j % 2, :], QS[:, p, h, c * P:(c + 1) * P], KS[:, p, h, :], start=True, stop=True).then_inc(max_full, 1)
                if kind == "shift":
                    pe.wait_ge(shift_ready, b + 1)
                    if not known(b, 2):
                        pe.wait_ge(turn_done, (b - 1) * CHUNKS)
                    T.transpose(turned16[0:STEPS_A, 0:P], nm[:, :], ident16[:, :]).then_inc(shift_turned, 1)
                if kind == "turn":
                    pe.wait_ge(o_lo, b * CHUNKS + j + 1)
                    if j > 0:
                        pe.wait_ge(turn_done, b * CHUNKS + j)
                    elif known(b, 1):
                        pe.wait_ge(shiftT_ready, 2)
                    else:
                        pe.wait_ge(out_done, b)
                    for part in range(PARTS):
                        for i in range(CHUNKS):
                            last = T.transpose(turned16[:, (part * CHUNKS + i) * P:(part * CHUNKS + i + 1) * P], op[:, part, j, i * P:(i + 1) * P], ident16[:, :])
                    last.then_inc(turn_full, 1)
                if kind == "out":
                    pe.wait_ge(turn_done, b * CHUNKS + j + 1 if is_last(b) else (b + 1) * CHUNKS)
                    if j == 0:
                        pe.wait_ge(shiftT_ready, SEQS if isinstance(b, int) and b >= SEQS - 3 else b + 3)
                        if not known(b, 1):
                            pe.wait_ge(out_done, b)
                    for i in range(CHUNKS):
                        last = split_products(T, out_bank(b)[:, j * D:(j + 1) * D], lambda part: OT[:, j, part, i, :],
                                              lambda part: wp[:, part, 3 * INNER + i * D:3 * INNER + (i + 1) * D],
                                              i == 0, i == CHUNKS - 1)
                    if j == CHUNKS - 1:
                        last.then_inc(out_full, 1)

            def values(b, p, n):
                h, c = n // CHUNKS, n % CHUNKS
                pe.wait_ge(p_lo, b * STEPS_A + n + 1)
                if c == 0 and not known(b * HEADS + h, 2):
                    pe.wait_ge(o_ready, b * HEADS + h - 1)
                for i in range(CHUNKS):
                    for x, (a, v) in enumerate(((HI, HI), (HI, LO), (LO, HI))):
                        last = T.matmul(psV[:, h % 2, i * (HEAD + 1):(i + 1) * (HEAD + 1)], pp[:, n % 4, a, i * P:(i + 1) * P],
                                        V1[:, p, v, c, h, :], start=(c == 0 and i == 0 and x == 0), stop=(c == CHUNKS - 1 and x == 2),
                                        skip_group_check=True)
                last.then_inc(av_done, 1)

            def first_scores(b, p):
                pe.wait_ge(shift_in[p], (b - p) * 8 + 16)
                score(b, p, 0)
                score(b, p, 1)

            def step(b, p, n):
                if known(b, 1) and n == 0:
                    first_scores(b, p)
                if ended(b):
                    values(b - 1, 1 - p, STEPS_A - 1)
                    return
                if n + 2 < STEPS_A:
                    score(b, p, n + 2)
                elif n + 2 == STEPS_A and not (isinstance(b, int) and b == SEQS - 1):
                    pe.wait_ge(shift_in[1 - p], (b + 1 - (1 - p)) * 8 + 16)
                    score(b + 1, 1 - p, 0)
                elif not (isinstance(b, int) and b == SEQS - 1):
                    score(b + 1, 1 - p, 1)
                if n > 0:
                    values(b, p, n - 1)
                elif not known(b, 1):
                    values(b - 1, 1 - p, STEPS_A - 1)

            pe.wait_ge(ones_ready, 2)
            pe.wait_ge(v_ones, 2)
            schedule(pe, task, step, tasks_first=True)

        @block.scalar
        def _(act):
            A = nc.scalar
            A.preload_act_table(ACT.Exp)
            for n in range(4):
                act.wait_ge(weights_in[n], 16)
                A.activation(wp[:, HI, n * INNER:(n + 1) * INNER], raw[:, n * INNER:(n + 1) * INNER], ACT.Copy,
                             scale=ATT_WO_SCALE if n == 3 else QK_SCALE).then_inc(weights_hi, 1)

            def task(kind, j, b, p):
                if kind == "qk":
                    act.wait_ge(qk_full, b * 2 * PAIRS + j + 1)
                    if j == 0 and not known(b, 2):
                        act.wait_ge(placed[p], (b - p) * 96)
                    A.activation(qk[:, p, HI, j, :], psM[:, j % 2, :], ACT.Copy, scale=1.0 / (X_SCALE * QK_SCALE)).then_inc(qk_hi, 1)
                if kind == "turned":
                    act.wait_ge(turn_full, b * CHUNKS + j + 1)
                    if not known(b, 1):
                        act.wait_ge(out_full, b)
                    A.activation(OT[:, j, :, :, :].rearrange("p a c q -> p (a c q)"), turned16, ACT.Copy).then_inc(turn_done, 1)

            def step(b, p, n):
                if ended(b):
                    return
                act.wait_ge(s_full, b * STEPS_A + n + 1)
                if not known(b * STEPS_A + n, 4):
                    act.wait_ge(av_done, b * STEPS_A + n - 3)
                A.activation(prob[:, n % 4, :], psS[:, n % 3, :], ACT.Exp, scale=HEAD ** -0.5, bias=gain[:, 0:1]).then_inc(p_full, 1)
                A.activation(pp[:, n % 4, HI, :], psS[:, n % 3, :], ACT.Exp, scale=HEAD ** -0.5, bias=gain[:, 0:1]).then_inc(p_ready, 1)

            act.wait_ge(gain_ready, 2)
            schedule(act, task, step)

        @block.gpsimd
        def _(pool):
            for p in range(2):
                nc.gpsimd.memset(K2[HEAD:HEAD + 1, p, :, :], SHIFT).then_inc(ones_ready, 1)

            def step(b, p, n):
                if ended(b):
                    return
                pool.wait_ge(p_full, b * STEPS_A + n + 1)
                pool.wait_ge(p_ready, b * STEPS_A + n + 1)
                nc.gpsimd.tensor_tensor(pp[:, n % 4, LO, :], prob[:, n % 4, :], pp[:, n % 4, HI, :], ALU.subtract).then_inc(p_lo, 1)

            def task(kind, j, b, p):
                if kind == "split":
                    pool.wait_ge(o_ready, (b + 1) * HEADS)
                    if not known(b, 1):
                        pool.wait_ge(turn_full, b * CHUNKS)
                    nc.gpsimd.tensor_tensor(op[:, HI, j, :], O[:, p, j, :], zero[:, :].broadcast_to([P, INNER]), ALU.add).then_inc(o_hi, 1)

            pool.wait_ge(ones_ready, 2)
            pool.wait_ge(consts_in, 16)
            b_b = b_out[:, :].rearrange("p (a d) -> p a d", a=1).broadcast_to([P, TILES, D])
            nc.gpsimd.tensor_tensor(H[:, :, :], H[:, :, :], b_b, ALU.add).then_inc(bias_added, 1)
            pool.wait_ge(bias_added, 1)
            pool.wait_ge(gain_ready, 2)
            schedule(pool, task, step, lag=1)

        @block.vector
        def _(dve):
            V = nc.vector
            V.memset(V1[:, :, HI, :, :, HEAD:], 1.0).then_inc(v_ones, 1)
            V.memset(V1[:, :, LO, :, :, HEAD:], 0.0).then_inc(v_ones, 1)
            V.memset(gain[:, :], PROB_GAIN).then_inc(gain_ready, 1)
            V.memset(zero[:, :], 0.0).then_inc(gain_ready, 1)
            for n in range(4):
                dve.wait_ge(weights_hi, n + 1)
                V.scalar_tensor_tensor(wp[:, LO, n * INNER:(n + 1) * INNER], raw[:, n * INNER:(n + 1) * INNER],
                                       ATT_WO_SCALE if n == 3 else QK_SCALE, wp[:, HI, n * INNER:(n + 1) * INNER],
                                       ALU.mult, ALU.subtract).then_inc(weights_ready, 1)

            def task(kind, j, b, p):
                if kind == "qk":
                    dve.wait_ge(qk_hi, b * 2 * PAIRS + j + 1)
                    V.scalar_tensor_tensor(qk[:, p, LO, j, :], psM[:, j % 2, :], 1.0 / (X_SCALE * QK_SCALE), qk[:, p, HI, j, :],
                                           ALU.mult, ALU.subtract).then_inc(qk_lo, 1)
                if kind == "v":
                    dve.wait_ge(v_full, b * CHUNKS + j + 1)
                    V.tensor_scalar(V1[:, p, HI, j, :, 0:HEAD], psM[:, j % 2, :].rearrange("p (h e) -> p h e", e=HEAD),
                                    V_SCALE / (X_SCALE * QK_SCALE), None, ALU.mult).then_inc(v_hi, 1)
                    dve.wait_ge(v_hi, b * CHUNKS + j + 1)
                    V.scalar_tensor_tensor(V1[:, p, LO, j, :, 0:HEAD], psM[:, j % 2, :].rearrange("p (h e) -> p h e", e=HEAD),
                                           V_SCALE / (X_SCALE * QK_SCALE), V1[:, p, HI, j, :, 0:HEAD],
                                           ALU.mult, ALU.subtract).then_inc(v_ready, 1)
                if kind == "max":
                    dve.wait_ge(max_full, b * STEPS_A + j + 1)
                    V.tensor_reduce(mx[:, j:j + 1], psM[:, j % 2, :], AX.X, ALU.max).then_inc(max_done, 1)
                if kind == "shift":
                    dve.wait_ge(max_done, (b + 1) * STEPS_A)
                    V.tensor_scalar(nm[:, :], mx[:, :], -1.0 / SHIFT, None, ALU.mult).then_inc(shift_ready, 1)
                    dve.wait_ge(shift_turned, b + 1)
                    if not known(b, 2):
                        dve.wait_ge(shift_in[p], (b - p) * 8)
                    V.tensor_copy(nmT[:, p, :], turned16[0:STEPS_A, 0:P]).then_inc(shiftT_ready, 1)
                if kind == "split_low":
                    dve.wait_ge(o_hi, b * CHUNKS + j + 1)
                    V.tensor_tensor(op[:, LO, j, :], O[:, p, j, :], op[:, HI, j, :], ALU.subtract).then_inc(o_lo, 1)
                if kind == "out" and j == CHUNKS - 1:
                    dve.wait_ge(bias_added, 1)
                    dve.wait_ge(out_full, b + 1)
                    here = H[:, bass.ds(b * CHUNKS, CHUNKS), :].rearrange("p c d -> p (c d)")
                    V.scalar_tensor_tensor(here, out_bank(b), 1.0 / (V_SCALE * ATT_WO_SCALE), here, ALU.mult, ALU.add).then_inc(out_done, 1)

            def head_output(b, p, h):
                dve.wait_ge(av_done, b * STEPS_A + (h + 1) * CHUNKS)
                if h == 0 and not known(b, 2):
                    dve.wait_ge(o_lo, (b - 1) * CHUNKS)
                sums = psV[:, h % 2, 0:CHUNKS * (HEAD + 1)].rearrange("p (c e) -> p c e", e=HEAD + 1)
                if not known(b * HEADS + h, 2):
                    dve.wait_ge(o_ready, b * HEADS + h - 1)
                V.reciprocal(rec[:, h % 2, :], sums[:, :, HEAD]).then_inc(rec_ready, 1)
                dve.wait_ge(rec_ready, b * HEADS + h + 1)
                V.tensor_tensor(O[:, p, :, h * HEAD:(h + 1) * HEAD], sums[:, :, 0:HEAD],
                                rec[:, h % 2, :].rearrange("p (c a) -> p c a", a=1).broadcast_to([P, CHUNKS, HEAD]), ALU.mult).then_inc(o_ready, 1)

            def step(b, p, n):
                if n > 1 and n % CHUNKS == 1:
                    head_output(b, p, n // CHUNKS - 1)
                elif ended(b) or n == 1 and not known(b, 1):
                    head_output(b - 1, 1 - p, HEADS - 1)

            schedule(dve, task, step, tasks_first=True)


GATE_HIDDEN = D // 2
EXPERT_HIDDEN = 2 * D
BLOCKS = EXPERT_HIDDEN // P
W1_SCALE = 2.0 ** 8
G_SCALE = 2.0 ** 6
W2_SCALE = 2.0 ** 8


class Gate:

    def __init__(self, nc, d, routing):
        self.nc, self.d = nc, d
        shape = [P, EXPERTS, EXPERT_HIDDEN]
        self.raw1, self.raw2 = routing.sbuf("w1", shape), routing.sbuf("w2", shape)
        self.w1, self.w2 = (routing.sbuf(name, [P, PARTS, EXPERTS, EXPERT_HIDDEN], F16) for name in ("w1_parts", "w2_parts"))
        self.logits = routing.psum("logits", [P, 512])
        self.bias, self.rank = routing.sbuf("gb2", [P, EXPERTS]), routing.sbuf("rank", [P, EXPERTS])

    def prepare(self, m):
        self.later_in = m.sem("later_in")
        self.gw1 = m.sbuf("gw1", [P, GATE_HIDDEN])
        self.parts = m.sbuf("gw1_parts", [P, PARTS, GATE_HIDDEN], F16)
        self.gb1 = m.sbuf("gb1", [GATE_HIDDEN, 1])
        self.gw2 = m.sbuf("gw2", [GATE_HIDDEN, EXPERTS])
        self.hidden = m.sbuf("gate_hidden", [GATE_HIDDEN, 2, SEQ])
        self.ps = m.psum("psG", [P, 2, SEQ])
        self.params_in, self.w_hi, self.w_parts, self.hidden_psum, self.hidden_ready, self.logits_done, self.hi_experts = (
            m.sem(n) for n in ("params_in", "w_hi", "w_parts", "hidden_psum", "hidden_ready", "logits_done", "hi_experts"))
        self.experts_in = [m.sem(f"expert_in{e}") for e in range(EXPERTS)]

    def load(self, sp):
        for to, name in ((self.gw1, "gw1"), (self.gb1, "gb1"), (self.gw2, "gw2")):
            sp.dma_start(to[:, :], self.d[name]).then_inc(self.params_in, 16)
        for e in range(EXPERTS):
            sp.dma_start(self.raw1[:, e, :], self.d["we1"][e * P:(e + 1) * P, :]).then_inc(self.experts_in[e], 16)
            sp.dma_start(self.raw2[:, e, :].rearrange("p (j d) -> p j d", d=D),
                         self.d["we2"][e * EXPERT_HIDDEN:(e + 1) * EXPERT_HIDDEN, :].rearrange("(j p) d -> p j d", p=P)
                         ).then_inc(self.experts_in[e], 16)
        for to, name in ((self.bias, "gb2"), (self.rank, "rank")):
            sp.dma_start(to[:, :], self.d[name]).then_inc(self.later_in, 16)
        sp.wait_ge(self.later_in, 32)

    def split_high(self, act):
        act.wait_ge(self.params_in, 48)
        self.nc.scalar.activation(self.parts[:, HI, :], self.gw1[:, :], ACT.Copy, scale=W_SCALE_ROUTER).then_inc(self.w_hi, 1)

    def split_low(self, dve):
        dve.wait_ge(self.w_hi, 1)
        self.nc.vector.scalar_tensor_tensor(self.parts[:, LO, :], self.gw1[:, :], W_SCALE_ROUTER, self.parts[:, HI, :],
                                            ALU.mult, ALU.subtract).then_inc(self.w_parts, 1)

    def split_expert_high(self, act, e):
        act.wait_ge(self.experts_in[e], 32)
        for raw, parts, scale in ((self.raw1, self.w1, W1_SCALE), (self.raw2, self.w2, W2_SCALE)):
            self.nc.scalar.activation(parts[:, HI, e, :], raw[:, e, :], ACT.Copy, scale=scale).then_inc(self.hi_experts, 1)

    def split_expert_low(self, dve, e):
        for x in {SEQS - 2: (e - 2,), SEQS - 1: (e - 2, e - 1, e)}.get(e, (e - 2,) if e >= 2 else ()):
            dve.wait_ge(self.hi_experts, 2 * (x + 1))
            for raw, parts, scale in ((self.raw1, self.w1, W1_SCALE), (self.raw2, self.w2, W2_SCALE)):
                self.nc.vector.scalar_tensor_tensor(parts[:, LO, x, :], raw[:, x, :], scale, parts[:, HI, x, :], ALU.mult, ALU.subtract)

    def hidden_product(self, pe, XT, b):
        if b == 0:
            pe.wait_ge(self.w_parts, 1)
        if b >= 2:
            pe.wait_ge(self.hidden_ready, b - 1)
        split_products(self.nc.tensor, self.ps[0:GATE_HIDDEN, b % 2, :], lambda part: self.parts[:, part, :],
                       lambda part: XT[:, b, part, :], True, True).then_inc(self.hidden_psum, 1)

    def relu(self, act, b):
        act.wait_ge(self.hidden_psum, b + 1)
        if b >= 2:
            act.wait_ge(self.logits_done, b - 1)
        self.nc.scalar.activation(self.hidden[:, b % 2, :], self.ps[0:GATE_HIDDEN, b % 2, :], ACT.Relu, bias=self.gb1[:, 0:1],
                                  scale=1.0 / (X_SCALE * W_SCALE_ROUTER)).then_inc(self.hidden_ready, 1)

    def logits_product(self, pe, b):
        pe.wait_ge(self.hidden_ready, b + 1)
        for c in range(CHUNKS):
            at = (b * CHUNKS + c) * EXPERTS
            last = self.nc.tensor.matmul(self.logits[:, at:at + EXPERTS], self.hidden[:, b % 2, c * P:(c + 1) * P], self.gw2[:, :],
                                         start=True, stop=True)
        last.then_inc(self.logits_done, 1)


def route_gated(nc, ident, d, combine, rows, bias_blocks, gate):
    COLS = 32
    with ExitStack() as ctx:
        m = Memory(nc, "gate", ctx)
        gb2, rank = gate.bias, gate.rank
        scores = m.sbuf("scores", [P, TILES, EXPERTS])
        first = m.sbuf("first", [P, TILES, EXPERTS])
        second = m.sbuf("second", [P, TILES, EXPERTS])
        per_token = m.sbuf("per_token", [P, 5, TILES])
        m1, m2, e, r1, work = (per_token[:, n, :] for n in range(5))
        record = m.sbuf("record", [P, TILES, COLS])
        psR = m.psum("psR", [P, SEQS, P])
        (cleared, bias_in, own_sem, shifted, exped, gap_ready, exp_ready, record_ready, rows_psum) = (
            m.sem(n) for n in ("cleared", "bias_in", "own", "shifted", "exped", "gap_ready", "exp_ready",
                               "record_ready", "rows_psum"))
        block = ctx.enter_context(nc.Block())

        @block.sync
        def _(sp):
            load_bias_blocks(sp, bias_blocks, d["be2"], cleared, bias_in)
            sp.wait_ge(bias_in, 16 * CHUNKS)

        @block.scalar
        def _(act):
            A = nc.scalar
            A.preload_act_table(ACT.Exp)
            act.wait_ge(shifted, 1)
            A.activation(first[:, :, :], scores[:, :, :], ACT.Exp).then_inc(exped, 1)
            act.wait_ge(gap_ready, 1)
            A.activation(e[:, :], e[:, :], ACT.Exp).then_inc(exp_ready, 1)
            act.wait_ge(rows_psum, 1)
            A.activation(rows[:, :, :], psR[:, :, :], ACT.Copy)

        @block.tensor
        def _(pe):
            pe.wait_ge(record_ready, 1)
            for b in range(SEQS):
                last = nc.tensor.transpose(psR[:, b, :], record[:, b * CHUNKS:(b + 1) * CHUNKS, :].rearrange("p c j -> p (c j)"), ident[:, :])
            last.then_inc(rows_psum, 1)

        @block.vector
        def _(dve):
            V = nc.vector
            own = Chain(dve, own_sem)
            V.memset(bias_blocks[:, :], 0.0).then_inc(cleared, 1)
            own(V.memset(record[:, :, EXPERTS:], 0.0))
            gb2_b = gb2[:, :].rearrange("p (a e) -> p a e", a=1).broadcast_to([P, TILES, EXPERTS])
            wide = lambda x: x.rearrange("p (t a) -> p t a", a=1).broadcast_to([P, TILES, EXPERTS])
            own.link(V.tensor_tensor(scores[:, :, :], gate.logits[:, 0:TILES * EXPERTS].rearrange("p (t e) -> p t e", e=EXPERTS), gb2_b, ALU.add))
            own.link(V.tensor_reduce(m1[:, :], scores[:, :, :], AX.X, ALU.max))
            V.tensor_tensor(scores[:, :, :], scores[:, :, :], wide(m1[:, :]), ALU.subtract).then_inc(shifted, 1)
            dve.wait_ge(exped, 1)
            own.link(V.tensor_reduce(work[:, :], first[:, :, :], AX.X, ALU.add))
            own.link(V.reciprocal(work[:, :], work[:, :]))
            own.link(V.tensor_tensor(scores[:, :, :], first[:, :, :], wide(work[:, :]), ALU.mult))
            top_two(V, own, scores[:, :, :], rank[:, :], first[:, :, :], second[:, :, :], m1[:, :], m2[:, :], work[:, :])
            V.tensor_tensor(e[:, :], m2[:, :], m1[:, :], ALU.subtract).then_inc(gap_ready, 1)
            dve.wait_ge(exp_ready, 1)
            own.link(V.tensor_scalar(r1[:, :], e[:, :], 1.0, None, ALU.add))
            own.link(V.reciprocal(r1[:, :], r1[:, :]))
            own(V.tensor_tensor(e[:, :], e[:, :], r1[:, :], ALU.mult))
            own.link(V.tensor_tensor(first[:, :, :], first[:, :, :], wide(r1[:, :]), ALU.mult))
            own.link(V.tensor_tensor(second[:, :, :], second[:, :, :], wide(e[:, :]), ALU.mult))
            own.link(V.tensor_tensor(record[:, :, 0:EXPERTS], first[:, :, :], second[:, :, :], ALU.add))
            V.tensor_scalar(combine[:, :, :], record[:, :, 0:EXPERTS], 1.0 / (G_SCALE * W2_SCALE), None, ALU.mult).then_inc(record_ready, 1)


def gated_experts(nc, H, XT, d, combine, rows, bias_blocks, gate, out):
    w1, w2 = gate.w1, gate.w2
    with ExitStack() as ctx:
        m = Memory(nc, "ffn", ctx)
        b1 = m.sbuf("b1", [P, EXPERTS * BLOCKS])
        act_out = m.sbuf("gelu", [P, 2, BLOCKS, SEQ])
        gp = m.sbuf("gelu_parts", [P, 2, PARTS, BLOCKS, SEQ], F16)
        psH = m.psum("psH", [P, 2, BLOCKS, SEQ])
        psY = m.psum("psY", [P, 2, CHUNKS * D])
        stored, bias_in, bias_psum, bias_added, h_psum, gelu_ready, hi_ready, lo_ready, y_psum, y_added = (m.sem(n) for n in (
            "stored", "bias_in", "bias_psum", "bias_added", "h_psum", "gelu_ready", "hi_ready", "lo_ready", "y_psum", "y_added"))
        bias_banks = [psY[:, p, :] for p in range(2)]
        block = ctx.enter_context(nc.Block())
        known = lambda u, least: isinstance(u, int) and u < least

        @block.sync
        def _(sp):
            sp.dma_start(b1[:, :], d["be1"]).then_inc(bias_in, 16)
            with sp.Fori(0, SEQS) as b:
                sp.wait_ge(y_added, (b + 1) * EXPERTS)
                sp.dma_start(out[bass.ds(b, 1), :, :].rearrange("b (c p) d -> p (b c) d", p=P), H[:, bass.ds(b * CHUNKS, CHUNKS), :]).then_inc(stored, 16)
            sp.wait_ge(stored, 16 * SEQS)

        @block.tensor
        def _(pe):
            def up(b, e):
                if not known(b * EXPERTS + e, 2):
                    pe.wait_ge(gelu_ready, (b * EXPERTS + e - 1) * BLOCKS)
                for j in range(BLOCKS):
                    split_products(nc.tensor, psH[:, e % 2, j, :], lambda part: w1[:, part, e, j * P:(j + 1) * P],
                                   lambda part: XT[:, bass.ds(b, 1), part, :].rearrange("p a n -> p (a n)"), True, True).then_inc(h_psum, 1)

            def down(b, e):
                u = b * EXPERTS + e
                pe.wait_ge(lo_ready, u + 1)
                if not known(u, 2):
                    pe.wait_ge(y_added, u - 1)
                if known(u, 1):
                    pe.wait_ge(bias_added, SEQS)
                for c in range(CHUNKS):
                    for j in range(BLOCKS):
                        last = split_products(nc.tensor, psY[:, e % 2, c * D:(c + 1) * D], lambda part: gp[:, e % 2, part, j, c * P:(c + 1) * P],
                                              lambda part: w2[:, part, e, j * D:(j + 1) * D], j == 0, j == BLOCKS - 1)
                last.then_inc(y_psum, 1)

            def sequence(b, last):
                for e in range(EXPERTS):
                    if e + 2 < EXPERTS:
                        up(b, e + 2)
                    elif not last:
                        up(b + 1, e + 2 - EXPERTS)
                    down(b, e)

            up(0, 0)
            up(0, 1)
            bias_share_products(pe, nc, bias_banks, rows, bias_blocks, bias_psum, bias_added)
            sequence(0, False)
            with pe.Fori(1, SEQS - 1) as b:
                sequence(b, False)
            sequence(SEQS - 1, True)

        @block.scalar
        def _(act):
            A = nc.scalar
            A.preload_act_table(ACT.Gelu)
            act.wait_ge(bias_in, 16)

            def sequence(b):
                for e in range(EXPERTS):
                    u = b * EXPERTS + e
                    if not known(u, 2):
                        act.wait_ge(lo_ready, u - 1)
                    for j in range(BLOCKS):
                        act.wait_ge(h_psum, u * BLOCKS + j + 1)
                        A.activation(act_out[:, e % 2, j, :], psH[:, e % 2, j, :], ACT.Gelu, bias=b1[:, e * BLOCKS + j:e * BLOCKS + j + 1],
                                     scale=1.0 / (X_SCALE * W1_SCALE)).then_inc(gelu_ready, 1)
                    act.wait_ge(gelu_ready, (u + 1) * BLOCKS)
                    if not known(u, 2):
                        act.wait_ge(y_psum, u - 1)
                    A.activation(gp[:, e % 2, HI, :, :], act_out[:, e % 2, :, :], ACT.Copy, scale=G_SCALE).then_inc(hi_ready, 1)

            sequence(0)
            with act.Fori(1, SEQS) as b:
                sequence(b)

        @block.vector
        def _(dve):
            V = nc.vector
            def low(b, e):
                dve.wait_ge(hi_ready, b * EXPERTS + e + 1)
                V.scalar_tensor_tensor(gp[:, e % 2, LO, :, :], act_out[:, e % 2, :, :], G_SCALE, gp[:, e % 2, HI, :, :],
                                       ALU.mult, ALU.subtract).then_inc(lo_ready, 1)

            def add(b, e):
                u = b * EXPERTS + e
                dve.wait_ge(y_psum, u + 1)
                if not known(u, 1):
                    dve.wait_ge(y_added, u)
                for c in range(CHUNKS):
                    here = H[:, bass.ds(b * CHUNKS + c, 1), :].rearrange("p a d -> p (a d)")
                    last = V.scalar_tensor_tensor(here, psY[:, e % 2, c * D:(c + 1) * D],
                                                  combine[:, bass.ds(b * CHUNKS + c, 1), e:e + 1].rearrange("p a b -> p (a b)"),
                                                  here, ALU.mult, ALU.add)
                last.then_inc(y_added, 1)

            def sequence(b, last):
                for e in range(EXPERTS):
                    if e + 1 < EXPERTS:
                        low(b, e + 1)
                    elif not last:
                        low(b + 1, 0)
                    add(b, e)

            add_bias_shares(dve, nc, H, bias_banks, bias_psum, bias_added)
            dve.wait_ge(bias_added, SEQS)
            low(0, 0)
            sequence(0, False)
            with dve.Fori(1, SEQS - 1) as b:
                sequence(b, False)
            sequence(SEQS - 1, True)


def build_program(nc, d, out):
    with ExitStack() as ctx:
        m = Memory(nc, "model", ctx)
        H = m.sbuf("h", [P, TILES, D])
        ident = m.sbuf("ident", [P, P])
        ident16 = m.sbuf("ident16", [P, P], F16)
        combine = m.sbuf("combine", [P, TILES, EXPERTS])
        XT = m.sbuf("xT", [P, SEQS, PARTS, SEQ], F16)
        mask_rows = nc.dram_tensor("mask_rows", (2 * EXPERTS, SEQS * SEQ), F16).ap()
        embed_and_convolve(nc, H, ident, ident16, d)
        with ExitStack() as inner:
            routing = Memory(nc, "routing2", inner)
            rows, bias_blocks = routing.sbuf("rows", [P, SEQS, P]), routing.sbuf("bias_blocks", [P, CHUNKS * D])
            with ExitStack() as scored:
                gate = RecurrentGate(nc, d, Memory(nc, "scores2", scored))
                normalize(nc, "norm2", H, XT, ident16, gate)
                route_recurrent(nc, ident, d, combine, mask_rows, rows, bias_blocks, gate)
            recurrent_experts(nc, H, XT, d, combine, mask_rows, rows, bias_blocks)
        normalize(nc, "norm3", H, XT, ident16)
        attention(nc, H, XT, ident16, d)
        with ExitStack() as inner:
            routing = Memory(nc, "routing4", inner)
            rows, bias_blocks = routing.sbuf("rows", [P, SEQS, P]), routing.sbuf("bias_blocks", [P, CHUNKS * D])
            gate = Gate(nc, d, routing)
            normalize(nc, "norm4", H, XT, ident16, gate)
            route_gated(nc, ident, d, combine, rows, bias_blocks, gate)
            gated_experts(nc, H, XT, d, combine, rows, bias_blocks, gate, out)


def dft_matrices():
    import numpy as np

    n, half = SEQ, SEQ // 2
    angle = 2 * np.pi * (np.outer(np.arange(n), np.arange(half)) % n) / n
    sign = (-1.0) ** np.arange(n)
    forward = np.concatenate([np.cos(angle), -np.sin(angle)], axis=1)
    forward[:, half] = sign
    inverse = 2 * forward.T / n
    inverse[[0, half]] /= 2
    return forward.astype(np.float32), np.ascontiguousarray(inverse).astype(np.float32)


def kernel(**inputs):
    import numpy as np
    import concourse.bacc as bacc
    from concourse.bass_utils import run_bass_kernel_spmd

    x = {name: np.asarray(a) for name, a in inputs.items()}
    fwd, inv = dft_matrices()
    rows = lambda a: np.ascontiguousarray(np.broadcast_to(a, (P,) + a.shape))
    positions = np.concatenate([np.arange(32), np.arange(0, SEQ, 32), [0.5]]).astype(np.float32)
    arrays = {
        "ids": np.ascontiguousarray(x["x"].reshape(TILES, P).T),
        "table": np.concatenate([x["L0_tok_fine_embed_w"], x["L0_tok_loc_to_cluster_w"].T], axis=1),
        "coarse_w": x["L0_tok_coarse_embed_w"],
        "cluster_b": rows(x["L0_tok_loc_to_cluster_b"]),
        "A_re": x["L0_attn_A_real"], "A_im": x["L0_attn_A_imag"], "B_in": x["L0_attn_B"], "C_in": x["L0_attn_C"],
        "delta": x["L0_attn_delta"].reshape(P, 1),
        "positions": rows(positions), "dft": fwd, "inverse_dft": inv, "ident": np.eye(P, dtype=np.float32),
        "ident16": np.eye(P, dtype=np.float16),
        "rank": rows(np.arange(EXPERTS, 0, -1, dtype=np.float32)),
        "w_q": x["L1_attn_w_q"], "w_k": x["L1_attn_w_k"], "w_v": x["L1_attn_w_v"], "w_out": x["L1_attn_w_out"],
        "b_out": rows(x["L1_attn_b_out"]),
        "router_w": x["L0_ffn_router_w"], "router_b": rows(x["L0_ffn_router_b"]),
        "Wi": x["L0_ffn_Wi"].reshape(EXPERTS * D, GATES * D), "Wh": x["L0_ffn_Wh"].reshape(EXPERTS * D, GATES * D),
        "Wo": x["L0_ffn_Wo"].reshape(EXPERTS * D, D), "bo": x["L0_ffn_bo"],
        "gw1": x["L1_ffn_gw1"], "gb1": x["L1_ffn_gb1"].reshape(GATE_HIDDEN, 1), "gw2": x["L1_ffn_gw2"], "gb2": rows(x["L1_ffn_gb2"]),
        "we1": x["L1_ffn_we1"].reshape(EXPERTS * D, EXPERT_HIDDEN), "we2": x["L1_ffn_we2"].reshape(EXPERTS * EXPERT_HIDDEN, D),
        "be1": np.ascontiguousarray(x["L1_ffn_be1"].reshape(EXPERTS * BLOCKS, P).T), "be2": x["L1_ffn_be2"],
        "lstm_b": np.ascontiguousarray(x["L0_ffn_b"].reshape(EXPERTS * GATES, D).T),
    }
    nc = bacc.Bacc("TRN2", target_bir_lowering=False, num_devices=1)
    d = {n: nc.dram_tensor(f"in_{n}", a.shape, mybir.dt.from_np(a.dtype), kind="ExternalInput").ap() for n, a in arrays.items()}
    out = nc.dram_tensor("out", (SEQS, SEQ, D), F32, kind="ExternalOutput").ap()
    build_program(nc, d, out)
    r = run_bass_kernel_spmd(nc, [{f"in_{n}": a for n, a in arrays.items()}], core_ids=[0])
    return r.results[0]["out"]
```
